# Optimizing a Trainium2 kernel written in Bass

```python
import numpy as np
import jax
import jax.numpy as jnp

def _softmax(x, axis=-1):
    return jax.nn.softmax(x, axis=axis)

def _gelu(x):
    return jax.nn.gelu(x, approximate=True)

def _silu(x):
    return jax.nn.silu(x)

def _sigmoid(x):
    return jax.nn.sigmoid(x)

def _layernorm(x, axis=-1, eps=1e-05):
    m = jnp.mean(x, axis=axis, keepdims=True)
    v = jnp.var(x, axis=axis, keepdims=True)
    return (x - m) / jnp.sqrt(v + eps)

def _scatter_add(tgt, idx, src, axis=0):
    return tgt.at[idx].add(src)

def _segment_sum(src, seg, n):
    return jax.ops.segment_sum(src, seg, n)
kernel_name = 'mk_audio_tower_d1_tok_aud1d256_r4_054bf9'

def setup_inputs(seed: int=0):
    np.random.seed(seed)
    _w = jnp.asarray

    def _rec_inputs():
        import jax
        import jax.numpy as jnp
        _rk = jax.random.key(seed)
        x = 0.000296351 + 0.99907 * jax.random.normal(jax.random.fold_in(_rk, 1), (32, 4000), jnp.float32)
        return x
    x = _rec_inputs()

    def _L0_tok_setup():
        import jax, jax.numpy as jnp
        import numpy as np
        B, L = (64, 4096)
        INTERP_FACTOR = 0.25
        WINDOW, STEP = (64, 64)
        ALPHA, BETA, TEMP = (0.12, 0.9, 1.0)
        A = -0.75

        def _cubic_w(t):
            at = jnp.abs(t)
            w_near = ((A + 2.0) * at - (A + 3.0)) * at * at + 1.0
            w_far = ((A * at - 5.0 * A) * at + 8.0 * A) * at - 4.0 * A
            return jnp.where(at <= 1.0, w_near, jnp.where(at < 2.0, w_far, 0.0))

        def cubic_interpolate_1d(signal, interp_factor):
            b, n = signal.shape
            num_points = int((n - 1) / interp_factor) + 1
            x = jnp.linspace(0.0, 1.0, num_points) * (n - 1)
            i0 = jnp.floor(x).astype(jnp.int32)
            frac = x - i0.astype(x.dtype)
            offs = jnp.arange(-1, 3)
            idx = jnp.clip(i0[:, None] + offs[None, :], 0, n - 1)
            w = _cubic_w(frac[:, None] - offs[None, :].astype(x.dtype))
            taps = signal[:, idx]
            return jnp.einsum('bpk,pk->bp', taps, w)

        def _apply_kernels(x):
            poly = (x + 1.3) ** 2
            gauss = jnp.exp(-0.5 * ((x - 0.7) / 1.0) ** 2)
            return 0.5 * poly + 0.5 * gauss

        def soft_minimum(a, b, temperature):
            b = jnp.broadcast_to(b, a.shape)
            stacked = jnp.stack([-a * temperature, -b * temperature], axis=0)
            return -jax.nn.logsumexp(stacked, axis=0) / temperature

        def _forward(signal):
            interp = cubic_interpolate_1d(signal, INTERP_FACTOR)
            n = interp.shape[1]
            n_windows = (n - WINDOW) // STEP + 1
            starts = jnp.arange(n_windows) * STEP
            idx = starts[:, None] + jnp.arange(WINDOW)[None, :]
            windows = interp[:, idx]
            kw = _apply_kernels(windows)
            M = jnp.abs(jnp.fft.fft(kw, axis=-1))
            Mmax = jnp.max(M, axis=-1, keepdims=True)
            thr = ALPHA * Mmax
            mask = jax.nn.sigmoid((M - thr) * TEMP)
            Mt = M * mask
            return soft_minimum(Mt, BETA * Mmax, TEMP)
        key = jax.random.key(seed)
        return {'signal': jax.random.normal(key, (B, L), dtype=jnp.float32)}
    _L0_tok_all = _L0_tok_setup()
    _L0_tok_in = {k: v for k, v in _L0_tok_all.items() if k in ()}
    del _L0_tok_all

    def _L0_attn_setup():
        import jax, jax.numpy as jnp
        import numpy as np
        PI = np.pi
        key = jax.random.key(seed)
        ks = jax.random.split(key, 24)
        B, L, D, P, H, MAXL = (1, 512, 64, 32, 4, 4096)
        Dh = D // 2
        n = lambda k, s, sc=0.02: (jax.random.normal(k, s) * sc).astype(jnp.float32)
        z = lambda s: jnp.zeros(s, jnp.float32)
        return {'x': n(ks[0], (B, L, D), 1.0), 'pos_phases': n(ks[1], (MAXL, P), PI), 'window_deltas': jnp.arange(-2, 3, dtype=jnp.float32), 'mc_w': n(ks[2], (D, D)), 'mc_b': z((D,)), 'hop_w1': n(ks[3], (D + P, D)), 'hop_b1': z((D,)), 'hop_w2': n(ks[4], (D, H * (P + 1))), 'hop_b2': z((H * (P + 1),)), 'cpe_w': n(ks[5], (D, P)), 'cpe_b': z((P,)), 've_w': n(ks[6], (D, D)), 've_b': z((D,)), 'kce_w': n(ks[7], (D, D)), 'kce_b': z((D,)), 'ksk_w1': n(ks[8], (2 * D, D)), 'ksk_b1': z((D,)), 'ksk_w2': n(ks[9], (D, P)), 'ksk_b2': z((P,)), 'sg_w1': n(ks[10], (D, Dh)), 'sg_b1': z((Dh,)), 'sg_w2': n(ks[11], (Dh, 1)), 'sg_b2': z((1,)), 'ln_g': jnp.ones((D,), jnp.float32), 'ln_b': z((D,)), 'out_w': n(ks[12], (D, D)), 'out_b': z((D,))}
    _L0_attn_all = _L0_attn_setup()
    _L0_attn_in = {k: v for k, v in _L0_attn_all.items() if k in ('pos_phases', 'window_deltas', 'mc_w', 'mc_b', 'hop_w1', 'hop_b1', 'hop_w2', 'hop_b2', 'cpe_w', 'cpe_b', 've_w', 've_b', 'kce_w', 'kce_b', 'ksk_w1', 'ksk_b1', 'ksk_w2', 'ksk_b2', 'sg_w1', 'sg_b1', 'sg_w2', 'sg_b2', 'ln_g', 'ln_b', 'out_w', 'out_b')}
    del _L0_attn_all

    def _L0_ffn_setup():
        import jax, jax.numpy as jnp
        import numpy as np
        B, A = (1024, 8)
        IN, OUT = (64, 64)
        SH1, SH2 = (64, 128)
        EH1, EH2 = (128, 64)
        E, TOPK = (4, 2)

        def _shared_mlp(x, W1, b1, W2, b2, W3, b3):
            h = jax.nn.relu(x @ W1 + b1)
            h = jax.nn.relu(h @ W2 + b2)
            return h @ W3 + b3

        def _experts_mlp(x, eW1, eb1, eW2, eb2, eW3, eb3):
            h = jax.nn.relu(jnp.einsum('baf,efh->ebah', x, eW1) + eb1[:, None, None, :])
            h = jax.nn.relu(jnp.einsum('ebah,ehg->ebag', h, eW2) + eb2[:, None, None, :])
            o = jnp.einsum('ebag,ego->ebao', h, eW3) + eb3[:, None, None, :]
            return jnp.moveaxis(o, 0, -1)
        key = jax.random.key(seed)
        ks = jax.random.split(key, 16)
        s = 0.05
        return {'x': jax.random.normal(ks[0], (B, A, IN), jnp.float32), 'sW1': jax.random.normal(ks[1], (IN, SH1), jnp.float32) * s, 'sb1': jnp.zeros((SH1,), jnp.float32), 'sW2': jax.random.normal(ks[2], (SH1, SH2), jnp.float32) * s, 'sb2': jnp.zeros((SH2,), jnp.float32), 'sW3': jax.random.normal(ks[3], (SH2, OUT), jnp.float32) * s, 'sb3': jnp.zeros((OUT,), jnp.float32), 'eW1': jax.random.normal(ks[4], (E, IN, EH1), jnp.float32) * s, 'eb1': jnp.zeros((E, EH1), jnp.float32), 'eW2': jax.random.normal(ks[5], (E, EH1, EH2), jnp.float32) * s, 'eb2': jnp.zeros((E, EH2), jnp.float32), 'eW3': jax.random.normal(ks[6], (E, EH2, OUT), jnp.float32) * s, 'eb3': jnp.zeros((E, OUT), jnp.float32), 'gW': jax.random.normal(ks[7], (IN, E), jnp.float32) * s, 'gb': jnp.zeros((E,), jnp.float32)}
    _L0_ffn_all = _L0_ffn_setup()
    _L0_ffn_in = {k: v for k, v in _L0_ffn_all.items() if k in ('sW1', 'sb1', 'sW2', 'sb2', 'sW3', 'sb3', 'eW1', 'eb1', 'eW2', 'eb2', 'eW3', 'eb3', 'gW', 'gb')}
    del _L0_ffn_all
    return {'x': x, 'L0_attn_pos_phases': _L0_attn_in['pos_phases'], 'L0_attn_window_deltas': _L0_attn_in['window_deltas'], 'L0_attn_mc_w': _L0_attn_in['mc_w'], 'L0_attn_mc_b': _L0_attn_in['mc_b'], 'L0_attn_hop_w1': _L0_attn_in['hop_w1'], 'L0_attn_hop_b1': _L0_attn_in['hop_b1'], 'L0_attn_hop_w2': _L0_attn_in['hop_w2'], 'L0_attn_hop_b2': _L0_attn_in['hop_b2'], 'L0_attn_cpe_w': _L0_attn_in['cpe_w'], 'L0_attn_cpe_b': _L0_attn_in['cpe_b'], 'L0_attn_ve_w': _L0_attn_in['ve_w'], 'L0_attn_ve_b': _L0_attn_in['ve_b'], 'L0_attn_kce_w': _L0_attn_in['kce_w'], 'L0_attn_kce_b': _L0_attn_in['kce_b'], 'L0_attn_ksk_w1': _L0_attn_in['ksk_w1'], 'L0_attn_ksk_b1': _L0_attn_in['ksk_b1'], 'L0_attn_ksk_w2': _L0_attn_in['ksk_w2'], 'L0_attn_ksk_b2': _L0_attn_in['ksk_b2'], 'L0_attn_sg_w1': _L0_attn_in['sg_w1'], 'L0_attn_sg_b1': _L0_attn_in['sg_b1'], 'L0_attn_sg_w2': _L0_attn_in['sg_w2'], 'L0_attn_sg_b2': _L0_attn_in['sg_b2'], 'L0_attn_ln_g': _L0_attn_in['ln_g'], 'L0_attn_ln_b': _L0_attn_in['ln_b'], 'L0_attn_out_w': _L0_attn_in['out_w'], 'L0_attn_out_b': _L0_attn_in['out_b'], 'L0_ffn_sW1': _L0_ffn_in['sW1'], 'L0_ffn_sb1': _L0_ffn_in['sb1'], 'L0_ffn_sW2': _L0_ffn_in['sW2'], 'L0_ffn_sb2': _L0_ffn_in['sb2'], 'L0_ffn_sW3': _L0_ffn_in['sW3'], 'L0_ffn_sb3': _L0_ffn_in['sb3'], 'L0_ffn_eW1': _L0_ffn_in['eW1'], 'L0_ffn_eb1': _L0_ffn_in['eb1'], 'L0_ffn_eW2': _L0_ffn_in['eW2'], 'L0_ffn_eb2': _L0_ffn_in['eb2'], 'L0_ffn_eW3': _L0_ffn_in['eW3'], 'L0_ffn_eb3': _L0_ffn_in['eb3'], 'L0_ffn_gW': _L0_ffn_in['gW'], 'L0_ffn_gb': _L0_ffn_in['gb']}

def reference(x, L0_attn_pos_phases, L0_attn_window_deltas, L0_attn_mc_w, L0_attn_mc_b, L0_attn_hop_w1, L0_attn_hop_b1, L0_attn_hop_w2, L0_attn_hop_b2, L0_attn_cpe_w, L0_attn_cpe_b, L0_attn_ve_w, L0_attn_ve_b, L0_attn_kce_w, L0_attn_kce_b, L0_attn_ksk_w1, L0_attn_ksk_b1, L0_attn_ksk_w2, L0_attn_ksk_b2, L0_attn_sg_w1, L0_attn_sg_b1, L0_attn_sg_w2, L0_attn_sg_b2, L0_attn_ln_g, L0_attn_ln_b, L0_attn_out_w, L0_attn_out_b, L0_ffn_sW1, L0_ffn_sb1, L0_ffn_sW2, L0_ffn_sb2, L0_ffn_sW3, L0_ffn_sb3, L0_ffn_eW1, L0_ffn_eb1, L0_ffn_eW2, L0_ffn_eb2, L0_ffn_eW3, L0_ffn_eb3, L0_ffn_gW, L0_ffn_gb):
    import jax
    import jax.numpy as jnp

    def _L0_tok_ref(signal):
        import jax, jax.numpy as jnp
        import numpy as np
        B, L = (64, 4096)
        INTERP_FACTOR = 0.25
        WINDOW, STEP = (64, 64)
        ALPHA, BETA, TEMP = (0.12, 0.9, 1.0)
        A = -0.75

        def _cubic_w(t):
            at = jnp.abs(t)
            w_near = ((A + 2.0) * at - (A + 3.0)) * at * at + 1.0
            w_far = ((A * at - 5.0 * A) * at + 8.0 * A) * at - 4.0 * A
            return jnp.where(at <= 1.0, w_near, jnp.where(at < 2.0, w_far, 0.0))

        def cubic_interpolate_1d(signal, interp_factor):
            b, n = signal.shape
            num_points = int((n - 1) / interp_factor) + 1
            x = jnp.linspace(0.0, 1.0, num_points) * (n - 1)
            i0 = jnp.floor(x).astype(jnp.int32)
            frac = x - i0.astype(x.dtype)
            offs = jnp.arange(-1, 3)
            idx = jnp.clip(i0[:, None] + offs[None, :], 0, n - 1)
            w = _cubic_w(frac[:, None] - offs[None, :].astype(x.dtype))
            taps = signal[:, idx]
            return jnp.einsum('bpk,pk->bp', taps, w)

        def _apply_kernels(x):
            poly = (x + 1.3) ** 2
            gauss = jnp.exp(-0.5 * ((x - 0.7) / 1.0) ** 2)
            return 0.5 * poly + 0.5 * gauss

        def soft_minimum(a, b, temperature):
            b = jnp.broadcast_to(b, a.shape)
            stacked = jnp.stack([-a * temperature, -b * temperature], axis=0)
            return -jax.nn.logsumexp(stacked, axis=0) / temperature

        def _forward(signal):
            interp = cubic_interpolate_1d(signal, INTERP_FACTOR)
            n = interp.shape[1]
            n_windows = (n - WINDOW) // STEP + 1
            starts = jnp.arange(n_windows) * STEP
            idx = starts[:, None] + jnp.arange(WINDOW)[None, :]
            windows = interp[:, idx]
            kw = _apply_kernels(windows)
            M = jnp.abs(jnp.fft.fft(kw, axis=-1))
            Mmax = jnp.max(M, axis=-1, keepdims=True)
            thr = ALPHA * Mmax
            mask = jax.nn.sigmoid((M - thr) * TEMP)
            Mt = M * mask
            return soft_minimum(Mt, BETA * Mmax, TEMP)
        return _forward(signal)

    def _L0_attn_ref(x, pos_phases, window_deltas, mc_w, mc_b, hop_w1, hop_b1, hop_w2, hop_b2, cpe_w, cpe_b, ve_w, ve_b, kce_w, kce_b, ksk_w1, ksk_b1, ksk_w2, ksk_b2, sg_w1, sg_b1, sg_w2, sg_b2, ln_g, ln_b, out_w, out_b):
        import jax, jax.numpy as jnp
        import numpy as np
        PI = np.pi
        B, L, D = x.shape
        P = cpe_w.shape[1]
        H = hop_b2.shape[0] // (P + 1)
        gelu = lambda t: jax.nn.gelu(t, approximate=False)
        sqrtP = jnp.sqrt(jnp.float32(P))
        pp = pos_phases[:L]
        pos_cos, pos_sin = (jnp.cos(pp), jnp.sin(pp))
        content = x @ mc_w + mc_b
        mem1_cos = jnp.cumsum(pos_cos[None, :, :, None] * content[:, :, None, :], axis=1)
        mem1_sin = jnp.cumsum(pos_sin[None, :, :, None] * content[:, :, None, :], axis=1)
        off_in = jnp.concatenate([x, jnp.broadcast_to(pp[None], (B, L, P))], axis=-1)
        ao = (gelu(off_in @ hop_w1 + hop_b1) @ hop_w2 + hop_b2).reshape(B, L, H, P + 1)
        center = jnp.tanh(ao[..., :P]) * PI
        width = jax.nn.sigmoid(ao[..., -1:]) * 2 + 0.1
        Wn = window_deltas.shape[0]
        deltas = window_deltas.reshape(1, 1, 1, Wn)
        weights = jnp.exp(-0.5 * deltas ** 2 / (width ** 2 + 1e-06))
        off_ph = center[:, :, :, None, :] + deltas[..., None] * 0.1
        oc, os_ = (jnp.cos(off_ph), jnp.sin(off_ph))
        pce = pos_cos.reshape(1, L, 1, 1, P)
        pse = pos_sin.reshape(1, L, 1, 1, P)
        qc = (pce * oc - pse * os_).reshape(B, L, H * Wn, P)
        qs = (pse * oc + pce * os_).reshape(B, L, H * Wn, P)
        retrieved = (jnp.einsum('blpd,blhp->blhd', mem1_cos, qc) + jnp.einsum('blpd,blhp->blhd', mem1_sin, qs)) / sqrtP
        retrieved = retrieved.reshape(B, L, H, Wn, D)
        ws = (retrieved * weights[..., None]).sum(axis=3)
        head_out = ws / (weights.sum(axis=3, keepdims=True) + 1e-06)
        mh_out = head_out.mean(axis=2)
        key_ph = jnp.tanh(x @ cpe_w + cpe_b) * PI
        key_cos, key_sin = (jnp.cos(key_ph), jnp.sin(key_ph))
        values = x @ ve_w + ve_b
        gate = jax.nn.sigmoid(gelu(x @ sg_w1 + sg_b1) @ sg_w2 + sg_b2)
        ctx = jnp.cumsum(x @ kce_w + kce_b, axis=1)
        pos = jnp.arange(1, L + 1, dtype=x.dtype).reshape(1, L, 1)
        storage_in = jnp.concatenate([x, ctx / pos], axis=-1)
        st_ph = jnp.tanh(gelu(storage_in @ ksk_w1 + ksk_b1) @ ksk_w2 + ksk_b2) * PI
        sc, ss = (jnp.cos(st_ph), jnp.sin(st_ph))
        gv = values[:, :, None, :] * gate[..., None]
        kv_cos = jnp.cumsum(sc[..., None] * gv, axis=1)
        kv_sin = jnp.cumsum(ss[..., None] * gv, axis=1)
        gate_cum = jnp.clip(jnp.cumsum(gate, axis=1), 1.0, None)
        kv_ret = (kv_cos * key_cos[..., None] + kv_sin * key_sin[..., None]).sum(axis=2)
        kv_ret = kv_ret / (jnp.sqrt(gate_cum) * sqrtP)
        combined = mh_out + kv_ret
        mu = combined.mean(-1, keepdims=True)
        var = combined.var(-1, keepdims=True)
        lnx = (combined - mu) / jnp.sqrt(var + 1e-05) * ln_g + ln_b
        return x + (lnx @ out_w + out_b)

    def _L0_ffn_ref(x, sW1, sb1, sW2, sb2, sW3, sb3, eW1, eb1, eW2, eb2, eW3, eb3, gW, gb):
        import jax, jax.numpy as jnp
        import numpy as np
        B, A = (1024, 8)
        IN, OUT = (64, 64)
        SH1, SH2 = (64, 128)
        EH1, EH2 = (128, 64)
        E, TOPK = (4, 2)

        def _shared_mlp(x, W1, b1, W2, b2, W3, b3):
            h = jax.nn.relu(x @ W1 + b1)
            h = jax.nn.relu(h @ W2 + b2)
            return h @ W3 + b3

        def _experts_mlp(x, eW1, eb1, eW2, eb2, eW3, eb3):
            h = jax.nn.relu(jnp.einsum('baf,efh->ebah', x, eW1) + eb1[:, None, None, :])
            h = jax.nn.relu(jnp.einsum('ebah,ehg->ebag', h, eW2) + eb2[:, None, None, :])
            o = jnp.einsum('ebag,ego->ebao', h, eW3) + eb3[:, None, None, :]
            return jnp.moveaxis(o, 0, -1)
        all_out = _experts_mlp(x, eW1, eb1, eW2, eb2, eW3, eb3)
        shared = _shared_mlp(x, sW1, sb1, sW2, sb2, sW3, sb3)
        gates = jax.nn.softmax(x @ gW + gb, axis=-1)
        topv, topi = jax.lax.top_k(gates, TOPK)
        topw = jax.nn.softmax(topv, axis=-1)
        sel = jnp.take_along_axis(all_out, topi[:, :, None, :], axis=-1)
        gated = jnp.sum(sel * topw[:, :, None, :], axis=-1)
        return shared + gated
    h = _L0_tok_ref(x)
    h = h + _L0_attn_ref(_layernorm(h, axis=-1), L0_attn_pos_phases, L0_attn_window_deltas, L0_attn_mc_w, L0_attn_mc_b, L0_attn_hop_w1, L0_attn_hop_b1, L0_attn_hop_w2, L0_attn_hop_b2, L0_attn_cpe_w, L0_attn_cpe_b, L0_attn_ve_w, L0_attn_ve_b, L0_attn_kce_w, L0_attn_kce_b, L0_attn_ksk_w1, L0_attn_ksk_b1, L0_attn_ksk_w2, L0_attn_ksk_b2, L0_attn_sg_w1, L0_attn_sg_b1, L0_attn_sg_w2, L0_attn_sg_b2, L0_attn_ln_g, L0_attn_ln_b, L0_attn_out_w, L0_attn_out_b)
    h = h + _L0_ffn_ref(_layernorm(h, axis=-1), L0_ffn_sW1, L0_ffn_sb1, L0_ffn_sW2, L0_ffn_sb2, L0_ffn_sW3, L0_ffn_sb3, L0_ffn_eW1, L0_ffn_eb1, L0_ffn_eW2, L0_ffn_eb2, L0_ffn_eW3, L0_ffn_eb3, L0_ffn_gW, L0_ffn_gb)
    return h

_drawn_inputs = setup_inputs


def setup_inputs(seed=0):
    import zlib

    import numpy as np

    out = dict(_drawn_inputs(seed))
    spreads = {'L0_attn_mc_b': (0.0, 0.8),
     'L0_attn_hop_b1': (0.0, 2.0),
     'L0_attn_hop_b2': (0.0, 2.0),
     'L0_attn_cpe_b': (0.0, 0.8),
     'L0_attn_ve_b': (0.0, 0.8),
     'L0_attn_kce_b': (0.0, 0.8),
     'L0_attn_ksk_b1': (0.0, 0.8),
     'L0_attn_ksk_b2': (0.0, 0.8),
     'L0_attn_sg_b1': (0.0, 2.0),
     'L0_attn_ln_g': (1.0, 0.6),
     'L0_attn_ln_b': (0.0, 0.8),
     'L0_attn_out_b': (0.0, 0.8),
     'L0_ffn_sb1': (0.0, 0.8),
     'L0_ffn_sb2': (0.0, 0.8),
     'L0_ffn_sb3': (0.0, 2.0),
     'L0_ffn_eb1': (0.0, 0.8),
     'L0_ffn_eb2': (0.0, 0.8),
     'L0_ffn_eb3': (0.0, 2.0),
     'L0_ffn_gb': (0.0, 0.8)}
    factors = {'L0_attn_pos_phases': 8.0,
     'L0_attn_window_deltas': 64.0,
     'L0_attn_mc_w': 8.0,
     'L0_attn_hop_w1': 8.0,
     'L0_attn_hop_w2': 8.0,
     'L0_attn_cpe_w': 8.0,
     'L0_attn_ve_w': 8.0,
     'L0_attn_kce_w': 8.0,
     'L0_attn_ksk_w1': 8.0,
     'L0_attn_ksk_w2': 8.0,
     'L0_attn_sg_w1': 8.0,
     'L0_attn_sg_w2': 23.427,
     'L0_attn_out_w': 5.452,
     'L0_ffn_sW1': 8.0,
     'L0_ffn_sW2': 8.0,
     'L0_ffn_sW3': 8.0,
     'L0_ffn_eW1': 8.0,
     'L0_ffn_eW2': 8.0,
     'L0_ffn_eW3': 8.0,
     'L0_ffn_gW': 8.0}
    for name, (base, spread) in spreads.items():
        noise = np.random.default_rng([zlib.crc32(name.encode()), seed]).standard_normal(out[name].shape)
        drawn = base * np.exp(spread * noise) if base else spread * noise
        out[name] = jnp.asarray(drawn.astype(out[name].dtype))
    for name, factor in factors.items():
        out[name] = (out[name] * factor).astype(out[name].dtype)
    return out
```

```python
from contextlib import ExitStack

import numpy as np

import concourse.bass as bass
from concourse import mybir

F32 = mybir.dt.float32
ALU = mybir.AluOpType
ACT = mybir.ActivationFunctionType
AX = mybir.AxisListType

NB, NS = 32, 4000
L, D, P, H, WN = 249, 64, 32, 4, 5
HP = 125
LP = 2 * HP
WIN, UP = 64, 4
NQ = NB // 4
QT = 4 * 2
QF = 2 * LP
NT = NB * 2
TAPS = WIN // UP + 3
NBIN = WIN // 2 + 1
E = 4
ALPHA, BETA = 0.12, 0.9
PI = float(np.pi)
PI_BELOW = float(np.nextafter(np.float32(np.pi), np.float32(0)))
ROUND = 1.5 * 2.0 ** 23
TWO_PI = (6.28125, 2 * PI - 6.28125 - (2 * PI - 6.28125) % 2.0 ** -19, (2 * PI - 6.28125) % 2.0 ** -19)



def columns(widths):
    at, out = 0, {}
    for name, w in widths:
        out[name] = (at, w)
        at += w
    return out, at


TOK_COLS, TOK_W = columns([("interp", 128), ("dft", 128), ("b_gauss", 1), ("b_poly", 1)])
MAIN_COLS, MAIN_W = columns([
    ("ident", 128), ("mask", 2 * HP), ("mean0", LP), ("mean1", HP), ("select", 2 * 128),
    ("posA", 3), ("posB", 3), ("posP", 3), ("half_pi", 1), ("minus_half", 8),
    ("pos", LP), ("hop1p", 128), ("kce_t", 128), ("kce_b", 1), ("kskc", 128),
    ("hop1", 128), ("ksk1", 128), ("sg1", 64), ("key1", 128), ("mc", 128), ("ve", 128),
    ("hopc", 128), ("hopw", 8), ("ksk2", 128), ("sg2", 2), ("outw", 128), ("outw64", 64),
    ("lnb", HP), ("lng", 1),
    ("b_hop1", 1), ("b_ksk1", 1), ("b_sg1", 1), ("b_cpe", 1), ("b_hopc", 1), ("b_ksk2", 1), ("b_sg2", 1),
    ("sW1", 128), ("sW2", 128), ("sW3", 64), ("eW1", E * 128), ("eW2", E * 64), ("eW3", 2 * 64), ("gW", 8),
    ("b_s1", 1), ("b_s2", 1), ("b_e1", E), ("b_e2", 2),
    ("r_mc", D), ("r_ve", D), ("r_hopw", H), ("r_out", D), ("r_gb", E), ("r_eb3", E * D), ("r_sb3", D),
    ("r_delta", WN),
])


def ready(u, slots=2):
    return u + (1 + slots)


def free(u, slots=2):
    return u + 1


class Chain:

    def __init__(self, eng, sem, base=0):
        self.eng, self.sem, self.base, self.n = eng, sem, base, 0

    def tick(self, ins):
        ins.then_inc(self.sem, 1)
        self.n += 1
        return ins

    def settle(self):
        self.eng.wait_ge(self.sem, self.base + self.n)


def audio_tower(nc, tok_pack, main_pack, windows, out):
    ctx = ExitStack()
    with ctx:
        def sb(name, shape, stack=ctx):
            return stack.enter_context(nc.sbuf_tensor(name, shape, F32))

        def bank(name, stack):
            return stack.enter_context(nc.psum_tensor(name, [128, 512], F32))

        def sem(name):
            return ctx.enter_context(nc.semaphore(name))

        main = sb("main", [128, MAIN_W])
        hid = sb("hid", [HP, NT * D])

        def w(name, rows=128, a=0, b=None, first=0):
            at, width = MAIN_COLS[name]
            return main[first:first + rows, at + a:at + (width if b is None else b)]

        main_loaded = sem("main_loaded")

        tokens(nc, sb, bank, sem, tok_pack, main_pack, windows, main, main_loaded, hid)
        s = setup(nc, sb, bank, sem, w, main_loaded)
        gw, lg = sb("gw", [HP, NT * E]), sb("lg", [HP, NT * E])
        cen = sb("cen", [128, NQ * 2 * QF])
        x2t = cen[:, 0:NQ * QF]
        with ExitStack() as st:
            key, sto = sb("key", [128, NQ * QF], st), sb("sto", [128, NQ * QF], st)
            cont, val = sb("cont", [HP, NT * D], st), sb("val", [HP, NT * D], st)
            wid, gat, root = sb("wid", [HP, NT * H], st), sb("gat", [HP, NT], st), sb("root", [HP, NT], st)
            mix = sb("mix", [HP, 2, NT * H], st)
            attention_inputs(nc, sb, bank, sem, w, s, hid, cen, key, sto, cont, val, wid, gat)
            window_weights(nc, sb, bank, sem, w, s, wid, gat, mix, root)
            attend(nc, sb, bank, sem, w, s, cen, key, sto, cont, val, mix, root)
            project(nc, sb, bank, sem, w, s, hid, cont, x2t, lg)
        gate_weights(nc, sb, sem, lg, gw)
        experts(nc, sb, bank, sem, w, hid, x2t, gw, out)


def tokens(nc, sb, bank, sem, tok_pack, main_pack, windows, main, main_loaded, hid):
    with ExitStack() as st:
        tok = sb("tok", [128, TOK_W], st)
        win = sb("win", [2 * TAPS, NQ * QF], st)
        power = sb("power", [HP, NT * NBIN], st)
        sq = [sb(f"sq{s}", [128, QF], st) for s in range(2)]
        poly = [sb(f"poly{s}", [128, QF], st) for s in range(2)]
        gauss = [sb(f"gauss{s}", [128, QF], st) for s in range(2)]
        kw = [sb(f"kw{s}", [128, QF], st) for s in range(2)]
        parts2 = [sb(f"parts2_{s}", [HP, 512], st) for s in range(2)]
        CW = NT * NBIN // 2
        CT = NT // 2
        mag = sb("mag", [HP, 2 * CW], st)
        d = sb("d", [HP, 2 * CW], st)
        e = sb("e", [HP, 2 * CW], st)
        mx = sb("mx", [HP, NT], st)
        psI = [bank(f"psI{s}", st) for s in range(2)]
        psD = [bank(f"psD{s}", st) for s in range(2)]

        tok_loaded, win_loaded = sem("tok_loaded"), sem("win_loaded")
        interp_ready, poly_ready, square_ready, gauss_ready = (
            sem("interp_ready"), sem("poly_ready"), sem("square_ready"), sem("gauss_ready"))
        kw_ready, dft_ready, parts_ready, power_ready = (
            sem("kw_ready"), sem("dft_ready"), sem("parts_ready"), sem("power_ready"))
        mag_ready, over_ready, mask_ready, gap_ready, exp_ready, log_ready = (
            sem("mag_ready"), sem("over_ready"), sem("mask_ready"), sem("gap_ready"), sem("exp_ready"),
            sem("log_ready"))
        vec_step = sem("tok_vec_step")

        def t(name, rows=128):
            at, width = TOK_COLS[name]
            return tok[0:rows, at:at + width]

        with nc.Block() as block:
            @block.sync
            def _(sp):
                sp.dma_start(tok[:, :], tok_pack[:, :]).then_inc(tok_loaded, 16)
                for c in range(4):
                    a, b = c * 2 * QF, (c + 1) * 2 * QF
                    sp.dma_start(win[:, a:b], windows[:, a:b]).then_inc(win_loaded, 16)
                    sp.wait_ge(win_loaded, 16 * (c + 1))
                sp.dma_start(main[:, :], main_pack[:, :]).then_inc(main_loaded, 16)

            @block.tensor
            def _(pe):
                pe.sem_inc(interp_ready, 2)
                pe.sem_inc(dft_ready, 2)
                pe.wait_ge(tok_loaded, 16)
                with pe.Fori(0, NQ // 2) as i:
                    pe.wait_ge(win_loaded, 16 * i + 16)
                    for s in range(2):
                        pe.wait_ge(poly_ready, free(2 * i + s))
                        nc.tensor.matmul(psI[s][:, 0:QF], t("interp", 2 * TAPS),
                                         win[:, bass.ds((2 * i + s) * QF, QF)], start=True, stop=True)\
                            .then_inc(interp_ready, 1)
                    for s in range(2):
                        pe.wait_ge(kw_ready, ready(2 * i + s))
                        pe.wait_ge(parts_ready, free(2 * i + s))
                        for half in range(2):
                            for pair in range(2):
                                c = pair * LP + half * HP
                                o = (half * 2 + pair) * 128
                                mm = nc.tensor.matmul(psD[s][0:HP, o:o + 128], kw[s][:, c:c + HP], t("dft"),
                                                      start=True, stop=True)
                        mm.then_inc(dft_ready, 1)

            @block.scalar
            def _(act):
                for x in (poly_ready, square_ready, gauss_ready, parts_ready):
                    act.sem_inc(x, 2)
                act.wait_ge(tok_loaded, 16)
                with act.Fori(0, NQ // 2) as i:
                    for s in range(2):
                        act.wait_ge(interp_ready, ready(2 * i + s))
                        nc.scalar.activation(sq[s][:, :], psI[s][:, 0:QF], ACT.Square, bias=t("b_gauss"))\
                            .then_inc(square_ready, 1)
                        act.wait_ge(kw_ready, free(2 * i + s))
                        nc.scalar.activation(poly[s][:, :], psI[s][:, 0:QF], ACT.Square, bias=t("b_poly"))\
                            .then_inc(poly_ready, 1)
                        act.wait_ge(square_ready, ready(2 * i + s))
                        nc.scalar.activation(gauss[s][:, :], sq[s][:, :], ACT.Exp, scale=-0.5)\
                            .then_inc(gauss_ready, 1)
                    for s in range(2):
                        act.wait_ge(dft_ready, ready(2 * i + s))
                        act.wait_ge(power_ready, free(2 * i + s))
                        nc.scalar.activation(parts2[s][:, :], psD[s][0:HP, :], ACT.Square)\
                            .then_inc(parts_ready, 1)
                act.wait_ge(power_ready, ready(NQ - 1))
                for c in range(2):
                    a, b = c * CW, (c + 1) * CW
                    nc.scalar.activation(mag[:, a:b], power[:, a:b], ACT.Sqrt).then_inc(mag_ready, 1)
                for c in range(2):
                    a, b = c * CW, (c + 1) * CW
                    act.wait_ge(over_ready, c + 1)
                    nc.scalar.activation(e[:, a:b], d[:, a:b], ACT.Tanh, scale=0.5).then_inc(mask_ready, 1)
                for c in range(2):
                    a, b = c * CW, (c + 1) * CW
                    act.wait_ge(gap_ready, c + 1)
                    nc.scalar.activation(e[:, a:b], power[:, a:b], ACT.Exp, scale=-0.5).then_inc(exp_ready, 1)
                    act.wait_ge(exp_ready, c + 1)
                    nc.scalar.activation(power[:, a:b], e[:, a:b], ACT.Ln, bias=1.0).then_inc(log_ready, 1)

            @block.vector
            def _(dve):
                dve.sem_inc(kw_ready, 2)
                dve.sem_inc(power_ready, 2)
                with dve.Fori(0, NQ // 2) as i:
                    for s in range(2):
                        dve.wait_ge(gauss_ready, ready(2 * i + s))
                        dve.wait_ge(poly_ready, ready(2 * i + s))
                        dve.wait_ge(dft_ready, free(2 * i + s))
                        nc.vector.tensor_tensor(kw[s][:, :], poly[s][:, :], gauss[s][:, :], ALU.add)\
                            .then_inc(kw_ready, 1)
                    for s in range(2):
                        dve.wait_ge(parts_ready, ready(2 * i + s))
                        v = parts2[s][:, :].rearrange("p (t f) -> p t f", f=WIN)
                        o = power[:, bass.ds((2 * i + s) * (QT * NBIN), QT * NBIN)]\
                            .rearrange("p (t f) -> p t f", f=NBIN)
                        nc.vector.tensor_copy(o[:, :, 0:NBIN:NBIN - 1], v[:, :, 0:NBIN:NBIN - 1])
                        nc.vector.tensor_tensor(o[:, :, 1:NBIN - 1], v[:, :, 1:NBIN - 1], v[:, :, NBIN:WIN],
                                                ALU.add).then_inc(power_ready, 1)
                ch = Chain(dve, vec_step)

                def view(x, c):
                    return x[:, c * CW:(c + 1) * CW].rearrange("p (t f) -> p t f", f=NBIN)

                def top(c):
                    return mx[:, c * CT:(c + 1) * CT].rearrange("p (t a) -> p t a", a=1)\
                        .broadcast_to([HP, CT, NBIN])

                for c in range(2):
                    dve.wait_ge(mag_ready, c + 1)
                    ch.tick(nc.vector.tensor_reduce(mx[:, c * CT:(c + 1) * CT], view(mag, c), AX.X, ALU.max))
                    ch.settle()
                    nc.vector.scalar_tensor_tensor(out=view(d, c), in0=top(c), scalar=-ALPHA, in1=view(mag, c),
                                                   op0=ALU.mult, op1=ALU.add).then_inc(over_ready, 1)
                for c in range(2):
                    a, b = c * CW, (c + 1) * CW
                    dve.wait_ge(mask_ready, c + 1)
                    ch.tick(nc.vector.scalar_tensor_tensor(out=mag[:, a:b], in0=e[:, a:b], scalar=1.0,
                                                           in1=mag[:, a:b], op0=ALU.add, op1=ALU.mult))
                    ch.settle()
                    ch.tick(nc.vector.scalar_tensor_tensor(out=view(d, c), in0=top(c), scalar=-2 * BETA,
                                                           in1=view(mag, c), op0=ALU.mult, op1=ALU.add))
                    ch.settle()
                    nc.vector.scalar_tensor_tensor(out=power[:, a:b], in0=d[:, a:b], scalar=-1.0, in1=d[:, a:b],
                                                   op0=ALU.mult, op1=ALU.max)\
                        .then_inc(gap_ready, 1)
                    ch.tick(nc.vector.scalar_tensor_tensor(out=view(mag, c), in0=top(c), scalar=2 * BETA,
                                                           in1=view(mag, c), op0=ALU.mult, op1=ALU.min))
                for c in range(2):
                    a, b = c * CW, (c + 1) * CW
                    dve.wait_ge(log_ready, c + 1)
                    h = hid[:, c * CT * D:(c + 1) * CT * D].rearrange("p (t f) -> p t f", f=D)
                    m, lg = view(mag, c), view(power, c)
                    ch.settle()
                    ch.tick(nc.vector.scalar_tensor_tensor(out=h[:, :, 0:NBIN], in0=m, scalar=0.5, in1=lg,
                                                           op0=ALU.mult, op1=ALU.subtract))
                    ch.settle()
                    ch.tick(nc.vector.tensor_copy(h[:, :, NBIN:D], h[:, :, NBIN - 2:0:-1]))
                ch.settle()


def setup(nc, sb, bank, sem, w, main_loaded):
    s = {}
    s["kskc"] = sb("kskc_bd", [128, 128])
    s["b_ksk"] = sb("b_ksk", [128, 1])
    s["outw"] = sb("outw_scaled", [128, 128])
    s["r_out"] = sb("r_outb", [HP, D])
    s["hop_pos"] = sb("hop_pos", [128, LP])
    s["tabA"] = sb("tabA", [128, LP])
    s["tabB"] = sb("tabB", [128, LP])
    s["cosd"] = sb("cosd", [HP, WN])
    s["sind"] = sb("sind", [HP, WN])
    s["decay"] = sb("decay", [HP, WN])
    s["b_sg2"] = sb("b_sg2_half", [HP, 1])
    with ExitStack() as loc:
        ps0, ps1 = bank("ps_setup0", loc), bank("ps_setup1", loc)
        turns, rest, shape = (sb(n, [128, LP + WN], loc) for n in ("turns", "rest", "shape"))
        shapeB = sb("shapeB", [128, LP], loc)
        setup_products, trig_args, trig_done = sem("setup_products"), sem("trig_args"), sem("trig_done")
        step, act_step = sem("setup_step"), sem("setup_act_step")
        with nc.Block() as block:
            @block.tensor
            def _(pe):
                pe.wait_ge(main_loaded, 16)
                nc.tensor.matmul(ps0[:, 0:64], w("kce_t", 64), w("kskc", 64, 0, 64), start=True, stop=True)
                nc.tensor.matmul(ps0[:, 64:65], w("kskc", 64), w("kce_b", 64), start=True, stop=True)
                nc.tensor.matmul(ps0[0:HP, 128:192], w("lnb", 64), w("outw64", 64), start=True, stop=True)
                nc.tensor.matmul(ps1[:, 0:LP], w("hop1p", 32), w("pos", 32), start=True, stop=True)\
                    .then_inc(setup_products, 1)

            @block.vector
            def _(dve):
                ch = Chain(dve, step)
                dve.wait_ge(main_loaded, 16)
                ch.tick(nc.vector.memset(s["kskc"][:, :], 0.0))
                ch.tick(nc.vector.tensor_scalar(s["outw"][:, :], w("outw"), w("lng"), None, ALU.mult))
                ch.tick(nc.vector.tensor_scalar(s["b_sg2"][:, :], w("b_sg2", HP), 0.5, None, ALU.mult))
                ch.tick(nc.vector.tensor_tensor(s["decay"][:, :], w("r_delta", HP), w("r_delta", HP), ALU.mult))
                ch.tick(nc.vector.tensor_copy(rest[:, 0:LP], w("pos")))
                ch.tick(nc.vector.memset(rest[:, LP:LP + WN], 0.0))
                ch.settle()
                ch.tick(nc.vector.tensor_scalar(rest[0:HP, LP:LP + WN], w("r_delta", HP), 0.1, None, ALU.mult))
                ch.tick(nc.vector.tensor_scalar(s["decay"][:, :], s["decay"][:, :], -0.5, None, ALU.mult))
                ch.settle()
                ch.tick(nc.vector.tensor_scalar(turns[:, :], rest[:, :], 1 / (2 * PI), ROUND, ALU.mult, ALU.add))
                ch.settle()
                ch.tick(nc.vector.tensor_scalar(turns[:, :], turns[:, :], -ROUND, None, ALU.add))
                for part in TWO_PI:
                    ch.settle()
                    ch.tick(nc.vector.scalar_tensor_tensor(out=rest[:, :], in0=turns[:, :], scalar=-part,
                                                           in1=rest[:, :], op0=ALU.mult, op1=ALU.add))
                ch.settle()
                ch.tick(nc.vector.tensor_scalar(rest[:, :], rest[:, :], PI_BELOW, -PI_BELOW, ALU.min, ALU.max))
                ch.settle()
                nc.vector.scalar_tensor_tensor(out=shape[:, 0:LP], in0=rest[:, 0:LP], scalar=w("posA", b=1),
                                               in1=rest[:, 0:LP], op0=ALU.mult, op1=ALU.max).then_inc(trig_args, 1)
                nc.vector.scalar_tensor_tensor(out=shapeB[:, :], in0=rest[:, 0:LP], scalar=w("posB", b=1),
                                               in1=rest[:, 0:LP], op0=ALU.mult, op1=ALU.max).then_inc(trig_args, 1)
                nc.vector.scalar_tensor_tensor(out=shape[0:HP, LP:], in0=rest[0:HP, LP:], scalar=-1.0,
                                               in1=rest[0:HP, LP:], op0=ALU.mult, op1=ALU.max)\
                    .then_inc(trig_args, 1)
                dve.wait_ge(setup_products, 1)
                for r in (0, 64):
                    ch.tick(nc.vector.tensor_copy(s["kskc"][r:r + 64, r:r + 64], ps0[r:r + 64, 0:64]))
                ch.tick(nc.vector.tensor_tensor(s["b_ksk"][:, :], ps0[:, 64:65], w("b_ksk1"), ALU.add))
                ch.tick(nc.vector.tensor_tensor(s["r_out"][:, :], ps0[0:HP, 128:192], w("r_out", HP), ALU.add))

            @block.scalar
            def _(act):
                act.wait_ge(trig_args, 3)
                nc.scalar.activation(s["tabA"][:, :], shape[:, 0:LP], ACT.Sin, bias=w("posA", a=2, b=3),
                                     scale=w("posA", a=1, b=2))
                nc.scalar.activation(s["tabB"][:, :], shapeB[:, :], ACT.Sin, bias=w("posB", a=2, b=3),
                                     scale=w("posB", a=1, b=2))
                nc.scalar.activation(s["cosd"][:, :], shape[0:HP, LP:], ACT.Sin, bias=w("half_pi", HP),
                                     scale=-1.0)
                nc.scalar.activation(s["sind"][:, :], rest[0:HP, LP:], ACT.Sin)
                act.wait_ge(setup_products, 1)
                nc.scalar.activation(s["hop_pos"][:, :], ps1[:, 0:LP], ACT.Identity, bias=w("b_hop1"))
    return s


def per_token(stat, n, f=D):
    return stat.rearrange("p (t a) -> p t a", a=1).broadcast_to([stat.shape[0], n, f])


def features(x, f=D):
    return x.rearrange("p (t f) -> p t f", f=f)


def row_of(x, n):
    return x.rearrange("p (a f) -> p a f", a=1).broadcast_to([x.shape[0], n, x.shape[1]])


def attention_inputs(nc, sb, bank, sem, w, s, hid, cen, key, sto, cont, val, wid, gat):
    with ExitStack() as st:
        two = range(2)
        mu, var, rstd, tg = ([sb(f"{n}{k}", [HP, QT], st) for k in two] for n in ("mu", "var", "rstd", "tg"))
        xc, xn, vraw = ([sb(f"{n}{k}", [HP, 512], st) for k in two] for n in ("xc", "xn", "vraw"))
        sqx = [sb(f"sqx{k}", [HP, 512], st) for k in two]
        xb = sb("xb", [HP, 512], st)
        xt, cm, hopin, hh, kh = ([sb(f"{n}{k}", [128, QF], st) for k in two] for n in ("xt", "cm", "hopin", "hh", "kh"))
        sh = [sb(f"sh{k}", [64, QF], st) for k in two]
        B = [[bank(f"in{k}_{j}", st) for j in range(4)] for k in two]
        (xc_ready, sqx_ready, var_ready, rstd_ready, xn_ready, hx_done, xt_psum, xt_done, cm_psum, cm_done,
         hop_psum, hopin_done, hh_done, sg_psum, sg_done, ksk_psum, ksk_done, key_psum, key_done, cont_psum,
         cont_done, val_psum, val_done, gv_done, cen0_psum, cen0_done, cen1_psum, cen1_done, st_psum, st_done,
         small_psum, width_done, tg_done, gat_ready) = (sem("in_" + n) for n in (
             "xc_ready sqx_ready var_ready rstd_ready xn_ready hx_done xt_psum xt_done cm_psum cm_done "
             "hop_psum hopin_done hh_done sg_psum sg_done ksk_psum ksk_done key_psum key_done cont_psum "
             "cont_done val_psum val_done gv_done cen0_psum cen0_done cen1_psum cen1_done st_psum st_done "
             "small_psum width_done tg_done gat_ready").split())
        vec_step, xb_ready = sem("in_vec_step"), sem("in_xb_ready")
        STEPS = 6

        def tile(x, half, pair, n=HP):
            c = pair * LP + half * HP
            return x[:, c:c + n]

        with nc.Block() as block:
            @block.tensor
            def _(pe):
                for x in (xt_psum, cm_psum, hop_psum, sg_psum, ksk_psum, key_psum, cont_psum, val_psum,
                          cen0_psum, cen1_psum, st_psum, small_psum):
                    pe.sem_inc(x, 2)
                mm = nc.tensor.matmul
                with pe.Fori(0, NQ // 2) as i:
                    for k in two:
                        u = 2 * i + k
                        b0, b1 = B[k][0], B[k][1]
                        pe.wait_ge(xn_ready, ready(u))
                        pe.wait_ge(cen1_done, free(u))
                        for half in two:
                            for pair in two:
                                o = (half * 2 + pair) * 128
                                x = nc.tensor.transpose(tile(b0, half, pair), xn[k][:, o:o + 128],
                                                        w("ident", HP, 0, HP))
                        x.then_inc(xt_psum, 1)
                        pe.wait_ge(cen0_done, free(u))
                        for pair in two:
                            mm(tile(b1, 0, pair, LP), xn[k][:, pair * 128:pair * 128 + 128], w("mean0", HP),
                               start=True, stop=False)
                            x = mm(tile(b1, 1, pair), xn[k][:, 256 + pair * 128:256 + pair * 128 + 128],
                                   w("mean1", HP), start=False, stop=True)
                        x.then_inc(cm_psum, 1)
                    for k in two:
                        u = 2 * i + k
                        b2, b3 = B[k][2], B[k][3]
                        pe.wait_ge(xt_done, ready(u))
                        pe.wait_ge(st_done, free(u))
                        mm(b2[:, 0:QF], w("hop1"), xt[k][:, :], start=True, stop=True).then_inc(hop_psum, 1)
                        pe.wait_ge(tg_done, free(u))
                        mm(b3[0:64, 0:QF], w("sg1"), xt[k][:, :], start=True, stop=True).then_inc(sg_psum, 1)
                    for k in two:
                        u = 2 * i + k
                        b0, b1 = B[k][0], B[k][1]
                        pe.wait_ge(cm_done, ready(u))
                        mm(b1[:, 0:QF], w("ksk1"), xt[k][:, :], start=True, stop=False)
                        mm(b1[:, 0:QF], s["kskc"][:, :], cm[k][:, :], start=False, stop=True)\
                            .then_inc(ksk_psum, 1)
                        mm(b0[:, 0:QF], w("key1"), xt[k][:, :], start=True, stop=True).then_inc(key_psum, 1)
                    for k in two:
                        u = 2 * i + k
                        for b, name, read, signal in ((B[k][2], "mc", hopin_done, cont_psum),
                                                      (B[k][3], "ve", sg_done, val_psum)):
                            pe.wait_ge(read, ready(u))
                            for half in two:
                                for pair in two:
                                    o = (half * 2 + pair) * 128
                                    x = mm(b[0:HP, o:o + 128], tile(xt[k], half, pair), w(name),
                                           start=True, stop=True)
                            x.then_inc(signal, 1)
                    for k in two:
                        u = 2 * i + k
                        b0, b1 = B[k][0], B[k][1]
                        pe.wait_ge(ksk_done, ready(u))
                        pe.wait_ge(hh_done, ready(u))
                        mm(b1[:, 0:QF], w("hopc", 64), hh[k][0:64, :], start=True, stop=True)\
                            .then_inc(cen0_psum, 1)
                        pe.wait_ge(key_done, ready(u))
                        mm(b0[:, 0:QF], w("hopc", 64, first=64), hh[k][64:128, :], start=True, stop=True)\
                            .then_inc(cen1_psum, 1)
                    for k in two:
                        u = 2 * i + k
                        b2, b3 = B[k][2], B[k][3]
                        pe.wait_ge(cont_done, ready(u))
                        mm(b2[:, 0:QF], w("ksk2"), kh[k][:, :], start=True, stop=True).then_inc(st_psum, 1)
                        pe.wait_ge(val_done, ready(u))
                        for half in two:
                            for pair in two:
                                o = half * 2 + pair
                                mm(b3[0:HP, o * 8:o * 8 + 8], tile(hh[k], half, pair), w("hopw"),
                                   start=True, stop=True)
                                x = mm(b3[0:HP, 32 + o * 2:34 + o * 2], tile(sh[k], half, pair), w("sg2", 64),
                                       start=True, stop=True)
                        x.then_inc(small_psum, 1)

            @block.scalar
            def _(act):
                for x in (sqx_ready, xt_done, sg_done, hh_done, ksk_done, key_done, cen0_done, cen1_done,
                          st_done, tg_done):
                    act.sem_inc(x, 2)
                f = nc.scalar.activation
                with act.Fori(0, NQ // 2) as i:
                    for k in two:
                        u = 2 * i + k
                        act.wait_ge(xc_ready, ready(u))
                        act.wait_ge(var_ready, free(u))
                        f(sqx[k][:, :], xc[k][:, :], ACT.Square).then_inc(sqx_ready, 1)
                    for k in two:
                        u = 2 * i + k
                        act.wait_ge(xt_psum, ready(u))
                        act.wait_ge(val_psum, free(u))
                        f(xt[k][:, :], B[k][0][:, 0:QF], ACT.Copy).then_inc(xt_done, 1)
                    for k in two:
                        u = 2 * i + k
                        act.wait_ge(small_psum, free(u))
                        act.wait_ge(sg_psum, ready(u))
                        f(sh[k][:, :], B[k][3][0:64, 0:QF], ACT.Gelu, bias=w("b_sg1", 64)).then_inc(sg_done, 1)
                        act.wait_ge(hopin_done, ready(u))
                        f(hh[k][:, :], hopin[k][:, :], ACT.Gelu).then_inc(hh_done, 1)
                    for k in two:
                        u = 2 * i + k
                        act.wait_ge(ksk_psum, ready(u))
                        act.wait_ge(st_psum, free(u))
                        f(kh[k][:, :], B[k][1][:, 0:QF], ACT.Gelu, bias=s["b_ksk"][:, :]).then_inc(ksk_done, 1)
                        act.wait_ge(key_psum, ready(u))
                        f(key[:, bass.ds(u * QF, QF)], B[k][0][:, 0:QF], ACT.Tanh, bias=w("b_cpe"))\
                            .then_inc(key_done, 1)
                    for k in two:
                        u = 2 * i + k
                        for parity, b, need, signal in ((0, 1, cen0_psum, cen0_done), (1, 0, cen1_psum, cen1_done)):
                            act.wait_ge(need, ready(u))
                            f(cen[:, bass.ds(u * (2 * QF) + parity * QF, QF)], B[k][b][:, 0:QF], ACT.Tanh,
                              bias=w("b_hopc")).then_inc(signal, 1)
                    for k in two:
                        u = 2 * i + k
                        act.wait_ge(st_psum, ready(u))
                        f(sto[:, bass.ds(u * QF, QF)], B[k][2][:, 0:QF], ACT.Tanh, bias=w("b_ksk2"))\
                            .then_inc(st_done, 1)
                        act.wait_ge(small_psum, ready(u))
                        act.wait_ge(width_done, ready(u))
                        act.wait_ge(gat_ready, free(u))
                        f(tg[k][:, :], B[k][3][0:HP, 32:40], ACT.Tanh, bias=s["b_sg2"][:, :], scale=0.5)\
                            .then_inc(tg_done, 1)

            @block.vector
            def _(dve):
                for x in (xc_ready, var_ready, xn_ready, cm_done, hopin_done, cont_done, val_done, width_done,
                          gat_ready):
                    dve.sem_inc(x, 2)
                v = nc.vector
                with dve.Fori(0, NQ // 2) as i:
                    ch = Chain(dve, vec_step, STEPS * i)
                    for k in two:
                        u = 2 * i + k
                        x = features(hid[:, bass.ds(u * 512, 512)])
                        ch.tick(v.tensor_reduce(mu[k][:, :], x, AX.X, ALU.add))
                        ch.settle()
                        ch.tick(v.tensor_scalar(mu[k][:, :], mu[k][:, :], -1.0 / D, None, ALU.mult))
                        ch.settle()
                        v.tensor_tensor(features(xc[k][:, :]), x, per_token(mu[k][:, :], QT), ALU.add)\
                            .then_inc(xc_ready, 1)
                    for k in two:
                        u = 2 * i + k
                        dve.wait_ge(sqx_ready, ready(u))
                        dve.wait_ge(rstd_ready, free(u))
                        ch.tick(v.tensor_reduce(var[k][:, :], features(sqx[k][:, :]), AX.X, ALU.add))
                        ch.settle()
                        v.tensor_scalar(var[k][:, :], var[k][:, :], 1.0 / D, 1e-5, ALU.mult, ALU.add)\
                            .then_inc(var_ready, 1)
                    for k in two:
                        u = 2 * i + k
                        dve.wait_ge(rstd_ready, ready(u))
                        dve.wait_ge(cm_psum, free(u))
                        dve.wait_ge(hx_done, free(u))
                        v.tensor_tensor(features(xn[k][:, :]), features(xc[k][:, :]), per_token(rstd[k][:, :], QT),
                                        ALU.mult).then_inc(xn_ready, 1)
                    for k in two:
                        u = 2 * i + k
                        dve.wait_ge(cm_psum, ready(u))
                        dve.wait_ge(ksk_psum, free(u))
                        v.tensor_copy(cm[k][:, :], B[k][1][:, 0:QF]).then_inc(cm_done, 1)
                    for k in two:
                        u = 2 * i + k
                        dve.wait_ge(hop_psum, ready(u))
                        dve.wait_ge(hh_done, free(u))
                        v.tensor_tensor(features(hopin[k][:, :], LP), features(B[k][2][:, 0:QF], LP),
                                        row_of(s["hop_pos"][:, :], 2), ALU.add).then_inc(hopin_done, 1)
                    for k in two:
                        u = 2 * i + k
                        dve.wait_ge(cont_psum, ready(u))
                        v.tensor_tensor(features(cont[:, bass.ds(u * 512, 512)]), features(B[k][2][0:HP, :]),
                                        row_of(w("r_mc", HP), QT), ALU.add).then_inc(cont_done, 1)
                        dve.wait_ge(val_psum, ready(u))
                        dve.wait_ge(gv_done, free(u))
                        v.tensor_tensor(features(vraw[k][:, :]), features(B[k][3][0:HP, :]),
                                        row_of(w("r_ve", HP), QT), ALU.add).then_inc(val_done, 1)
                    for k in two:
                        u = 2 * i + k
                        dve.wait_ge(small_psum, ready(u))
                        v.tensor_tensor(features(wid[:, bass.ds(u * 32, 32)], H), features(B[k][3][0:HP, 0:32], H),
                                        row_of(w("r_hopw", HP), QT), ALU.add).then_inc(width_done, 1)
                        dve.wait_ge(tg_done, ready(u))
                        v.tensor_scalar(gat[:, bass.ds(u * QT, QT)], tg[k][:, :], 0.5, 0.5, ALU.mult, ALU.add)\
                            .then_inc(gat_ready, 1)
                    assert ch.n == STEPS

            @block.gpsimd
            def _(pool):
                for x in (rstd_ready, hx_done, gv_done):
                    pool.sem_inc(x, 2)
                g = nc.gpsimd
                with pool.Fori(0, NQ // 2) as i:
                    for k in two:
                        u = 2 * i + k
                        pool.wait_ge(var_ready, ready(u))
                        pool.wait_ge(xn_ready, free(u))
                        g.tensor_tensor(rstd[k][:, :], var[k][:, :], w("minus_half", HP), ALU.pow)\
                            .then_inc(rstd_ready, 1)
                    for k in two:
                        u = 2 * i + k
                        pool.wait_ge(xn_ready, ready(u))
                        pool.wait_ge(hx_done, free(u + 1))
                        g.tensor_tensor(features(xb[:, :]), features(xn[k][:, :]), row_of(s["r_out"][:, :], QT),
                                        ALU.add).then_inc(xb_ready, 1)
                        pool.wait_ge(xb_ready, u + 1)
                        h = hid[:, bass.ds(u * 512, 512)]
                        g.tensor_tensor(h, h, xb[:, :], ALU.add).then_inc(hx_done, 1)
                    for k in two:
                        u = 2 * i + k
                        pool.wait_ge(val_done, ready(u))
                        pool.wait_ge(gat_ready, ready(u))
                        g.tensor_tensor(features(val[:, bass.ds(u * 512, 512)]), features(vraw[k][:, :]),
                                        per_token(gat[:, bass.ds(u * QT, QT)], QT), ALU.mult)\
                            .then_inc(gv_done, 1)


def window_weights(nc, sb, bank, sem, w, s, wid, gat, mix, root):
    with ExitStack() as st:
        n = NT * H
        ew, recip, both, total = (sb(a, [HP, b], st) for a, b in (
            ("ew", WN * n), ("recip", n), ("both", n), ("total", n)))
        cum, half = sb("cum", [HP, NT], st), sb("cum_half", [HP, NT], st)
        ps = bank("ps_cum", st)
        width_ready, recip_ready, ew_ready, cum_psum, cum_ready, step = (sem("ww_" + x) for x in (
            "width_ready", "recip_ready", "ew_ready", "cum_psum", "cum_ready", "step"))
        g = gat[:, :].rearrange("p (q h b) -> p q h b", h=2, b=4)

        with nc.Block() as block:
            @block.tensor
            def _(pe):
                m = w("mask", HP)
                nc.tensor.matmul(ps[0:HP, 0:32], m[:, 0:HP], g[:, :, 0, :], start=True, stop=True)
                nc.tensor.matmul(ps[0:HP, 32:64], m[:, HP:2 * HP], g[:, :, 0, :], start=True, stop=False)
                nc.tensor.matmul(ps[0:HP, 32:64], m[:, 0:HP], g[:, :, 1, :], start=False, stop=True)\
                    .then_inc(cum_psum, 1)

            @block.scalar
            def _(act):
                nc.scalar.activation(both[:, :], wid[:, :], ACT.Tanh, scale=0.5).then_inc(width_ready, 1)
                act.wait_ge(recip_ready, 1)
                for d in range(WN):
                    nc.scalar.activation(ew[:, d * n:(d + 1) * n], recip[:, :], ACT.Exp,
                                         scale=s["decay"][:, d:d + 1]).then_inc(ew_ready, 1)

            @block.vector
            def _(dve):
                v = nc.vector
                ch = Chain(dve, step)
                dve.wait_ge(width_ready, 1)
                ch.tick(v.tensor_scalar(both[:, :], both[:, :], 1.1, None, ALU.add))
                ch.settle()
                ch.tick(v.tensor_tensor(both[:, :], both[:, :], both[:, :], ALU.mult))
                ch.settle()
                ch.tick(v.tensor_scalar(both[:, :], both[:, :], 1e-6, None, ALU.add))
                ch.settle()
                v.reciprocal(recip[:, :], both[:, :]).then_inc(recip_ready, 1)
                dve.wait_ge(cum_psum, 1)
                v.tensor_scalar(cum[:, :].rearrange("p (q h b) -> p h q b", h=2, b=4),
                                ps[0:HP, 0:64].rearrange("p (h q b) -> p h q b", h=2, b=4), 1.0, None, ALU.max)\
                    .then_inc(cum_ready, 1)
                for d in range(WN):
                    e = ew[:, d * n:(d + 1) * n]
                    dve.wait_ge(ew_ready, d + 1)
                    ch.settle()
                    if d == 0:
                        ch.tick(v.tensor_scalar(total[:, :], e, 1e-6, None, ALU.add))
                        ch.tick(v.tensor_scalar(mix[:, 0, :], e, s["cosd"][:, d:d + 1], None, ALU.mult))
                        ch.tick(v.tensor_scalar(mix[:, 1, :], e, s["sind"][:, d:d + 1], None, ALU.mult))
                        continue
                    ch.tick(v.tensor_tensor(total[:, :], total[:, :], e, ALU.add))
                    for a, tab in ((0, "cosd"), (1, "sind")):
                        ch.tick(v.scalar_tensor_tensor(out=mix[:, a, :], in0=e, scalar=s[tab][:, d:d + 1],
                                                       in1=mix[:, a, :], op0=ALU.mult, op1=ALU.add))
                ch.settle()
                ch.tick(v.reciprocal(total[:, :], total[:, :]))
                ch.settle()
                for a in range(2):
                    ch.tick(v.scalar_tensor_tensor(out=mix[:, a, :], in0=mix[:, a, :],
                                                   scalar=1.0 / (H * P ** 0.5), in1=total[:, :],
                                                   op0=ALU.mult, op1=ALU.mult))

            @block.gpsimd
            def _(pool):
                nc.gpsimd.memset(half[:, :], -0.5).then_inc(cum_ready, 1)
                pool.wait_ge(cum_ready, 2)
                nc.gpsimd.tensor_tensor(cum[:, :], cum[:, :], half[:, :], ALU.pow).then_inc(cum_ready, 1)
                pool.wait_ge(cum_ready, 3)
                nc.gpsimd.tensor_scalar(root[:, :], cum[:, :], P ** -0.5, None, ALU.mult)


def done(n, back=0):
    return n + (9 - back)


def attend(nc, sb, bank, sem, w, s, cen, key, sto, cont, val, mix, root):
    with ExitStack() as st:
        two = range(2)
        kk, qq = ([sb(f"{n}{k}", [128, QF], st) for k in two] for n in ("kk", "qq"))
        mag = sb("cen_abs", [128, 2 * QF], st)
        cs = [sb(f"cs{k}", [128, 4, 2, LP], st) for k in two]
        ab = [sb(f"ab{k}", [HP, 2, QT * H, P], st) for k in two]
        ua, vb = (sb(n, [128, 2, LP], st) for n in ("ua", "vb"))
        turned = [sb(f"turned{k}", [128, 2, LP], st) for k in two]
        qd = [sb(f"qd{k}", [128, LP], st) for k in two]
        sm = [sb(f"sm{k}", [HP, 6 * HP], st) for k in two]
        part = sb("part", [HP, 512], st)
        psAB, psO, psD, psF, psP1, psP2 = (bank(f"at_{n}", st) for n in ("ab", "o", "d", "f", "p1", "p2"))
        ku_ready, ks_ready, abs_done, cs_ready, ab_ready, comb_ready, part_ready = (sem("at_" + n) for n in (
            "ku_ready", "ks_ready", "abs_done", "cs_ready", "ab_ready", "comb_ready", "part_ready"))
        ab_psum, uv_ready, y_ready, o_psum, qd_ready, s_psum, smd_ready, smf_ready, pv_psum = (
            sem("at_" + n) for n in ("ab_psum", "uv_ready", "y_ready", "o_psum", "qd_ready", "s_psum",
                                     "smd_ready", "smf_ready", "pv_psum"))
        BODY = 8
        DIAG, OFF = ((0, HP), (2 * HP, 3 * HP)), (4 * HP, 5 * HP)

        def where(n):
            return n // 4 % 2, n % 4 // 2, n % 2

        with nc.Block() as block:
            @block.gpsimd
            def _(pool):
                pool.sem_inc(ab_ready, 2)
                with pool.Fori(0, NQ // 2) as i:
                    for k in two:
                        pool.wait_ge(ab_psum, done(BODY * i + 4 * k + 3, BODY))
                        for a in two:
                            m = mix[:, a, bass.ds((2 * i + k) * (QT * H), QT * H)]
                            x = nc.gpsimd.tensor_copy(ab[k][:, a, :, :], per_token(m, QT * H, P))
                        x.then_inc(ab_ready, 1)

            @block.scalar
            def _(act):
                for x in (ks_ready, cs_ready):
                    act.sem_inc(x, 2)
                act.sem_inc(smf_ready, BODY)
                f = nc.scalar.activation

                def centres(u, k):
                    c = cen[:, bass.ds(u * (2 * QF), 2 * QF)]
                    act.wait_ge(cs_ready, ready(u - 1))
                    act.wait_ge(uv_ready, done(4 * u + 3, BODY))
                    f(mag[:, :], c, ACT.Abs).then_inc(abs_done, 1)
                    f(cs[k][:, :, 1, :], features(c, LP), ACT.Sin, scale=PI_BELOW)
                    act.wait_ge(abs_done, u + 1)
                    f(cs[k][:, :, 0, :], features(mag[:, :], LP), ACT.Sin, bias=w("half_pi"),
                      scale=-PI_BELOW).then_inc(cs_ready, 1)

                def keys(u, k):
                    act.wait_ge(ku_ready, ready(u))
                    for x in (kk[k], qq[k]):
                        y = f(x[:, :], x[:, :], ACT.Sin, bias=w("posP", a=2, b=3), scale=w("posP", a=1, b=2))
                    y.then_inc(ks_ready, 1)

                def copy_off(g, n):
                    act.wait_ge(s_psum, done(g))
                    act.wait_ge(pv_psum, done(g, 2))
                    f(sm[n % 2][:, 4 * HP:6 * HP], psF[0:HP, 0:2 * HP], ACT.Copy).then_inc(smf_ready, 1)

                def body(i, last):
                    for n in range(BODY):
                        g = BODY * i + n
                        if n % 4 == 0 and not (last and n // 4 + 1 > 1):
                            centres(2 * i + n // 4 + 1, (n // 4 + 1) % 2)
                        if n % 4 == 1 and not (last and n // 4 + 1 > 1):
                            keys(2 * i + n // 4 + 1, (n // 4 + 1) % 2)
                        if not (last and n + 1 >= BODY):
                            copy_off(g + 1, n + 1)

                centres(0, 0)
                keys(0, 0)
                copy_off(0, 0)
                with act.Fori(0, NQ // 2 - 1) as i:
                    body(i, False)
                body(NQ // 2 - 1, True)

            @block.tensor
            def _(pe):
                for x in (ab_psum, o_psum, s_psum, pv_psum):
                    pe.sem_inc(x, BODY)
                mm = nc.tensor.matmul

                def spread(i, n):
                    k, parity, pair = where(n)
                    pe.wait_ge(ab_ready, ready(2 * i + n // 4))
                    pe.wait_ge(uv_ready, done(BODY * i + n, 1))
                    for a in two:
                        for half in two:
                            t = (half * 4 + pair * 2 + parity) * H
                            src = ab[k][:, a, t:t + H, :].rearrange("p h f -> p (h f)")
                            x = nc.tensor.transpose(psAB[:, a * LP + half * HP:a * LP + half * HP + HP], src,
                                                    w("ident", HP, 0, HP))
                    x.then_inc(ab_psum, 1)

                def query(i, n):
                    g = BODY * i + n
                    pe.wait_ge(y_ready, done(g))
                    pe.wait_ge(qd_ready, done(g, 1))
                    mm(psO[:, 0:LP], w("select", b=128), turned[n % 2][:, 0, :], start=True, stop=False)
                    mm(psO[:, 0:LP], w("select", a=128), turned[n % 2][:, 1, :], start=False, stop=True)\
                        .then_inc(o_psum, 1)

                def scores(i, n):
                    k, parity, pair = where(n)
                    g = BODY * i + n
                    r, c = 64 * parity, pair * LP
                    pe.wait_ge(ks_ready, ready(2 * i + n // 4))
                    pe.wait_ge(qd_ready, done(g))
                    pe.wait_ge(smd_ready, done(g, 1))
                    pe.wait_ge(smf_ready, done(g, 1))
                    for j, (keys, q) in enumerate(((s["tabA"], qd[n % 2]),
                                                   (kk[k][r:r + 64, c:c + LP], qq[k][r:r + 64, c:c + LP]))):
                        for m, l in ((0, 0), (0, 1), (1, 1)):
                            b, o = (psD, DIAG[j][m]) if m == l else (psF, j * HP)
                            x = mm(b[0:HP, o:o + HP], keys[:, m * HP:m * HP + HP], q[:, l * HP:l * HP + HP],
                                   start=True, stop=True)
                    x.then_inc(s_psum, 1)

                def weigh(i, n):
                    k, parity, pair = where(n)
                    b = pair * 2 + parity
                    g = BODY * i + n
                    pe.wait_ge(smd_ready, done(g))
                    pe.wait_ge(smf_ready, done(g))
                    if n % 4 == 0:
                        pe.wait_ge(comb_ready, ready(2 * i + n // 4 - 1))
                    sc = sm[n % 2]
                    for j, (ps, rows) in enumerate(((psP1, cont), (psP2, val))):
                        first = rows[:, bass.ds((2 * i + k) * 512 + b * D, D)]
                        second = rows[:, bass.ds((2 * i + k) * 512 + (4 + b) * D, D)]
                        mm(ps[0:HP, b * D:b * D + D], sc[:, DIAG[j][0]:DIAG[j][0] + HP], first,
                           start=True, stop=True)
                        o = ps[0:HP, (4 + b) * D:(5 + b) * D]
                        mm(o, sc[:, OFF[j]:OFF[j] + HP], first, start=True, stop=False)
                        x = mm(o, sc[:, DIAG[j][1]:DIAG[j][1] + HP], second, start=False, stop=True)
                    x.then_inc(pv_psum, 1)

                def body(i, last):
                    for n in range(BODY):
                        for stage, ahead in ((spread, 3), (query, 2), (scores, 1), (weigh, 0)):
                            if not (last and n + ahead >= BODY):
                                stage(i, n + ahead)

                for stage, n in ((spread, 0), (spread, 1), (query, 0), (spread, 2), (query, 1), (scores, 0)):
                    stage(0, n)
                with pe.Fori(0, NQ // 2 - 1) as i:
                    body(i, False)
                body(NQ // 2 - 1, True)

            @block.vector
            def _(dve):
                for x in (uv_ready, y_ready, qd_ready, smd_ready):
                    dve.sem_inc(x, BODY)
                for x in (ku_ready, comb_ready):
                    dve.sem_inc(x, 2)
                v = nc.vector

                def keys(u, k):
                    dve.wait_ge(s_psum, done(4 * u + 3, BODY))
                    for x, src in ((kk[k], sto), (qq[k], key)):
                        p = src[:, bass.ds(u * QF, QF)]
                        y = v.scalar_tensor_tensor(out=x[:, :], in0=p, scalar=w("posP", b=1), in1=p,
                                                   op0=ALU.mult, op1=ALU.max)
                    y.then_inc(ku_ready, 1)

                def turn(i, n):
                    k, parity, pair = where(n)
                    g = BODY * i + n
                    dve.wait_ge(ab_psum, done(g))
                    dve.wait_ge(cs_ready, ready(2 * i + n // 4))
                    dve.wait_ge(y_ready, done(g, 1))
                    dve.wait_ge(o_psum, done(g, 2))
                    c = cs[k][:, parity * 2 + pair, :, :]
                    v.tensor_tensor(ua[:, :, :], c, row_of(psAB[:, 0:LP], 2), ALU.mult)
                    v.tensor_tensor(vb[:, :, :], c[:, 1::-1, :], row_of(psAB[:, LP:2 * LP], 2), ALU.mult)\
                        .then_inc(uv_ready, 1)
                    dve.wait_ge(uv_ready, done(g))
                    y = turned[n % 2]
                    v.tensor_tensor(y[:, 0, :], ua[:, 0, :], vb[:, 0, :], ALU.subtract)
                    v.tensor_tensor(y[:, 1, :], ua[:, 1, :], vb[:, 1, :], ALU.add).then_inc(y_ready, 1)

                def place(i, n):
                    g = BODY * i + n
                    dve.wait_ge(o_psum, done(g))
                    dve.wait_ge(s_psum, done(g, 2))
                    v.tensor_tensor(qd[n % 2][:, :], psO[:, 0:LP], s["tabB"][:, :], ALU.mult)\
                        .then_inc(qd_ready, 1)

                def mask(i, n):
                    g = BODY * i + n
                    dve.wait_ge(s_psum, done(g))
                    dve.wait_ge(pv_psum, done(g, 2))
                    v.tensor_tensor(features(sm[n % 2][:, 0:4 * HP], HP), features(psD[0:HP, 0:4 * HP], HP),
                                    row_of(w("mask", HP, 0, HP), 4), ALU.mult).then_inc(smd_ready, 1)

                def combine(u):
                    dve.wait_ge(pv_psum, done(4 * u + 3))
                    dve.wait_ge(comb_ready, ready(u - 1))
                    v.tensor_tensor(features(part[:, :]), features(psP2[0:HP, :]),
                                    per_token(root[:, bass.ds(u * QT, QT)], QT), ALU.mult).then_inc(part_ready, 1)
                    dve.wait_ge(part_ready, u + 1)
                    c = cont[:, bass.ds(u * 512, 512)]
                    v.tensor_tensor(c, part[:, :], psP1[0:HP, :], ALU.add).then_inc(comb_ready, 1)

                def body(i, last):
                    for n in range(BODY):
                        if n % 4 == 1 and not (last and n // 4 + 1 > 1):
                            keys(2 * i + n // 4 + 1, (n // 4 + 1) % 2)
                        for stage, ahead in ((turn, 3), (place, 2), (mask, 1)):
                            if not (last and n + ahead >= BODY):
                                stage(i, n + ahead)
                        if n % 4 == 3:
                            combine(2 * i + n // 4)

                keys(0, 0)
                for stage, n in ((turn, 0), (turn, 1), (place, 0), (turn, 2), (place, 1), (mask, 0)):
                    stage(0, n)
                with dve.Fori(0, NQ // 2 - 1) as i:
                    body(i, False)
                body(NQ // 2 - 1, True)


class Norm:

    def __init__(self, name, sb, sem, st):
        self.mu, self.var, self.rstd = ([sb(f"{name}_{n}{k}", [HP, QT], st) for k in range(2)]
                                        for n in ("mu", "var", "rstd"))
        self.xc, self.sq, self.xn = ([sb(f"{name}_{n}{k}", [HP, 512], st) for k in range(2)]
                                     for n in ("xc", "sq", "xn"))
        self.mu_ready, self.xc_ready, self.sq_ready, self.sum_ready, self.var_ready, self.rstd_ready, \
            self.xn_ready = (sem(f"{name}_{n}") for n in (
                "mu_ready", "xc_ready", "sq_ready", "sum_ready", "var_ready", "rstd_ready", "xn_ready"))


def project(nc, sb, bank, sem, w, s, hid, comb, x2t, lg):
    with ExitStack() as st:
        two = range(2)
        N1, N2 = Norm("n1", sb, sem, st), Norm("n2", sb, sem, st)
        ct, xs = ([sb(f"{n}{k}", [128, QF], st) for k in two] for n in ("ct", "xs"))
        new = [sb(f"new{k}", [HP, 512], st) for k in two]
        B = [[bank(f"pr{k}_{j}", st) for j in range(4)] for k in two]
        ct_psum, ct_done, out_psum, hid_done, xs_psum, xs_done, xcopy_done, lg_psum, lg_done, hid_stored = (
            sem("pr_" + n) for n in ("ct_psum", "ct_done", "out_psum", "hid_done", "xs_psum", "xs_done",
                                     "xcopy_done", "lg_psum", "lg_done", "hid_stored"))

        def centre(dve, N, k, u, x):
            v = nc.vector
            v.tensor_reduce(N.mu[k][:, :], x, AX.X, ALU.add).then_inc(N.mu_ready, 1)
            dve.wait_ge(N.mu_ready, 2 * u + 1)
            v.tensor_scalar(N.mu[k][:, :], N.mu[k][:, :], -1.0 / D, None, ALU.mult).then_inc(N.mu_ready, 1)
            dve.wait_ge(N.mu_ready, 2 * u + 2)
            v.tensor_tensor(features(N.xc[k][:, :]), x, per_token(N.mu[k][:, :], QT), ALU.add)\
                .then_inc(N.xc_ready, 1)

        def variance(dve, N, k, u):
            v = nc.vector
            dve.wait_ge(N.sq_ready, ready(u))
            dve.wait_ge(N.rstd_ready, free(u))
            v.tensor_reduce(N.var[k][:, :], features(N.sq[k][:, :]), AX.X, ALU.add).then_inc(N.sum_ready, 1)
            dve.wait_ge(N.sum_ready, u + 1)
            v.tensor_scalar(N.var[k][:, :], N.var[k][:, :], 1.0 / D, 1e-5, ALU.mult, ALU.add)\
                .then_inc(N.var_ready, 1)

        def scale(dve, N, k, u, read):
            dve.wait_ge(N.rstd_ready, ready(u))
            dve.wait_ge(read, free(u))
            nc.vector.tensor_tensor(features(N.xn[k][:, :]), features(N.xc[k][:, :]),
                                    per_token(N.rstd[k][:, :], QT), ALU.mult).then_inc(N.xn_ready, 1)

        def square(act, N, k, u):
            act.wait_ge(N.xc_ready, ready(u))
            act.wait_ge(N.var_ready, free(u))
            nc.scalar.activation(N.sq[k][:, :], N.xc[k][:, :], ACT.Square).then_inc(N.sq_ready, 1)

        def root(pool, N, k, u):
            pool.wait_ge(N.var_ready, ready(u))
            pool.wait_ge(N.xn_ready, free(u))
            nc.gpsimd.tensor_tensor(N.rstd[k][:, :], N.var[k][:, :], w("minus_half", HP), ALU.pow)\
                .then_inc(N.rstd_ready, 1)

        def turn(dst, src):
            for half in two:
                for pair in two:
                    o, c = (half * 2 + pair) * 128, pair * LP + half * HP
                    x = nc.tensor.transpose(dst[:, c:c + HP], src[:, o:o + 128], w("ident", HP, 0, HP))
            return x

        with nc.Block() as block:
            @block.vector
            def _(dve):
                for N in (N1, N2):
                    for x in (N.xc_ready, N.var_ready, N.xn_ready):
                        dve.sem_inc(x, 2)
                dve.sem_inc(hid_done, 2)
                dve.sem_inc(lg_done, 2)
                with dve.Fori(0, NQ // 2) as i:
                    for k in two:
                        centre(dve, N1, k, 2 * i + k, features(comb[:, bass.ds((2 * i + k) * 512, 512)]))
                    for k in two:
                        variance(dve, N1, k, 2 * i + k)
                    for k in two:
                        scale(dve, N1, k, 2 * i + k, ct_psum)
                    for k in two:
                        u = 2 * i + k
                        h = hid[:, bass.ds(u * 512, 512)]
                        dve.wait_ge(out_psum, ready(u))
                        dve.wait_ge(hid_stored, free(u))
                        nc.vector.tensor_tensor(new[k][:, :], h, B[k][1][0:HP, :], ALU.add).then_inc(hid_done, 1)
                        dve.wait_ge(hid_done, ready(u))
                        centre(dve, N2, k, u, features(new[k][:, :]))
                    for k in two:
                        variance(dve, N2, k, 2 * i + k)
                    for k in two:
                        scale(dve, N2, k, 2 * i + k, xs_psum)
                    for k in two:
                        u = 2 * i + k
                        dve.wait_ge(lg_psum, ready(u))
                        nc.vector.tensor_tensor(features(lg[:, bass.ds(u * QT * E, QT * E)], E),
                                                features(B[k][3][0:HP, 0:QT * E], E), row_of(w("r_gb", HP), QT),
                                                ALU.add).then_inc(lg_done, 1)

            @block.scalar
            def _(act):
                for x in (N1.sq_ready, N2.sq_ready, ct_done, xs_done):
                    act.sem_inc(x, 2)
                with act.Fori(0, NQ // 2) as i:
                    for k in two:
                        square(act, N1, k, 2 * i + k)
                    for k in two:
                        u = 2 * i + k
                        act.wait_ge(ct_psum, ready(u))
                        act.wait_ge(out_psum, free(u))
                        nc.scalar.activation(ct[k][:, :], B[k][0][:, 0:QF], ACT.Copy).then_inc(ct_done, 1)
                    for k in two:
                        square(act, N2, k, 2 * i + k)
                    for k in two:
                        u = 2 * i + k
                        act.wait_ge(xs_psum, ready(u))
                        act.wait_ge(lg_psum, free(u))
                        act.wait_ge(xcopy_done, free(u))
                        nc.scalar.activation(xs[k][:, :], B[k][2][:, 0:QF], ACT.Copy).then_inc(xs_done, 1)

            @block.gpsimd
            def _(pool):
                for x in (N1.rstd_ready, N2.rstd_ready, xcopy_done, hid_stored):
                    pool.sem_inc(x, 2)
                with pool.Fori(0, NQ // 2) as i:
                    for k in two:
                        root(pool, N1, k, 2 * i + k)
                    for k in two:
                        root(pool, N2, k, 2 * i + k)
                    for k in two:
                        pool.wait_ge(hid_done, ready(2 * i + k))
                        nc.gpsimd.tensor_copy(hid[:, bass.ds((2 * i + k) * 512, 512)], new[k][:, :])\
                            .then_inc(hid_stored, 1)
                    for k in two:
                        u = 2 * i + k
                        pool.wait_ge(xs_done, ready(u))
                        nc.gpsimd.tensor_copy(x2t[:, bass.ds(u * QF, QF)], xs[k][:, :]).then_inc(xcopy_done, 1)

            @block.tensor
            def _(pe):
                for x in (ct_psum, out_psum, xs_psum, lg_psum):
                    pe.sem_inc(x, 2)
                mm = nc.tensor.matmul
                with pe.Fori(0, NQ // 2) as i:
                    for k in two:
                        u = 2 * i + k
                        pe.wait_ge(N1.xn_ready, ready(u))
                        pe.wait_ge(ct_done, free(u))
                        turn(B[k][0], N1.xn[k]).then_inc(ct_psum, 1)
                    for k in two:
                        u = 2 * i + k
                        pe.wait_ge(ct_done, ready(u))
                        pe.wait_ge(hid_done, free(u))
                        for half in two:
                            for pair in two:
                                o, c = (half * 2 + pair) * 128, pair * LP + half * HP
                                x = mm(B[k][1][0:HP, o:o + 128], ct[k][:, c:c + HP], s["outw"][:, :],
                                       start=True, stop=True)
                        x.then_inc(out_psum, 1)
                    for k in two:
                        u = 2 * i + k
                        pe.wait_ge(N2.xn_ready, ready(u))
                        pe.wait_ge(xs_done, free(u))
                        turn(B[k][2], N2.xn[k]).then_inc(xs_psum, 1)
                    for k in two:
                        u = 2 * i + k
                        pe.wait_ge(xs_done, ready(u))
                        pe.wait_ge(lg_done, free(u))
                        for half in two:
                            for pair in two:
                                o, c = (half * 2 + pair) * 8, pair * LP + half * HP
                                x = mm(B[k][3][0:HP, o:o + 8], xs[k][:, c:c + HP], w("gW"), start=True, stop=True)
                        x.then_inc(lg_psum, 1)


def gate_weights(nc, sb, sem, lg, gw):
    with ExitStack() as st:
        mx, tot = sb("g_mx", [HP, NT], st), sb("g_tot", [HP, NT], st)
        gates, ex, rank, beats = (sb(n, [HP, NT * E], st) for n in ("gates", "ex", "rank", "beats"))
        arg_ready, ex_ready, step = sem("g_arg_ready"), sem("g_ex_ready"), sem("g_step")
        with nc.Block() as block:
            @block.scalar
            def _(act):
                for r in range(2):
                    act.wait_ge(arg_ready, r + 1)
                    nc.scalar.activation(ex[:, :], ex[:, :], ACT.Exp).then_inc(ex_ready, 1)

            @block.vector
            def _(dve):
                v = nc.vector
                ch = Chain(dve, step)

                def less_max(src):
                    ch.tick(v.tensor_reduce(mx[:, :], features(src[:, :], E), AX.X, ALU.max))
                    ch.settle()
                    v.tensor_tensor(features(ex[:, :], E), features(src[:, :], E), per_token(mx[:, :], NT, E),
                                    ALU.subtract).then_inc(arg_ready, 1)

                def normalise(dst):
                    ch.tick(v.tensor_reduce(tot[:, :], features(ex[:, :], E), AX.X, ALU.add))
                    ch.settle()
                    ch.tick(v.reciprocal(tot[:, :], tot[:, :]))
                    ch.settle()
                    ch.tick(v.tensor_tensor(features(dst[:, :], E), features(ex[:, :], E),
                                            per_token(tot[:, :], NT, E), ALU.mult))
                    ch.settle()

                less_max(lg)
                dve.wait_ge(ex_ready, 1)
                normalise(gates)
                g, r, b = (features(x[:, :], E) for x in (gates, rank, beats))
                for a in range(E):
                    ch.tick(v.memset(r[:, :, a], float(E - 1 - a)))
                ch.settle()
                for a in range(E - 1):
                    n = E - 1 - a
                    low = gates[:, a:NT * E:E].rearrange("p (t o) -> p t o", o=1).broadcast_to([HP, NT, n])
                    ch.tick(v.tensor_tensor(b[:, :, 0:n], low, g[:, :, a + 1:E], ALU.is_ge))
                    ch.settle()
                    ch.tick(v.tensor_tensor(r[:, :, a + 1:E], r[:, :, a + 1:E], b[:, :, 0:n], ALU.add))
                    ch.tick(v.tensor_reduce(mx[:, :], b[:, :, 0:n], AX.X, ALU.add))
                    ch.settle()
                    ch.tick(v.tensor_tensor(r[:, :, a], r[:, :, a], mx[:, :], ALU.subtract))
                    ch.settle()
                less_max(gates)
                dve.wait_ge(ex_ready, 2)
                ch.tick(v.scalar_tensor_tensor(out=ex[:, :], in0=rank[:, :], scalar=1.5, in1=ex[:, :],
                                               op0=ALU.is_lt, op1=ALU.mult))
                ch.settle()
                normalise(gw)


def experts(nc, sb, bank, sem, w, hid, x2t, gw, out):
    with ExitStack() as st:
        two = range(2)
        xs = [sb(f"ex_x{k}", [128, QF], st) for k in two]
        g4 = [sb(f"ex_g{k}", [HP, QT * E, 64], st) for k in two]
        t1 = sb("ex_t1", [128, QF], st)
        s2 = [sb(f"ex_s2_{p}", [128, QF], st) for p in two]
        h1 = [sb(f"ex_h1_{j}", [128, QF], st) for j in range(8)]
        zr = [sb(f"ex_zr{p}", [128, QF], st) for p in two]
        zg = [sb(f"ex_zg{j}", [128, QF], st) for j in range(4)]
        tmp = sb("ex_tmp", [HP, 512], st)
        base = [sb(f"ex_base{k}", [HP, 512], st) for k in two]
        y = [sb(f"ex_y{k}", [HP, 512], st) for k in two]
        A = [bank(f"exA{j}", st) for j in range(3)]
        Z = [bank(f"exZ{j}", st) for j in two]
        G = [bank(f"exG{j}", st) for j in two]
        Y = bank("exY", st)

        plan = [("t", 0), ("w1", 0, 0), ("s2", 0), ("w1", 0, 1), ("z", 0, 0), ("t", 1), ("z", 0, 1), ("w1", 1, 0),
                ("y", 0), ("s2", 1), ("w1", 1, 1), ("z", 1, 0), ("z", 1, 1), ("y", 1)]
        a_jobs = []
        for job in plan:
            if job[0] == "t":
                a_jobs.append(("t", job[1], 0, 0, 0))
            elif job[0] == "s2":
                a_jobs += [("s2", job[1], 0, 0, p) for p in two]
            elif job[0] == "w1":
                a_jobs += [("w1", job[1], job[2], e, p) for e in two for p in two]
        NA = len(a_jobs)
        a_users = [len(range(b, NA, 3)) for b in range(3)]
        on_act = [j % 2 == 0 for j in range(NA)]
        a_filled = [sem(f"ex_a_filled{b}") for b in range(3)]
        a_emptied = [sem(f"ex_a_emptied{b}") for b in range(3)]
        (x_ready, g_ready, w1_done, s2_done, z_psum, zr_done, g_psum, zg_done, y_psum, y_done, base_step) = (
            sem("ex_" + n) for n in ("x_ready", "g_ready", "w1_done", "s2_done", "z_psum", "zr_done", "g_psum",
                                     "zg_done", "y_psum", "y_done", "base_step"))
        out_stored = [sem(f"ex_out_stored{k}") for k in two]

        def a_index(kind, slot, pair=0, e=0, parity=0):
            return a_jobs.index((kind, slot, pair, e, parity))

        def a_fill_value(i, j):
            return a_users[j % 3] * i + j // 3 + 1


        def wait_emptied(eng, i, j):
            eng.wait_ge(a_emptied[j % 3], a_users[j % 3] * i + j // 3 + 2)

        def wait_bank(eng, i, j):
            eng.wait_ge(a_emptied[j % 3], a_users[j % 3] * i + j // 3 + 1)

        def wait_before(eng, i, j):
            eng.wait_ge(a_emptied[j % 3], a_users[j % 3] * i + 1)

        with nc.Block() as block:
            @block.gpsimd
            def _(pool):
                pool.sem_inc(x_ready, 2)
                pool.sem_inc(g_ready, 2)
                pool.sem_inc(base_step, 1)
                g = nc.gpsimd
                with pool.Fori(0, NQ // 2) as i:
                    for k in two:
                        u = 2 * i + k
                        pool.wait_ge(y_psum, free(u))
                        g.tensor_copy(xs[k][:, :], x2t[:, bass.ds(u * QF, QF)]).then_inc(x_ready, 1)
                        g.tensor_copy(g4[k][:, :, :], per_token(gw[:, bass.ds(u * QT * E, QT * E)], QT * E))\
                            .then_inc(g_ready, 1)
                    for k in two:
                        u = 2 * i + k
                        pool.wait_ge(y_done, free(u))
                        pool.wait_ge(base_step, 9 * u + 1)
                        g.tensor_tensor(features(base[k][:, :]), features(hid[:, bass.ds(u * 512, 512)]),
                                        row_of(w("r_sb3", HP), QT), ALU.add).then_inc(base_step, 1)
                        for e in range(E):
                            pool.wait_ge(base_step, 9 * u + 2 * e + 2)
                            g.tensor_tensor(features(tmp[:, :]), row_of(w("r_eb3", HP, e * D, e * D + D), QT),
                                            g4[k][:, e::E, :], ALU.mult).then_inc(base_step, 1)
                            pool.wait_ge(base_step, 9 * u + 2 * e + 3)
                            g.tensor_tensor(base[k][:, :], base[k][:, :], tmp[:, :], ALU.add)\
                                .then_inc(base_step, 1)

            @block.tensor
            def _(pe):
                pe.sem_inc(y_psum, 2)
                mm = nc.tensor.matmul

                def fill(i, job):
                    kind, k, pair, e, parity = job
                    j = a_jobs.index(job)
                    r = 64 * parity
                    wait_bank(pe, i, j)
                    o = A[j % 3][:, 0:QF]
                    if kind == "t":
                        pe.wait_ge(x_ready, ready(2 * i + k))
                        x = mm(o, w("sW1"), xs[k][:, :], start=True, stop=True)
                    elif kind == "s2":
                        wait_emptied(pe, i, a_index("t", k))
                        x = mm(o, w("sW2", 64, first=r), t1[r:r + 64, :], start=True, stop=True)
                    else:
                        c = (2 * pair + e) * 128
                        x = mm(o, w("eW1", 64, c, c + 128, first=r), xs[k][r:r + 64, :], start=True, stop=True)
                    x.then_inc(a_filled[j % 3], 1)

                with pe.Fori(0, NQ // 2) as i:
                    for job in plan:
                        k = job[1]
                        if job[0] in ("t", "s2", "w1"):
                            for a in a_jobs:
                                if a[0] == job[0] and a[1] == k and (job[0] != "w1" or a[2] == job[2]):
                                    fill(i, a)
                        elif job[0] == "z":
                            pair = job[2]
                            for p in two:
                                n = 8 * i + 4 * k + 2 * pair + p
                                pe.wait_ge(zr_done, ready(n - 2))
                                for e in two:
                                    wait_emptied(pe, i, a_index("w1", k, pair, e, p))
                                    c = (2 * pair + e) * 64
                                    x = mm(Z[p][64 * e:64 * e + 64, 0:QF], w("eW2", a=c, b=c + 64),
                                           h1[4 * pair + 2 * e + p][:, :], start=True, stop=True)
                                x.then_inc(z_psum, 1)
                                pe.wait_ge(g_ready, ready(2 * i + k))
                                pe.wait_ge(zg_done, ready(n - 2))
                                for q in two:
                                    for half in two:
                                        t = (half * 4 + q * 2 + p) * E + 2 * pair
                                        src = g4[k][:, t:t + 2, :].rearrange("p e f -> p (e f)")
                                        x = nc.tensor.transpose(G[p][:, q * LP + half * HP:q * LP + half * HP + HP],
                                                                src, w("ident", HP, 0, HP))
                                x.then_inc(g_psum, 1)
                        else:
                            u = 2 * i + k
                            pe.wait_ge(zg_done, 8 * i + 4 * k + 4 + 2)
                            for p in two:
                                wait_emptied(pe, i, a_index("s2", k, parity=p))
                            pe.wait_ge(y_done, ready(u - 1))
                            for half in two:
                                for q in two:
                                    for p in two:
                                        c = q * LP + half * HP
                                        o = (half * 4 + q * 2 + p) * D
                                        o = Y[0:HP, o:o + D]
                                        mm(o, s2[p][:, c:c + HP], w("sW3"), start=True, stop=False)
                                        mm(o, zg[p][:, c:c + HP], w("eW3", a=0, b=64), start=False, stop=False)
                                        x = mm(o, zg[2 + p][:, c:c + HP], w("eW3", a=64, b=128), start=False,
                                               stop=True)
                            x.then_inc(y_psum, 1)

            def empty(eng, i, job, is_act):
                kind, k, pair, e, parity = job
                j = a_jobs.index(job)
                if on_act[j] != is_act:
                    return
                u = 2 * i + k
                if kind == "t":
                    dst, bias = t1, w("b_s1")
                    for p in two:
                        if k:
                            wait_emptied(eng, i, a_index("s2", 0, parity=p))
                        else:
                            wait_before(eng, i, a_index("s2", 1, parity=p))
                elif kind == "s2":
                    dst, bias = s2[parity], w("b_s2")
                    eng.wait_ge(y_psum, u + 2)
                else:
                    dst, bias = h1[4 * pair + 2 * e + parity], w("b_e1", a=2 * pair + e, b=2 * pair + e + 1)
                    eng.wait_ge(z_psum, 8 * i + 4 * k + 2 * pair + parity + 1 - 4 + 4)
                eng.wait_ge(a_filled[j % 3], a_fill_value(i, j))
                src = A[j % 3][:, 0:QF]
                if is_act:
                    x = nc.scalar.activation(dst[:, :], src, ACT.Relu, bias=bias)
                else:
                    x = nc.vector.tensor_scalar(dst[:, :], src, bias, 0.0, ALU.add, ALU.max)
                x.then_inc(a_emptied[j % 3], 1)

            def jobs_of(job):
                return [a for a in a_jobs if a[0] == job[0] and a[1] == job[1] and (job[0] != "w1" or a[2] == job[2])]

            @block.scalar
            def _(act):
                act.sem_inc(zr_done, 2)
                for x in a_emptied:
                    act.sem_inc(x, 1)
                act.sem_inc(z_psum, 4)
                with act.Fori(0, NQ // 2) as i:
                    for job in plan:
                        if job[0] in ("t", "s2", "w1"):
                            for a in jobs_of(job):
                                empty(act, i, a, True)
                        elif job[0] == "z":
                            _, k, pair = job
                            for p in two:
                                n = 8 * i + 4 * k + 2 * pair + p
                                act.wait_ge(z_psum, n + 1 + 4)
                                act.wait_ge(zg_done, n - 2 + 1 + 2)
                                nc.scalar.activation(zr[p][:, :], Z[p][:, 0:QF], ACT.Relu,
                                                     bias=w("b_e2", a=pair, b=pair + 1)).then_inc(zr_done, 1)

            @block.vector
            def _(dve):
                dve.sem_inc(zg_done, 2)
                dve.sem_inc(y_done, 2)
                v = nc.vector
                with dve.Fori(0, NQ // 2) as i:
                    for job in plan:
                        if job[0] in ("t", "s2", "w1"):
                            for a in jobs_of(job):
                                empty(dve, i, a, False)
                        elif job[0] == "z":
                            _, k, pair = job
                            for p in two:
                                n = 8 * i + 4 * k + 2 * pair + p
                                dve.wait_ge(zr_done, n + 1 + 2)
                                dve.wait_ge(g_psum, n + 1)
                                dve.wait_ge(y_psum, 2 * i + k + 2)
                                v.tensor_tensor(zg[2 * pair + p][:, :], zr[p][:, :], G[p][:, 0:QF], ALU.mult)\
                                    .then_inc(zg_done, 1)
                        else:
                            k = job[1]
                            u = 2 * i + k
                            dve.wait_ge(y_psum, ready(u))
                            dve.wait_ge(base_step, 9 * u + 10)
                            dve.wait_ge(out_stored[k], 32 * i + 16)
                            v.tensor_tensor(y[k][:, :], base[k][:, :], Y[0:HP, :], ALU.add)\
                                .then_inc(y_done, 1)

            @block.sync
            def _(sp):
                for x in out_stored:
                    sp.sem_inc(x, 16)
                with sp.Fori(0, NQ // 2) as i:
                    for k in two:
                        u = 2 * i + k
                        sp.wait_ge(y_done, ready(u))
                        for half in two:
                            rows = HP if half == 0 else L - HP
                            sp.dma_start(out[bass.ds(4 * u, 4), half * HP:half * HP + rows, :]
                                         .rearrange("b p f -> p b f"),
                                         y[k][0:rows, half * 256:half * 256 + 256].rearrange("p (b f) -> p b f", f=D))\
                                .then_inc(out_stored[k], 16)
                for k in two:
                    sp.wait_ge(out_stored[k], 16 + 32 * (NQ // 2))



def cubic(t):
    a, at = -0.75, abs(t)
    if at <= 1.0:
        return ((a + 2.0) * at - (a + 3.0)) * at * at + 1.0
    return ((a * at - 5.0 * a) * at + 8.0 * a) * at - 4.0 * a if at < 2.0 else 0.0


def diag(m, copies=2):
    r, c = m.shape
    out = np.zeros((r * copies, c * copies), m.dtype)
    for k in range(copies):
        out[k * r:(k + 1) * r, k * c:(k + 1) * c] = m
    return out


def token_pack():
    pack = np.zeros((128, TOK_W), np.float32)

    def put(name, a):
        at, width = TOK_COLS[name]
        assert a.shape[1] == width
        pack[0:a.shape[0], at:at + width] = a

    interp = np.zeros((TAPS, WIN))
    for j in range(WIN):
        for tap in range(4):
            interp[j // UP + tap, j] = cubic((j % UP) / UP - (tap - 1))
    put("interp", diag(interp.astype(np.float32)))
    j, k = np.arange(WIN)[:, None], np.arange(WIN)[None, :]
    angle = 2 * np.pi * ((j * np.where(k < NBIN, k, k - NBIN + 1)) % WIN) / WIN
    put("dft", diag((0.5 * np.where(k < NBIN, np.cos(angle), -np.sin(angle))).astype(np.float32)))
    put("b_gauss", np.full((128, 1), -0.7, np.float32))
    put("b_poly", np.full((128, 1), 1.3, np.float32))
    return pack


def phase_columns(kinds, unit=1.0):
    rows = [(-1.0, -unit, PI / 2) if kind == "c" else (1.0, unit, 0.0) for kind in kinds for _ in range(P)]
    return np.array(rows, np.float32)


def main_constants(put):
    put("ident", np.eye(128, dtype=np.float32))
    m, l = np.arange(HP)[:, None], np.arange(HP)[None, :]
    tri = (m <= l).astype(np.float32)
    put("mask", np.concatenate([tri, np.ones((HP, HP), np.float32)], 1))
    inv = (1.0 / (np.arange(LP) + 1.0))[None, :]
    put("mean0", (np.concatenate([tri, np.ones((HP, HP))], 1) * inv).astype(np.float32))
    put("mean1", (tri * inv[:, HP:]).astype(np.float32))
    s = np.tile(np.eye(P, dtype=np.float32), (H, 1))
    z = np.zeros_like(s)
    put("select", np.concatenate([s, z, z, s, z, s, -s, z], 1))
    put("posA", phase_columns("cscs"))
    put("posB", phase_columns("ccss"))
    put("posP", phase_columns("cscs", PI_BELOW))
    put("half_pi", np.full((128, 1), PI / 2, np.float32))
    put("minus_half", np.full((128, 8), -0.5, np.float32))


def kernel(**inputs):
    import concourse.bacc as _bacc
    from concourse import mybir as _mybir
    from concourse.bass_utils import run_bass_kernel_spmd as _run

    a = {k.replace("L0_attn_", "").replace("L0_ffn_", ""): np.asarray(v) for k, v in inputs.items()}
    pack = np.zeros((128, MAIN_W), np.float32)

    def put(name, m, first=0):
        at, width = MAIN_COLS[name]
        assert m.shape[1] == width, (name, m.shape)
        pack[first:first + m.shape[0], at:at + width] = m

    def col(name, v, copies=1):
        put(name, np.tile(v.reshape(-1, 1), (copies, 1)))

    def row(name, v):
        put(name, np.tile(v.reshape(1, -1), (HP, 1)))

    def dup(m):
        return np.concatenate([m, m], 1)

    main_constants(put)
    pos = np.zeros((P, LP), np.float32)
    pos[:, :L] = a["pos_phases"][:L].T
    put("pos", np.tile(pos, (4, 1)))
    put("hop1p", dup(a["hop_w1"][D:]))
    put("kce_t", dup(a["kce_w"].T))
    col("kce_b", a["kce_b"])
    put("kskc", dup(a["ksk_w1"][D:]))
    put("hop1", diag(a["hop_w1"][:D]))
    put("ksk1", diag(a["ksk_w1"][:D]))
    put("sg1", diag(a["sg_w1"]))
    put("key1", diag(dup(a["cpe_w"])))
    put("mc", diag(a["mc_w"]))
    put("ve", diag(a["ve_w"]))
    hop2 = a["hop_w2"].reshape(D, H, P + 1)
    put("hopc", np.tile(hop2[:, :, :P].reshape(D, H * P), (2, 1)))
    put("hopw", diag(hop2[:, :, P]))
    put("ksk2", diag(dup(a["ksk_w2"])))
    put("sg2", diag(a["sg_w2"]))
    put("outw", diag(a["out_w"]))
    put("outw64", a["out_w"])
    put("lnb", np.tile(a["ln_b"].reshape(D, 1), (1, HP)))
    col("lng", a["ln_g"], 2)
    col("b_hop1", a["hop_b1"], 2)
    col("b_ksk1", a["ksk_b1"], 2)
    col("b_sg1", a["sg_b1"], 2)
    col("b_cpe", a["cpe_b"], 4)
    hopb = a["hop_b2"].reshape(H, P + 1)
    col("b_hopc", hopb[:, :P].reshape(-1))
    row("r_hopw", hopb[:, P])
    col("b_ksk2", a["ksk_b2"], 4)
    col("b_sg2", a["sg_b2"], HP)
    put("sW1", diag(a["sW1"]))
    put("sW2", np.tile(a["sW2"], (2, 1)))
    put("sW3", a["sW3"])
    put("eW1", np.tile(a["eW1"].transpose(1, 0, 2).reshape(D, -1), (2, 1)))
    put("eW2", a["eW2"].transpose(1, 0, 2).reshape(128, -1))
    put("eW3", a["eW3"].reshape(2, 128, D).transpose(1, 0, 2).reshape(128, -1))
    put("gW", diag(a["gW"]))
    col("b_s1", a["sb1"], 2)
    col("b_s2", a["sb2"])
    put("b_e1", a["eb1"].T)
    put("b_e2", a["eb2"].reshape(2, 128).T)
    row("r_mc", a["mc_b"])
    row("r_ve", a["ve_b"])
    row("r_out", a["out_b"])
    row("r_gb", a["gb"])
    row("r_eb3", a["eb3"])
    row("r_sb3", a["sb3"])
    row("r_delta", a["window_deltas"])

    at = np.clip(np.arange(TAPS)[:, None] - 1 + (WIN // UP) * np.arange(LP)[None, :], 0, NS - 1)
    windows = a["x"][:, at].reshape(NB // 2, 2, TAPS, LP).transpose(1, 2, 0, 3).reshape(2 * TAPS, -1)

    nc = _bacc.Bacc("TRN2", target_bir_lowering=False, num_devices=1)
    arrays, args = {}, []
    for name, arr in (("tok_pack", token_pack()), ("main_pack", pack), ("windows", windows)):
        arrays[name] = np.ascontiguousarray(arr)
        args.append(nc.dram_tensor(name, arr.shape, _mybir.dt.from_np(arr.dtype), kind="ExternalInput").ap())
    args.append(nc.dram_tensor("tower_out", (NB, L, D), _mybir.dt.float32, kind="ExternalOutput").ap())
    audio_tower(nc, *args)
    r = _run(nc, [arrays], core_ids=[0])
    return r.results[0]["tower_out"]
```

```python
from contextlib import ExitStack

import numpy as np

import concourse.bass as bass
from concourse import mybir

F32, F32R = mybir.dt.float32, mybir.dt.float32r
ALU = mybir.AluOpType
ACT = mybir.ActivationFunctionType
AX = mybir.AxisListType

NB, NS = 32, 4000
L, D, P, H, WN = 249, 64, 32, 4, 5
HP = 125
LP = 2 * HP
WIN, UP = 64, 4
NQ = NB // 4
QT = 4 * 2
QF = 2 * LP
NT = NB * 2
TAPS = WIN // UP + 3
NBIN = WIN // 2 + 1
E = 4
GONE = 32
G_STEPS = 18
ALPHA, BETA = 0.12, 0.9
PI = float(np.pi)
PI_BELOW = float(np.nextafter(np.float32(np.pi), np.float32(0)))
ROUND = 1.5 * 2.0 ** 23
TWO_PI = (6.28125, 2 * PI - 6.28125 - (2 * PI - 6.28125) % 2.0 ** -19, (2 * PI - 6.28125) % 2.0 ** -19)



def columns(widths):
    at, out = 0, {}
    for name, w in widths:
        out[name] = (at, w)
        at += w
    return out, at


TOK_COLS, TOK_W = columns([("interp", 128), ("dft", 128), ("b_gauss", 1), ("b_poly", 1)])
MAIN_COLS, MAIN_W = columns([
    ("ident", 128), ("mask", 2 * HP), ("mean0", LP), ("mean1", HP), ("select", 2 * 128),
    ("posA", 3), ("posB", 3), ("posP", 3), ("half_pi", 1), ("minus_half", 8),
    ("pos", LP), ("hop1p", 128), ("kce_t", 128), ("kce_b", 1), ("kskc", 128),
    ("hop1", 128), ("ksk1", 128), ("sg1", 64), ("key1", 128), ("mc", 128), ("ve", 128),
    ("hopc", 128), ("hopw", 8), ("ksk2", 128), ("sg2", 2), ("outw", 128), ("outw64", 64),
    ("lnb", HP), ("lng", 1),
    ("b_hop1", 1), ("b_ksk1", 1), ("b_sg1", 1), ("b_cpe", 1), ("b_hopc", 1), ("b_ksk2", 1), ("b_sg2", 1),
    ("sW1", 128), ("sW2", 128), ("sW3", 3 * D), ("eW1", E * 128), ("eW2", E * 64), ("eW3a", 3 * D), ("eW3b", 3 * D), ("gW", 8),
    ("b_s1", 1), ("b_s2", 1), ("b_e1", E), ("b_e2", 2),
    ("r_mc", D), ("r_ve", D), ("r_hopw", H), ("r_out", D), ("r_gb", E), 
    ("r_delta", WN), ("r_lower", E * E), ("r_higher", E * E), ("spread", 4 * 128), ("third_b", 128),
])


def ready(u, slots=2):
    return u + (1 + slots)


def free(u, slots=2):
    return u + 1


def bodies(eng, body):
    with eng.Fori(0, NQ // 2 - 1) as i:
        body(i, True)
    body(NQ // 2 - 1, False)


class Chain:

    def __init__(self, eng, sem, base=0, n=0):
        self.eng, self.sem, self.base, self.n = eng, sem, base, n

    def tick(self, ins):
        ins.then_inc(self.sem, 1)
        self.n += 1
        return ins

    def settle(self):
        self.eng.wait_ge(self.sem, self.base + self.n)


def audio_tower(nc, tok_pack, main_pack, windows, out):
    ctx = ExitStack()
    with ctx:
        def sb(name, shape, stack=ctx):
            return stack.enter_context(nc.sbuf_tensor(name, shape, F32))

        def bank(name, stack):
            return stack.enter_context(nc.psum_tensor(name, [128, 512], F32))

        def sem(name):
            return ctx.enter_context(nc.semaphore(name))

        main = sb("main", [128, MAIN_W])
        table = sb("table", [128, 1])
        hid = sb("hid", [HP, NT * D])

        def w(name, rows=128, a=0, b=None, first=0):
            at, width = MAIN_COLS[name]
            return main[first:first + rows, at + a:at + (width if b is None else b)]

        main_loaded = sem("main_loaded")

        with ExitStack() as st:
            s, setup_work = setup(nc, sb, bank, sem, w, main_loaded, st)
            tokens(nc, sb, bank, sem, tok_pack, main_pack, windows, main, main_loaded, hid, table, setup_work)
        cont = sb("cont", [HP, NT * D])
        with ExitStack() as st:
            cen = sb("cen", [128, NQ * 2 * QF], st)
            key, sto = sb("key", [128, NQ * QF], st), sb("sto", [128, NQ * QF], st)
            val = sb("val", [HP, NT * D], st)
            wid, gat, root = sb("wid", [HP, NT * H], st), sb("gat", [HP, NT], st), sb("root", [HP, NT], st)
            mix = sb("mix", [HP, 2, NT * H], st)
            attention_inputs(nc, sb, bank, sem, w, s, table, hid, cen, key, sto, cont, val, wid, gat)
            window_weights(nc, sb, bank, sem, w, s, wid, gat, mix, root)
            attend(nc, sb, bank, sem, w, s, cen, key, sto, cont, val, mix, root)
        project_and_experts(nc, sb, bank, sem, w, s, hid, cont, out)


def tokens(nc, sb, bank, sem, tok_pack, main_pack, windows, main, main_loaded, hid, table, setup_work):
    with ExitStack() as st:
        tok = sb("tok", [128, TOK_W], st)
        win = sb("win", [2 * TAPS, NQ * QF], st)
        power = sb("power", [HP, NT * NBIN], st)
        sq = [sb(f"sq{s}", [128, QF], st) for s in range(2)]
        poly = [sb(f"poly{s}", [128, QF], st) for s in range(2)]
        gauss = [sb(f"gauss{s}", [128, QF], st) for s in range(2)]
        kw = [sb(f"kw{s}", [128, QF], st) for s in range(2)]
        parts2 = [sb(f"parts2_{s}", [HP, 512], st) for s in range(2)]
        CW = NT * NBIN // 2
        CT = NT // 2
        mag = sb("mag", [HP, 2 * CW], st)
        d = sb("d", [HP, 2 * CW], st)
        e = sb("e", [HP, 2 * CW], st)
        mx = sb("mx", [HP, NT], st)
        psI = [bank(f"psI{s}", st) for s in range(2)]
        psD = [bank(f"psD{s}", st) for s in range(2)]

        tok_loaded, win_loaded = sem("tok_loaded"), sem("win_loaded")
        interp_ready, poly_ready, square_ready, gauss_ready = (
            sem("interp_ready"), sem("poly_ready"), sem("square_ready"), sem("gauss_ready"))
        kw_ready, dft_ready, parts_ready, power_ready = (
            sem("kw_ready"), sem("dft_ready"), sem("parts_ready"), sem("power_ready"))
        mag_ready, over_ready, mask_ready, gap_ready, gap_abs, exp_ready, log_ready = (
            sem("mag_ready"), sem("over_ready"), sem("mask_ready"), sem("gap_ready"), sem("gap_abs"), sem("exp_ready"),
            sem("log_ready"))
        vec_step = sem("tok_vec_step")

        def t(name, rows=128):
            at, width = TOK_COLS[name]
            return tok[0:rows, at:at + width]

        with nc.Block() as block:
            @block.sync
            def _(sp):
                sp.dma_start(tok[:, :], tok_pack[:, :]).then_inc(tok_loaded, 16)
                for c in range(4):
                    a, b = c * 2 * QF, (c + 1) * 2 * QF
                    sp.dma_start(win[:, a:b], windows[:, a:b]).then_inc(win_loaded, 16)
                    sp.wait_ge(win_loaded, 16 * (c + 1))
                sp.dma_start(main[:, :], main_pack[:, :]).then_inc(main_loaded, 16)

            @block.tensor
            def _(pe):
                pe.sem_inc(interp_ready, 2)
                pe.sem_inc(dft_ready, 2)
                pe.wait_ge(tok_loaded, 16)

                def interpolate(i):
                    pe.wait_ge(win_loaded, 16 * i + 16)
                    for s in range(2):
                        pe.wait_ge(poly_ready, free(2 * i + s))
                        nc.tensor.matmul(psI[s][:, 0:QF], t("interp", 2 * TAPS),
                                         win[:, bass.ds((2 * i + s) * QF, QF)], start=True, stop=True)\
                            .then_inc(interp_ready, 1)

                def body(i, more):
                    if more:
                        interpolate(i + 1)
                    for s in range(2):
                        pe.wait_ge(kw_ready, ready(2 * i + s))
                        pe.wait_ge(parts_ready, free(2 * i + s))
                        for half in range(2):
                            for pair in range(2):
                                c = pair * LP + half * HP
                                o = (half * 2 + pair) * 128
                                mm = nc.tensor.matmul(psD[s][0:HP, o:o + 128], kw[s][:, c:c + HP], t("dft"),
                                                      start=True, stop=True)
                        mm.then_inc(dft_ready, 1)

                interpolate(0)
                bodies(pe, body)
                setup_work["tensor"](pe)

            @block.scalar
            def _(act):
                for x in (poly_ready, square_ready, gauss_ready, parts_ready):
                    act.sem_inc(x, 2)
                act.wait_ge(tok_loaded, 16)
                nc.scalar.activation(table[0:1, :], t("b_poly", 1), ACT.Exp)

                def kernels(i):
                    for s in range(2):
                        act.wait_ge(interp_ready, ready(2 * i + s))
                        nc.scalar.activation(sq[s][:, :], psI[s][:, 0:QF], ACT.Square, bias=t("b_gauss"))\
                            .then_inc(square_ready, 1)
                        act.wait_ge(kw_ready, free(2 * i + s))
                        nc.scalar.activation(poly[s][:, :], psI[s][:, 0:QF], ACT.Square, bias=t("b_poly"))\
                            .then_inc(poly_ready, 1)
                        act.wait_ge(square_ready, ready(2 * i + s))
                        nc.scalar.activation(gauss[s][:, :], sq[s][:, :], ACT.Exp, scale=-0.5)\
                            .then_inc(gauss_ready, 1)

                def body(i, more):
                    if more:
                        kernels(i + 1)
                    for s in range(2):
                        act.wait_ge(dft_ready, ready(2 * i + s))
                        act.wait_ge(power_ready, free(2 * i + s))
                        nc.scalar.activation(parts2[s][:, :], psD[s][0:HP, :], ACT.Square)\
                            .then_inc(parts_ready, 1)

                kernels(0)
                bodies(act, body)
                act.wait_ge(power_ready, ready(NQ - 1))
                for c in range(2):
                    a, b = c * CW, (c + 1) * CW
                    nc.scalar.activation(mag[:, a:b], power[:, a:b], ACT.Sqrt).then_inc(mag_ready, 1)
                for c in range(2):
                    a, b = c * CW, (c + 1) * CW
                    act.wait_ge(over_ready, c + 1)
                    nc.scalar.activation(e[:, a:b], d[:, a:b], ACT.Tanh, scale=0.5).then_inc(mask_ready, 1)
                for c in range(2):
                    a, b = c * CW, (c + 1) * CW
                    act.wait_ge(gap_ready, c + 1)
                    nc.scalar.activation(power[:, a:b], d[:, a:b], ACT.Abs).then_inc(gap_abs, 1)
                    act.wait_ge(gap_abs, c + 1)
                    nc.scalar.activation(e[:, a:b], power[:, a:b], ACT.Exp, scale=-0.5).then_inc(exp_ready, 1)
                for c in range(2):
                    a, b = c * CW, (c + 1) * CW
                    act.wait_ge(exp_ready, c + 1)
                    nc.scalar.activation(power[:, a:b], e[:, a:b], ACT.Ln, bias=1.0).then_inc(log_ready, 1)
                setup_work["scalar"](act)

            @block.vector
            def _(dve):
                dve.sem_inc(kw_ready, 2)
                dve.sem_inc(power_ready, 2)

                def mix_kernels(i):
                    for s in range(2):
                        dve.wait_ge(gauss_ready, ready(2 * i + s))
                        dve.wait_ge(poly_ready, ready(2 * i + s))
                        dve.wait_ge(dft_ready, free(2 * i + s))
                        nc.vector.tensor_tensor(kw[s][:, :], poly[s][:, :], gauss[s][:, :], ALU.add)\
                            .then_inc(kw_ready, 1)

                def body(i, more):
                    if more:
                        mix_kernels(i + 1)
                    for s in range(2):
                        dve.wait_ge(parts_ready, ready(2 * i + s))
                        v = parts2[s][:, :].rearrange("p (t f) -> p t f", f=WIN)
                        o = power[:, bass.ds((2 * i + s) * (QT * NBIN), QT * NBIN)]\
                            .rearrange("p (t f) -> p t f", f=NBIN)
                        nc.vector.tensor_copy(o[:, :, 0:NBIN:NBIN - 1], v[:, :, 0:NBIN:NBIN - 1])
                        nc.vector.tensor_tensor(o[:, :, 1:NBIN - 1], v[:, :, 1:NBIN - 1], v[:, :, NBIN:WIN],
                                                ALU.add).then_inc(power_ready, 1)

                mix_kernels(0)
                bodies(dve, body)
                setup_work["vector"](dve)
                ch = Chain(dve, vec_step)

                def view(x, c):
                    return x[:, c * CW:(c + 1) * CW].rearrange("p (t f) -> p t f", f=NBIN)

                def top(c):
                    return mx[:, c * CT:(c + 1) * CT].rearrange("p (t a) -> p t a", a=1)\
                        .broadcast_to([HP, CT, NBIN])

                for c in range(2):
                    dve.wait_ge(mag_ready, c + 1)
                    ch.tick(nc.vector.tensor_reduce(mx[:, c * CT:(c + 1) * CT], view(mag, c), AX.X, ALU.max))
                    ch.settle()
                    nc.vector.scalar_tensor_tensor(out=view(d, c), in0=top(c), scalar=-ALPHA, in1=view(mag, c),
                                                   op0=ALU.mult, op1=ALU.add).then_inc(over_ready, 1)
                for c in range(2):
                    a, b = c * CW, (c + 1) * CW
                    dve.wait_ge(mask_ready, c + 1)
                    ch.tick(nc.vector.scalar_tensor_tensor(out=mag[:, a:b], in0=e[:, a:b], scalar=1.0,
                                                           in1=mag[:, a:b], op0=ALU.add, op1=ALU.mult))
                    ch.settle()
                    nc.vector.scalar_tensor_tensor(out=view(d, c), in0=top(c), scalar=-2 * BETA,
                                                   in1=view(mag, c), op0=ALU.mult, op1=ALU.add)\
                        .then_inc(gap_ready, 1)
                    dve.wait_ge(gap_ready, c + 1)
                    ch.tick(nc.vector.scalar_tensor_tensor(out=view(mag, c), in0=top(c), scalar=2 * BETA,
                                                           in1=view(mag, c), op0=ALU.mult, op1=ALU.min))
                for c in range(2):
                    a, b = c * CW, (c + 1) * CW
                    dve.wait_ge(log_ready, c + 1)
                    h = hid[:, c * CT * D:(c + 1) * CT * D].rearrange("p (t f) -> p t f", f=D)
                    m, lg = view(mag, c), view(power, c)
                    ch.settle()
                    ch.tick(nc.vector.scalar_tensor_tensor(out=h[:, :, 0:NBIN], in0=m, scalar=0.5, in1=lg,
                                                           op0=ALU.mult, op1=ALU.subtract))
                    ch.settle()
                    ch.tick(nc.vector.tensor_copy(h[:, :, NBIN:D], h[:, :, NBIN - 2:0:-1]))
                ch.settle()


def setup(nc, sb, bank, sem, w, main_loaded, loc):
    s = {}
    s["kskc"] = sb("kskc_bd", [128, 128])
    s["b_ksk"] = sb("b_ksk", [128, 1])
    s["outw"] = sb("outw_scaled", [128, 128])
    s["r_out"] = sb("r_outb", [HP, D])
    s["hop_pos"] = sb("hop_pos", [128, LP])
    s["tabA"] = sb("tabA", [128, LP])
    s["tabB"] = sb("tabB", [128, LP])
    s["cosd"] = sb("cosd", [HP, WN])
    s["sind"] = sb("sind", [HP, WN])
    s["decay"] = sb("decay", [HP, WN])
    s["b_sg2"] = sb("b_sg2_half", [HP, 1])
    ps0, ps1 = bank("ps_setup0", loc), bank("ps_setup1", loc)
    turns, rest, shape = (sb(n, [128, LP + WN], loc) for n in ("turns", "rest", "shape"))
    shapeB = sb("shapeB", [128, LP], loc)
    setup_products, trig_args, trig_done = sem("setup_products"), sem("trig_args"), sem("trig_done")
    step, act_step = sem("setup_step"), sem("setup_act_step")
    def tensor(pe):
        pe.wait_ge(main_loaded, 16)
        nc.tensor.matmul(ps0[:, 0:64], w("kce_t", 64), w("kskc", 64, 0, 64), start=True, stop=True)
        nc.tensor.matmul(ps0[:, 64:65], w("kskc", 64), w("kce_b", 64), start=True, stop=True)
        nc.tensor.matmul(ps0[0:HP, 128:192], w("lnb", 64), w("outw64", 64), start=True, stop=True)
        nc.tensor.matmul(ps1[:, 0:LP], w("hop1p", 32), w("pos", 32), start=True, stop=True)\
            .then_inc(setup_products, 1)

    def vector(dve):
        ch = Chain(dve, step)
        dve.wait_ge(main_loaded, 16)
        ch.tick(nc.vector.memset(s["kskc"][:, :], 0.0))
        ch.tick(nc.vector.tensor_scalar(s["outw"][:, :], w("outw"), w("lng"), None, ALU.mult))
        ch.tick(nc.vector.tensor_scalar(s["b_sg2"][:, :], w("b_sg2", HP), 0.5, None, ALU.mult))
        ch.tick(nc.vector.tensor_tensor(s["decay"][:, :], w("r_delta", HP), w("r_delta", HP), ALU.mult))
        ch.tick(nc.vector.tensor_copy(rest[:, 0:LP], w("pos")))
        ch.tick(nc.vector.memset(rest[:, LP:LP + WN], 0.0))
        ch.settle()
        ch.tick(nc.vector.tensor_scalar(rest[0:HP, LP:LP + WN], w("r_delta", HP), 0.1, None, ALU.mult))
        ch.tick(nc.vector.tensor_scalar(s["decay"][:, :], s["decay"][:, :], -0.5, None, ALU.mult))
        ch.settle()
        ch.tick(nc.vector.tensor_scalar(turns[:, :], rest[:, :], 1 / (2 * PI), ROUND, ALU.mult, ALU.add))
        ch.settle()
        ch.tick(nc.vector.tensor_scalar(turns[:, :], turns[:, :], -ROUND, None, ALU.add))
        for part in TWO_PI:
            ch.settle()
            ch.tick(nc.vector.scalar_tensor_tensor(out=rest[:, :], in0=turns[:, :], scalar=-part,
                                                   in1=rest[:, :], op0=ALU.mult, op1=ALU.add))
        ch.settle()
        ch.tick(nc.vector.tensor_scalar(rest[:, :], rest[:, :], PI_BELOW, -PI_BELOW, ALU.min, ALU.max))
        ch.settle()
        nc.vector.scalar_tensor_tensor(out=shape[:, 0:LP], in0=rest[:, 0:LP], scalar=w("posA", b=1),
                                       in1=rest[:, 0:LP], op0=ALU.mult, op1=ALU.max).then_inc(trig_args, 1)
        nc.vector.scalar_tensor_tensor(out=shapeB[:, :], in0=rest[:, 0:LP], scalar=w("posB", b=1),
                                       in1=rest[:, 0:LP], op0=ALU.mult, op1=ALU.max).then_inc(trig_args, 1)
        nc.vector.scalar_tensor_tensor(out=shape[0:HP, LP:], in0=rest[0:HP, LP:], scalar=-1.0,
                                       in1=rest[0:HP, LP:], op0=ALU.mult, op1=ALU.max)\
            .then_inc(trig_args, 1)
        dve.wait_ge(setup_products, 1)
        for r in (0, 64):
            ch.tick(nc.vector.tensor_copy(s["kskc"][r:r + 64, r:r + 64], ps0[r:r + 64, 0:64]))
        ch.tick(nc.vector.tensor_tensor(s["b_ksk"][:, :], ps0[:, 64:65], w("b_ksk1"), ALU.add))
        ch.tick(nc.vector.tensor_tensor(s["r_out"][:, :], ps0[0:HP, 128:192], w("r_out", HP), ALU.add))

    def scalar(act):
        act.wait_ge(trig_args, 3)
        nc.scalar.activation(s["tabA"][:, :], shape[:, 0:LP], ACT.Sin, bias=w("posA", a=2, b=3),
                             scale=w("posA", a=1, b=2))
        nc.scalar.activation(s["tabB"][:, :], shapeB[:, :], ACT.Sin, bias=w("posB", a=2, b=3),
                             scale=w("posB", a=1, b=2))
        nc.scalar.activation(s["cosd"][:, :], shape[0:HP, LP:], ACT.Sin, bias=w("half_pi", HP),
                             scale=-1.0)
        nc.scalar.activation(s["sind"][:, :], rest[0:HP, LP:], ACT.Sin)
        act.wait_ge(setup_products, 1)
        nc.scalar.activation(s["hop_pos"][:, :], ps1[:, 0:LP], ACT.Identity, bias=w("b_hop1"))
    return s, {"tensor": tensor, "vector": vector, "scalar": scalar}


def per_token(stat, n, f=D):
    return stat.rearrange("p (t a) -> p t a", a=1).broadcast_to([stat.shape[0], n, f])


def features(x, f=D):
    return x.rearrange("p (t f) -> p t f", f=f)


def row_of(x, n):
    return x.rearrange("p (a f) -> p a f", a=1).broadcast_to([x.shape[0], n, x.shape[1]])


def attention_inputs(nc, sb, bank, sem, w, s, table, hid, cen, key, sto, cont, val, wid, gat):
    with ExitStack() as st:
        two = range(2)
        mu, var, rstd, tg = ([sb(f"{n}{k}", [HP, QT], st) for k in two] for n in ("mu", "var", "rstd", "tg"))
        xc, xn, vraw = ([sb(f"{n}{k}", [HP, 512], st) for k in two] for n in ("xc", "xn", "vraw"))
        sqx = [sb(f"sqx{k}", [HP, 512], st) for k in two]
        xb = sb("xb", [HP, 512], st)
        xt, cm, hopin, hh, kh = ([sb(f"{n}{k}", [128, QF], st) for k in two] for n in ("xt", "cm", "hopin", "hh", "kh"))
        sh = [sb(f"sh{k}", [64, QF], st) for k in two]
        B = [[bank(f"in{k}_{j}", st) for j in range(4)] for k in two]
        (xc_ready, sqx_ready, var_ready, rstd_ready, xn_ready, hx_done, xt_psum, xt_done, cm_psum, cm_done,
         hop_psum, hopin_done, hh_done, sg_psum, sg_done, ksk_psum, ksk_done, key_psum, key_done, cont_psum,
         cont_done, val_psum, val_done, gv_done, cen0_psum, cen0_done, cen1_psum, cen1_done, st_psum, st_done,
         small_psum, width_done, tg_done, gat_ready) = (sem("in_" + n) for n in (
             "xc_ready sqx_ready var_ready rstd_ready xn_ready hx_done xt_psum xt_done cm_psum cm_done "
             "hop_psum hopin_done hh_done sg_psum sg_done ksk_psum ksk_done key_psum key_done cont_psum "
             "cont_done val_psum val_done gv_done cen0_psum cen0_done cen1_psum cen1_done st_psum st_done "
             "small_psum width_done tg_done gat_ready").split())
        vec_step, xb_ready = sem("in_vec_step"), sem("in_xb_ready")
        STEPS = 6

        def tile(x, half, pair, n=HP):
            c = pair * LP + half * HP
            return x[:, c:c + n]

        with nc.Block() as block:
            @block.tensor
            def _(pe):
                for x in (xt_psum, cm_psum, hop_psum, sg_psum, ksk_psum, key_psum, cont_psum, val_psum,
                          cen0_psum, cen1_psum, st_psum, small_psum):
                    pe.sem_inc(x, 2)
                mm = nc.tensor.matmul
                def turn_and_mean(i):
                    for k in two:
                        u = 2 * i + k
                        b0, b1 = B[k][0], B[k][1]
                        pe.wait_ge(xn_ready, ready(u))
                        pe.wait_ge(cen1_done, free(u))
                        for half in two:
                            for pair in two:
                                o = (half * 2 + pair) * 128
                                x = nc.tensor.transpose(tile(b0, half, pair), xn[k][:, o:o + 128],
                                                        w("ident", HP, 0, HP))
                        x.then_inc(xt_psum, 1)
                        pe.wait_ge(cen0_done, free(u))
                        for pair in two:
                            mm(tile(b1, 0, pair, LP), xn[k][:, pair * 128:pair * 128 + 128], w("mean0", HP),
                               start=True, stop=False)
                            x = mm(tile(b1, 1, pair), xn[k][:, 256 + pair * 128:256 + pair * 128 + 128],
                                   w("mean1", HP), start=False, stop=True)
                        x.then_inc(cm_psum, 1)
                def body(i, more):
                    for k in two:
                        u = 2 * i + k
                        b2, b3 = B[k][2], B[k][3]
                        pe.wait_ge(xt_done, ready(u))
                        pe.wait_ge(st_done, free(u))
                        mm(b2[:, 0:QF], w("hop1"), xt[k][:, :], start=True, stop=True).then_inc(hop_psum, 1)
                        pe.wait_ge(tg_done, free(u))
                        mm(b3[0:64, 0:QF], w("sg1"), xt[k][:, :], start=True, stop=True).then_inc(sg_psum, 1)
                    for k in two:
                        u = 2 * i + k
                        b0, b1 = B[k][0], B[k][1]
                        pe.wait_ge(cm_done, ready(u))
                        mm(b1[:, 0:QF], w("ksk1"), xt[k][:, :], start=True, stop=False)
                        mm(b1[:, 0:QF], s["kskc"][:, :], cm[k][:, :], start=False, stop=True)\
                            .then_inc(ksk_psum, 1)
                        mm(b0[:, 0:QF], w("key1"), xt[k][:, :], start=True, stop=True).then_inc(key_psum, 1)
                    for k in two:
                        u = 2 * i + k
                        for b, name, read, signal in ((B[k][2], "mc", hopin_done, cont_psum),
                                                      (B[k][3], "ve", sg_done, val_psum)):
                            pe.wait_ge(read, ready(u))
                            for half in two:
                                for pair in two:
                                    o = (half * 2 + pair) * 128
                                    x = mm(b[0:HP, o:o + 128], tile(xt[k], half, pair), w(name),
                                           start=True, stop=True)
                            x.then_inc(signal, 1)
                    for k in two:
                        u = 2 * i + k
                        b0, b1 = B[k][0], B[k][1]
                        pe.wait_ge(ksk_done, ready(u))
                        pe.wait_ge(hh_done, ready(u))
                        mm(b1[:, 0:QF], w("hopc", 64), hh[k][0:64, :], start=True, stop=True)\
                            .then_inc(cen0_psum, 1)
                        pe.wait_ge(key_done, ready(u))
                        mm(b0[:, 0:QF], w("hopc", 64, first=64), hh[k][64:128, :], start=True, stop=True)\
                            .then_inc(cen1_psum, 1)
                    for k in two:
                        u = 2 * i + k
                        b2, b3 = B[k][2], B[k][3]
                        pe.wait_ge(cont_done, ready(u))
                        mm(b2[:, 0:QF], w("ksk2"), kh[k][:, :], start=True, stop=True).then_inc(st_psum, 1)
                        pe.wait_ge(val_done, ready(u))
                        for half in two:
                            for pair in two:
                                o = half * 2 + pair
                                mm(b3[0:HP, o * 8:o * 8 + 8], tile(hh[k], half, pair), w("hopw"),
                                   start=True, stop=True)
                                x = mm(b3[0:HP, 32 + o * 2:34 + o * 2], tile(sh[k], half, pair), w("sg2", 64),
                                       start=True, stop=True)
                        x.then_inc(small_psum, 1)
                    if more:
                        turn_and_mean(i + 1)

                turn_and_mean(0)
                bodies(pe, body)

            @block.scalar
            def _(act):
                for x in (sqx_ready, xt_done, sg_done, hh_done, ksk_done, key_done, cen0_done, cen1_done,
                          st_done, tg_done):
                    act.sem_inc(x, 2)
                f = nc.scalar.activation
                def squares(i):
                    for k in two:
                        u = 2 * i + k
                        act.wait_ge(xc_ready, ready(u))
                        act.wait_ge(var_ready, free(u))
                        f(sqx[k][:, :], xc[k][:, :], ACT.Square).then_inc(sqx_ready, 1)

                def body(i, more):
                    for k in two:
                        u = 2 * i + k
                        act.wait_ge(xt_psum, ready(u))
                        act.wait_ge(val_psum, free(u))
                        f(xt[k][:, :], B[k][0][:, 0:QF], ACT.Copy).then_inc(xt_done, 1)
                    for k in two:
                        u = 2 * i + k
                        act.wait_ge(small_psum, free(u))
                        act.wait_ge(sg_psum, ready(u))
                        f(sh[k][:, :], B[k][3][0:64, 0:QF], ACT.Gelu, bias=w("b_sg1", 64)).then_inc(sg_done, 1)
                        act.wait_ge(hopin_done, ready(u))
                        f(hh[k][:, :], hopin[k][:, :], ACT.Gelu).then_inc(hh_done, 1)
                    if more:
                        squares(i + 1)
                    for k in two:
                        u = 2 * i + k
                        act.wait_ge(ksk_psum, ready(u))
                        act.wait_ge(st_psum, free(u))
                        f(kh[k][:, :], B[k][1][:, 0:QF], ACT.Gelu, bias=s["b_ksk"][:, :]).then_inc(ksk_done, 1)
                        act.wait_ge(key_psum, ready(u))
                        f(key[:, bass.ds(u * QF, QF)], B[k][0][:, 0:QF], ACT.Tanh, bias=w("b_cpe"))\
                            .then_inc(key_done, 1)
                    for k in two:
                        u = 2 * i + k
                        for parity, b, need, signal in ((0, 1, cen0_psum, cen0_done), (1, 0, cen1_psum, cen1_done)):
                            act.wait_ge(need, ready(u))
                            f(cen[:, bass.ds(u * (2 * QF) + parity * QF, QF)], B[k][b][:, 0:QF], ACT.Tanh,
                              bias=w("b_hopc")).then_inc(signal, 1)
                    for k in two:
                        u = 2 * i + k
                        act.wait_ge(st_psum, ready(u))
                        f(sto[:, bass.ds(u * QF, QF)], B[k][2][:, 0:QF], ACT.Tanh, bias=w("b_ksk2"))\
                            .then_inc(st_done, 1)
                        act.wait_ge(small_psum, ready(u))
                        act.wait_ge(width_done, ready(u))
                        act.wait_ge(gat_ready, free(u))
                        f(tg[k][:, :], B[k][3][0:HP, 32:40], ACT.Tanh, bias=s["b_sg2"][:, :], scale=0.5)\
                            .then_inc(tg_done, 1)

                f(table[0:HP, :], s["b_sg2"][:, :], ACT.Gelu)
                squares(0)
                bodies(act, body)

            @block.vector
            def _(dve):
                for x in (xc_ready, var_ready, xn_ready, cm_done, hopin_done, cont_done, val_done, width_done,
                          gat_ready):
                    dve.sem_inc(x, 2)
                v = nc.vector
                def centre(i):
                    ch = Chain(dve, vec_step, STEPS * i)
                    for k in two:
                        u = 2 * i + k
                        x = features(hid[:, bass.ds(u * 512, 512)])
                        ch.tick(v.tensor_reduce(mu[k][:, :], x, AX.X, ALU.add))
                        ch.settle()
                        ch.tick(v.tensor_scalar(mu[k][:, :], mu[k][:, :], -1.0 / D, None, ALU.mult))
                        ch.settle()
                        v.tensor_tensor(features(xc[k][:, :]), x, per_token(mu[k][:, :], QT), ALU.add)\
                            .then_inc(xc_ready, 1)

                def variance(i):
                    ch = Chain(dve, vec_step, STEPS * i, 4)
                    for k in two:
                        u = 2 * i + k
                        dve.wait_ge(sqx_ready, ready(u))
                        dve.wait_ge(rstd_ready, free(u))
                        ch.tick(v.tensor_reduce(var[k][:, :], features(sqx[k][:, :]), AX.X, ALU.add))
                        ch.settle()
                        v.tensor_scalar(var[k][:, :], var[k][:, :], 1.0 / D, 1e-5, ALU.mult, ALU.add)\
                            .then_inc(var_ready, 1)

                def scale(i):
                    for k in two:
                        u = 2 * i + k
                        dve.wait_ge(rstd_ready, ready(u))
                        dve.wait_ge(cm_psum, free(u))
                        dve.wait_ge(hx_done, free(u))
                        v.tensor_tensor(features(xn[k][:, :]), features(xc[k][:, :]), per_token(rstd[k][:, :], QT),
                                        ALU.mult).then_inc(xn_ready, 1)

                def body(i, more):
                    for k in two:
                        u = 2 * i + k
                        dve.wait_ge(cm_psum, ready(u))
                        dve.wait_ge(ksk_psum, free(u))
                        v.tensor_copy(cm[k][:, :], B[k][1][:, 0:QF]).then_inc(cm_done, 1)
                    for k in two:
                        u = 2 * i + k
                        dve.wait_ge(hop_psum, ready(u))
                        dve.wait_ge(hh_done, free(u))
                        v.tensor_tensor(features(hopin[k][:, :], LP), features(B[k][2][:, 0:QF], LP),
                                        row_of(s["hop_pos"][:, :], 2), ALU.add).then_inc(hopin_done, 1)
                    if more:
                        centre(i + 1)
                    for k in two:
                        u = 2 * i + k
                        dve.wait_ge(cont_psum, ready(u))
                        v.tensor_tensor(features(cont[:, bass.ds(u * 512, 512)]), features(B[k][2][0:HP, :]),
                                        row_of(w("r_mc", HP), QT), ALU.add).then_inc(cont_done, 1)
                        dve.wait_ge(val_psum, ready(u))
                        dve.wait_ge(gv_done, free(u))
                        v.tensor_tensor(features(vraw[k][:, :]), features(B[k][3][0:HP, :]),
                                        row_of(w("r_ve", HP), QT), ALU.add).then_inc(val_done, 1)
                        if more and k == 0:
                            variance(i + 1)
                    if more:
                        scale(i + 1)
                    for k in two:
                        u = 2 * i + k
                        dve.wait_ge(small_psum, ready(u))
                        v.tensor_tensor(features(wid[:, bass.ds(u * 32, 32)], H), features(B[k][3][0:HP, 0:32], H),
                                        row_of(w("r_hopw", HP), QT), ALU.add).then_inc(width_done, 1)
                        dve.wait_ge(tg_done, ready(u))
                        v.tensor_scalar(gat[:, bass.ds(u * QT, QT)], tg[k][:, :], 0.5, 0.5, ALU.mult, ALU.add)\
                            .then_inc(gat_ready, 1)

                centre(0)
                variance(0)
                scale(0)
                bodies(dve, body)

            @block.gpsimd
            def _(pool):
                for x in (rstd_ready, hx_done, gv_done):
                    pool.sem_inc(x, 2)
                g = nc.gpsimd
                def roots(i):
                    for k in two:
                        u = 2 * i + k
                        pool.wait_ge(var_ready, ready(u))
                        pool.wait_ge(xn_ready, free(u))
                        g.tensor_tensor(rstd[k][:, :], var[k][:, :], w("minus_half", HP), ALU.pow)\
                            .then_inc(rstd_ready, 1)

                def body(i, more):
                    for k in two:
                        u = 2 * i + k
                        pool.wait_ge(xn_ready, ready(u))
                        pool.wait_ge(hx_done, free(u + 1))
                        g.tensor_tensor(features(xb[:, :]), features(xn[k][:, :]), row_of(s["r_out"][:, :], QT),
                                        ALU.add).then_inc(xb_ready, 1)
                        pool.wait_ge(xb_ready, u + 1)
                        h = hid[:, bass.ds(u * 512, 512)]
                        g.tensor_tensor(h, h, xb[:, :], ALU.add).then_inc(hx_done, 1)
                    if more:
                        roots(i + 1)
                    for k in two:
                        u = 2 * i + k
                        pool.wait_ge(val_done, ready(u))
                        pool.wait_ge(gat_ready, ready(u))
                        g.tensor_tensor(features(val[:, bass.ds(u * 512, 512)]), features(vraw[k][:, :]),
                                        per_token(gat[:, bass.ds(u * QT, QT)], QT), ALU.mult)\
                            .then_inc(gv_done, 1)

                roots(0)
                bodies(pool, body)


def window_weights(nc, sb, bank, sem, w, s, wid, gat, mix, root):
    with ExitStack() as st:
        n = NT * H
        ew, recip, both, total = (sb(a, [HP, b], st) for a, b in (
            ("ew", WN * n), ("recip", n), ("both", n), ("total", n)))
        cum, half = sb("cum", [HP, NT], st), sb("cum_half", [HP, NT], st)
        ps = bank("ps_cum", st)
        width_ready, recip_ready, ew_ready, cum_psum, cum_ready, step = (sem("ww_" + x) for x in (
            "width_ready", "recip_ready", "ew_ready", "cum_psum", "cum_ready", "step"))
        g = gat[:, :].rearrange("p (q h b) -> p q h b", h=2, b=4)

        with nc.Block() as block:
            @block.tensor
            def _(pe):
                m = w("mask", HP)
                nc.tensor.matmul(ps[0:HP, 0:32], m[:, 0:HP], g[:, :, 0, :], start=True, stop=True)
                nc.tensor.matmul(ps[0:HP, 32:64], m[:, HP:2 * HP], g[:, :, 0, :], start=True, stop=False)
                nc.tensor.matmul(ps[0:HP, 32:64], m[:, 0:HP], g[:, :, 1, :], start=False, stop=True)\
                    .then_inc(cum_psum, 1)

            @block.scalar
            def _(act):
                nc.scalar.activation(both[:, :], wid[:, :], ACT.Tanh, scale=0.5).then_inc(width_ready, 1)
                act.wait_ge(recip_ready, 1)
                for d in range(WN):
                    nc.scalar.activation(ew[:, d * n:(d + 1) * n], recip[:, :], ACT.Exp,
                                         scale=s["decay"][:, d:d + 1]).then_inc(ew_ready, 1)

            @block.vector
            def _(dve):
                v = nc.vector
                ch = Chain(dve, step)
                dve.wait_ge(width_ready, 1)
                ch.tick(v.tensor_scalar(both[:, :], both[:, :], 1.1, None, ALU.add))
                ch.settle()
                ch.tick(v.tensor_tensor(both[:, :], both[:, :], both[:, :], ALU.mult))
                ch.settle()
                ch.tick(v.tensor_scalar(both[:, :], both[:, :], 1e-6, None, ALU.add))
                ch.settle()
                v.reciprocal(recip[:, :], both[:, :]).then_inc(recip_ready, 1)
                dve.wait_ge(cum_psum, 1)
                v.tensor_scalar(cum[:, :].rearrange("p (q h b) -> p h q b", h=2, b=4),
                                ps[0:HP, 0:64].rearrange("p (h q b) -> p h q b", h=2, b=4), 1.0, None, ALU.max)\
                    .then_inc(cum_ready, 1)
                for d in range(WN):
                    e = ew[:, d * n:(d + 1) * n]
                    dve.wait_ge(ew_ready, d + 1)
                    ch.settle()
                    if d == 0:
                        ch.tick(v.tensor_scalar(total[:, :], e, 1e-6, None, ALU.add))
                        ch.tick(v.tensor_scalar(mix[:, 0, :], e, s["cosd"][:, d:d + 1], None, ALU.mult))
                        ch.tick(v.tensor_scalar(mix[:, 1, :], e, s["sind"][:, d:d + 1], None, ALU.mult))
                        continue
                    ch.tick(v.tensor_tensor(total[:, :], total[:, :], e, ALU.add))
                    for a, tab in ((0, "cosd"), (1, "sind")):
                        ch.tick(v.scalar_tensor_tensor(out=mix[:, a, :], in0=e, scalar=s[tab][:, d:d + 1],
                                                       in1=mix[:, a, :], op0=ALU.mult, op1=ALU.add))
                ch.settle()
                ch.tick(v.reciprocal(total[:, :], total[:, :]))
                ch.settle()
                for a in range(2):
                    ch.tick(v.scalar_tensor_tensor(out=mix[:, a, :], in0=mix[:, a, :],
                                                   scalar=1.0 / (H * P ** 0.5), in1=total[:, :],
                                                   op0=ALU.mult, op1=ALU.mult))

            @block.gpsimd
            def _(pool):
                nc.gpsimd.memset(half[:, :], -0.5).then_inc(cum_ready, 1)
                pool.wait_ge(cum_ready, 2)
                nc.gpsimd.tensor_tensor(cum[:, :], cum[:, :], half[:, :], ALU.pow).then_inc(cum_ready, 1)
                pool.wait_ge(cum_ready, 3)
                nc.gpsimd.tensor_scalar(root[:, :], cum[:, :], P ** -0.5, None, ALU.mult)


def done(n, back=0):
    return n + (9 - back)


def attend(nc, sb, bank, sem, w, s, cen, key, sto, cont, val, mix, root):
    with ExitStack() as st:
        two = range(2)
        kk, qq = ([sb(f"{n}{k}", [128, QF], st) for k in two] for n in ("kk", "qq"))
        mag = sb("cen_abs", [128, 2 * QF], st)
        cs = [sb(f"cs{k}", [128, 4, 2, LP], st) for k in two]
        ab = [sb(f"ab{k}", [HP, 2, QT * H, P], st) for k in two]
        ua, vb = (sb(n, [128, 2, LP], st) for n in ("ua", "vb"))
        turned = [sb(f"turned{k}", [128, 2, LP], st) for k in two]
        qd = [sb(f"qd{k}", [128, LP], st) for k in two]
        sm = [sb(f"sm{k}", [HP, 6 * HP], st) for k in two]
        part = sb("part", [HP, 512], st)
        psAB, psO, psD, psF, psP1, psP2 = (bank(f"at_{n}", st) for n in ("ab", "o", "d", "f", "p1", "p2"))
        ku_ready, ks_ready, abs_done, cs_ready, ab_ready, comb_ready, part_ready = (sem("at_" + n) for n in (
            "ku_ready", "ks_ready", "abs_done", "cs_ready", "ab_ready", "comb_ready", "part_ready"))
        ab_psum, uv_ready, y_ready, o_psum, qd_ready, s_psum, smd_ready, smf_ready, pv_psum = (
            sem("at_" + n) for n in ("ab_psum", "uv_ready", "y_ready", "o_psum", "qd_ready", "s_psum",
                                     "smd_ready", "smf_ready", "pv_psum"))
        BODY = 8
        DIAG, OFF = ((0, HP), (2 * HP, 3 * HP)), (4 * HP, 5 * HP)

        def where(n):
            return n // 4 % 2, n % 4 // 2, n % 2

        with nc.Block() as block:
            @block.gpsimd
            def _(pool):
                pool.sem_inc(ab_ready, 2)
                with pool.Fori(0, NQ // 2) as i:
                    for k in two:
                        pool.wait_ge(ab_psum, done(BODY * i + 4 * k + 3, BODY))
                        for a in two:
                            m = mix[:, a, bass.ds((2 * i + k) * (QT * H), QT * H)]
                            x = nc.gpsimd.tensor_copy(ab[k][:, a, :, :], per_token(m, QT * H, P))
                        x.then_inc(ab_ready, 1)

            @block.scalar
            def _(act):
                for x in (ks_ready, cs_ready):
                    act.sem_inc(x, 2)
                act.sem_inc(smf_ready, BODY)
                f = nc.scalar.activation

                def centres(u, k):
                    c = cen[:, bass.ds(u * (2 * QF), 2 * QF)]
                    act.wait_ge(cs_ready, ready(u - 1))
                    act.wait_ge(uv_ready, done(4 * u + 3, BODY))
                    f(mag[:, :], c, ACT.Abs).then_inc(abs_done, 1)
                    f(cs[k][:, :, 1, :], features(c, LP), ACT.Sin, scale=PI_BELOW)
                    act.wait_ge(abs_done, u + 1)
                    f(cs[k][:, :, 0, :], features(mag[:, :], LP), ACT.Sin, bias=w("half_pi"),
                      scale=-PI_BELOW).then_inc(cs_ready, 1)

                def keys(u, k):
                    act.wait_ge(ku_ready, ready(u))
                    for x in (kk[k], qq[k]):
                        y = f(x[:, :], x[:, :], ACT.Sin, bias=w("posP", a=2, b=3), scale=w("posP", a=1, b=2))
                    y.then_inc(ks_ready, 1)

                def copy_off(g, n):
                    act.wait_ge(s_psum, done(g))
                    act.wait_ge(pv_psum, done(g, 2))
                    f(sm[n % 2][:, 4 * HP:6 * HP], psF[0:HP, 0:2 * HP], ACT.Copy).then_inc(smf_ready, 1)

                def body(i, last):
                    for n in range(BODY):
                        g = BODY * i + n
                        if n % 4 == 0 and not (last and n // 4 + 1 > 1):
                            centres(2 * i + n // 4 + 1, (n // 4 + 1) % 2)
                        if n % 4 == 1 and not (last and n // 4 + 1 > 1):
                            keys(2 * i + n // 4 + 1, (n // 4 + 1) % 2)
                        if not (last and n + 1 >= BODY):
                            copy_off(g + 1, n + 1)

                centres(0, 0)
                keys(0, 0)
                copy_off(0, 0)
                with act.Fori(0, NQ // 2 - 1) as i:
                    body(i, False)
                body(NQ // 2 - 1, True)

            @block.tensor
            def _(pe):
                for x in (ab_psum, o_psum, s_psum, pv_psum):
                    pe.sem_inc(x, BODY)
                mm = nc.tensor.matmul

                def spread(i, n):
                    k, parity, pair = where(n)
                    pe.wait_ge(ab_ready, ready(2 * i + n // 4))
                    pe.wait_ge(uv_ready, done(BODY * i + n, 1))
                    for a in two:
                        for half in two:
                            t = (half * 4 + pair * 2 + parity) * H
                            src = ab[k][:, a, t:t + H, :].rearrange("p h f -> p (h f)")
                            x = nc.tensor.transpose(psAB[:, a * LP + half * HP:a * LP + half * HP + HP], src,
                                                    w("ident", HP, 0, HP))
                    x.then_inc(ab_psum, 1)

                def query(i, n):
                    g = BODY * i + n
                    pe.wait_ge(y_ready, done(g))
                    pe.wait_ge(qd_ready, done(g, 1))
                    mm(psO[:, 0:LP], w("select", b=128), turned[n % 2][:, 0, :], start=True, stop=False)
                    mm(psO[:, 0:LP], w("select", a=128), turned[n % 2][:, 1, :], start=False, stop=True)\
                        .then_inc(o_psum, 1)

                def scores(i, n):
                    k, parity, pair = where(n)
                    g = BODY * i + n
                    r, c = 64 * parity, pair * LP
                    pe.wait_ge(ks_ready, ready(2 * i + n // 4))
                    pe.wait_ge(qd_ready, done(g))
                    pe.wait_ge(smd_ready, done(g, 1))
                    pe.wait_ge(smf_ready, done(g, 1))
                    for j, (keys, q) in enumerate(((s["tabA"], qd[n % 2]),
                                                   (kk[k][r:r + 64, c:c + LP], qq[k][r:r + 64, c:c + LP]))):
                        for m, l in ((0, 0), (0, 1), (1, 1)):
                            b, o = (psD, DIAG[j][m]) if m == l else (psF, j * HP)
                            x = mm(b[0:HP, o:o + HP], keys[:, m * HP:m * HP + HP], q[:, l * HP:l * HP + HP],
                                   start=True, stop=True)
                    x.then_inc(s_psum, 1)

                def weigh(i, n):
                    k, parity, pair = where(n)
                    b = pair * 2 + parity
                    g = BODY * i + n
                    pe.wait_ge(smd_ready, done(g))
                    pe.wait_ge(smf_ready, done(g))
                    if n % 4 == 0:
                        pe.wait_ge(comb_ready, ready(2 * i + n // 4 - 1))
                    sc = sm[n % 2]
                    for j, (ps, rows) in enumerate(((psP1, cont), (psP2, val))):
                        first = rows[:, bass.ds((2 * i + k) * 512 + b * D, D)]
                        second = rows[:, bass.ds((2 * i + k) * 512 + (4 + b) * D, D)]
                        mm(ps[0:HP, b * D:b * D + D], sc[:, DIAG[j][0]:DIAG[j][0] + HP], first,
                           start=True, stop=True)
                        o = ps[0:HP, (4 + b) * D:(5 + b) * D]
                        mm(o, sc[:, OFF[j]:OFF[j] + HP], first, start=True, stop=False)
                        x = mm(o, sc[:, DIAG[j][1]:DIAG[j][1] + HP], second, start=False, stop=True)
                    x.then_inc(pv_psum, 1)

                def body(i, last):
                    for n in range(BODY):
                        for stage, ahead in ((spread, 3), (query, 2), (scores, 1), (weigh, 0)):
                            if not (last and n + ahead >= BODY):
                                stage(i, n + ahead)

                for stage, n in ((spread, 0), (spread, 1), (query, 0), (spread, 2), (query, 1), (scores, 0)):
                    stage(0, n)
                with pe.Fori(0, NQ // 2 - 1) as i:
                    body(i, False)
                body(NQ // 2 - 1, True)

            @block.vector
            def _(dve):
                for x in (uv_ready, y_ready, qd_ready, smd_ready):
                    dve.sem_inc(x, BODY)
                for x in (ku_ready, comb_ready):
                    dve.sem_inc(x, 2)
                v = nc.vector

                def keys(u, k):
                    dve.wait_ge(s_psum, done(4 * u + 3, BODY))
                    for x, src in ((kk[k], sto), (qq[k], key)):
                        p = src[:, bass.ds(u * QF, QF)]
                        y = v.scalar_tensor_tensor(out=x[:, :], in0=p, scalar=w("posP", b=1), in1=p,
                                                   op0=ALU.mult, op1=ALU.max)
                    y.then_inc(ku_ready, 1)

                def turn(i, n):
                    k, parity, pair = where(n)
                    g = BODY * i + n
                    dve.wait_ge(ab_psum, done(g))
                    dve.wait_ge(cs_ready, ready(2 * i + n // 4))
                    dve.wait_ge(y_ready, done(g, 1))
                    dve.wait_ge(o_psum, done(g, 2))
                    c = cs[k][:, parity * 2 + pair, :, :]
                    v.tensor_tensor(ua[:, :, :], c, row_of(psAB[:, 0:LP], 2), ALU.mult)
                    v.tensor_tensor(vb[:, :, :], c[:, 1::-1, :], row_of(psAB[:, LP:2 * LP], 2), ALU.mult)\
                        .then_inc(uv_ready, 1)
                    dve.wait_ge(uv_ready, done(g))
                    y = turned[n % 2]
                    v.tensor_tensor(y[:, 0, :], ua[:, 0, :], vb[:, 0, :], ALU.subtract)
                    v.tensor_tensor(y[:, 1, :], ua[:, 1, :], vb[:, 1, :], ALU.add).then_inc(y_ready, 1)

                def place(i, n):
                    g = BODY * i + n
                    dve.wait_ge(o_psum, done(g))
                    dve.wait_ge(s_psum, done(g, 2))
                    v.tensor_tensor(qd[n % 2][:, :], psO[:, 0:LP], s["tabB"][:, :], ALU.mult)\
                        .then_inc(qd_ready, 1)

                def mask(i, n):
                    g = BODY * i + n
                    dve.wait_ge(s_psum, done(g))
                    dve.wait_ge(pv_psum, done(g, 2))
                    v.tensor_tensor(features(sm[n % 2][:, 0:4 * HP], HP), features(psD[0:HP, 0:4 * HP], HP),
                                    row_of(w("mask", HP, 0, HP), 4), ALU.mult).then_inc(smd_ready, 1)

                def combine(u):
                    dve.wait_ge(pv_psum, done(4 * u + 3))
                    dve.wait_ge(comb_ready, ready(u - 1))
                    v.tensor_tensor(features(part[:, :]), features(psP2[0:HP, :]),
                                    per_token(root[:, bass.ds(u * QT, QT)], QT), ALU.mult).then_inc(part_ready, 1)
                    dve.wait_ge(part_ready, u + 1)
                    c = cont[:, bass.ds(u * 512, 512)]
                    v.tensor_tensor(c, part[:, :], psP1[0:HP, :], ALU.add).then_inc(comb_ready, 1)

                def body(i, last):
                    for n in range(BODY):
                        if n % 4 == 1 and not (last and n // 4 + 1 > 1):
                            keys(2 * i + n // 4 + 1, (n // 4 + 1) % 2)
                        for stage, ahead in ((turn, 3), (place, 2), (mask, 1)):
                            if not (last and n + ahead >= BODY):
                                stage(i, n + ahead)
                        if n % 4 == 3:
                            combine(2 * i + n // 4)

                keys(0, 0)
                for stage, n in ((turn, 0), (turn, 1), (place, 0), (turn, 2), (place, 1), (mask, 0)):
                    stage(0, n)
                with dve.Fori(0, NQ // 2 - 1) as i:
                    body(i, False)
                body(NQ // 2 - 1, True)


class Norm:

    def __init__(self, name, sb, sem, st):
        self.mu, self.var, self.rstd = ([sb(f"{name}_{n}{k}", [HP, QT], st) for k in range(2)]
                                        for n in ("mu", "var", "rstd"))
        self.xc, self.sq, self.xn = ([sb(f"{name}_{n}{k}", [HP, 512], st) for k in range(2)]
                                     for n in ("xc", "sq", "xn"))
        self.mu_ready, self.xc_ready, self.sq_ready, self.sum_ready, self.var_ready, self.rstd_ready, \
            self.xn_ready = (sem(f"{name}_{n}") for n in (
                "mu_ready", "xc_ready", "sq_ready", "sum_ready", "var_ready", "rstd_ready", "xn_ready"))


def project_and_experts(nc, sb, bank, sem, w, s, hid, comb, out):
    with ExitStack() as st:
        two = range(2)
        N1, N2 = Norm("n1", sb, sem, st), Norm("n2", sb, sem, st)
        ct, xs, s2, zr = ([sb(f"{n}{k}", [128, QF], st) for k in two] for n in ("ct", "xs", "s2_", "zr"))
        new, y = ([sb(f"{n}{k}", [HP, 512], st) for k in two] for n in ("new", "y"))
        t1 = sb("t1", [128, QF], st)
        h1 = [sb(f"h1_{j}", [128, QF], st) for j in range(8)]
        zg = [sb(f"zg{j}", [128, QF], st) for j in range(4)]
        lg = [sb(f"lg{k}", [HP, QT * E], st) for k in two]
        ex, gates, gw, gsplit = (sb(n, [HP, QT * E * m], st) for n, m in (("ex", 1), ("gates", 1), ("gw", 1),
                                                                         ("gsplit", 2)))
        top, tot, rank = sb("top", [HP, QT], st), sb("tot", [HP, QT], st), sb("rank", [HP, QT * E], st)
        ge, gt = (sb(n, [HP, QT * E * E], st) for n in ("ge", "gt"))
        gT = [sb(f"gT{k}", [GONE + 1, QF], st) for k in two]
        spread = sb("spread", [GONE + 1, 4 * 128], st)
        A = [bank(f"A{j}", st) for j in range(3)]
        Z, G, Y = bank("Z", st), bank("G", st), bank("Y", st)
        B = [bank(f"B{k}", st) for k in two]

        def first_layer(k, pair, e, p):
            return ("w1", k, pair, e, p)

        def section(k):
            m = 1 - k
            return [("out", m), ("t", k, 0, 0, 0), ("new", m), first_layer(k, 0, 0, 0), first_layer(k, 0, 0, 1),
                    ("square2", m), ("gates3", k), ("split_gates", k), first_layer(k, 0, 1, 0), ("var2", m),
                    first_layer(k, 0, 1, 1), ("s2", k, 0, 0, 0), ("scale2", m), ("s2", k, 0, 0, 1),
                    ("turn_gates", k), ("gT", k), first_layer(k, 1, 0, 0), ("z", k, 0, 0), ("centre1", k),
                    first_layer(k, 1, 0, 1), ("turn2", m), ("xs", m), ("z", k, 0, 1), ("var1", k),
                    first_layer(k, 1, 1, 0), first_layer(k, 1, 1, 1), ("z", k, 1, 0), ("scale1", k), ("logits", m),
                    ("lg", m), ("gates1", m), ("exp1", m), ("z", k, 1, 1), ("turn1", k), ("ct", k), ("gates2", m),
                    ("exp2", m), ("y", k)]

        plan = section(0) + section(1)
        after_next = ("centre1", "var1", "scale1", "turn1", "ct")
        next_one = ("out", "new", "square2", "var2", "scale2", "turn2", "xs", "logits", "lg", "gates1", "exp1",
                    "gates2", "exp2")
        start = [("centre1", 0), ("centre1", 1), ("var1", 0), ("scale1", 0), ("turn1", 0), ("ct", 0), ("var1", 1),
                 ("out", 0), ("scale1", 1), ("new", 0), ("turn1", 1), ("square2", 0), ("ct", 1), ("var2", 0),
                 ("scale2", 0), ("turn2", 0), ("xs", 0), ("logits", 0), ("lg", 0), ("gates1", 0), ("exp1", 0),
                 ("gates2", 0), ("exp2", 0)]

        def quad_of(i, at):
            name = plan[at][0]
            return 2 * i + at // (len(plan) // 2) + (2 if name in after_next else 1 if name in next_one else 0)

        def steps(eng):
            def walk(each):
                for entry in start:
                    each(entry[0], entry[1], None, entry)
                with eng.Fori(0, NQ // 2 - 1) as i:
                    for at, entry in enumerate(plan):
                        each(entry[0], quad_of(i, at), i, entry)
                i = NQ // 2 - 1
                for at, entry in enumerate(plan):
                    if quad_of(i, at) < NQ:
                        each(entry[0], quad_of(i, at), i, entry)
            return walk

        a_jobs = [entry for entry in plan if entry[0] in ("t", "s2", "w1")]
        NA = len(a_jobs)
        a_users = [len(range(b, NA, 3)) for b in range(3)]
        on_act = [j % 2 == 0 for j in range(NA)]
        a_filled = [sem(f"a_filled{b}") for b in range(3)]
        a_emptied = [sem(f"a_emptied{b}") for b in range(3)]
        (ct_psum, ct_done, out_psum, new_done, xs_psum, xs_done, lg_psum, lg_done, g_step, g_exp, gates_done,
         gt_psum, gt_done, z_psum, zr_done, g_psum, zg_done, y_psum, y_done, set_up) = (
            sem("tl_" + n) for n in (
                "ct_psum", "ct_done", "out_psum", "new_done", "xs_psum", "xs_done", "lg_psum", "lg_done", "g_step",
                "g_exp", "gates_done", "gt_psum", "gt_done", "z_psum", "zr_done", "g_psum", "zg_done",
                "y_psum", "y_done", "set_up"))
        out_stored = [sem(f"out_stored{k}") for k in two]

        def a_index(kind, slot, pair=0, e=0, parity=0):
            return a_jobs.index((kind, slot, pair, e, parity))


        def wait_emptied(eng, i, j):
            eng.wait_ge(a_emptied[j % 3], a_users[j % 3] * i + j // 3 + 2)

        def wait_bank(eng, i, j):
            eng.wait_ge(a_emptied[j % 3], a_users[j % 3] * i + j // 3 + 1)

        def wait_before(eng, i, j):
            eng.wait_ge(a_emptied[j % 3], a_users[j % 3] * i + 1)


        def centre(dve, N, k, u, x):
            v = nc.vector
            v.tensor_reduce(N.mu[k][:, :], x, AX.X, ALU.add).then_inc(N.mu_ready, 1)
            dve.wait_ge(N.mu_ready, 2 * u + 1)
            v.tensor_scalar(N.mu[k][:, :], N.mu[k][:, :], -1.0 / D, None, ALU.mult).then_inc(N.mu_ready, 1)
            dve.wait_ge(N.mu_ready, 2 * u + 2)
            v.tensor_tensor(features(N.xc[k][:, :]), x, per_token(N.mu[k][:, :], QT), ALU.add)\
                .then_inc(N.xc_ready, 1)

        def variance(dve, N, k, u):
            v = nc.vector
            dve.wait_ge(N.sq_ready, ready(u))
            dve.wait_ge(N.rstd_ready, free(u))
            v.tensor_reduce(N.var[k][:, :], features(N.sq[k][:, :]), AX.X, ALU.add).then_inc(N.sum_ready, 1)
            dve.wait_ge(N.sum_ready, u + 1)
            v.tensor_scalar(N.var[k][:, :], N.var[k][:, :], 1.0 / D, 1e-5, ALU.mult, ALU.add)\
                .then_inc(N.var_ready, 1)

        def scale(dve, N, k, u, read):
            dve.wait_ge(N.rstd_ready, ready(u))
            dve.wait_ge(read, free(u))
            nc.vector.tensor_tensor(features(N.xn[k][:, :]), features(N.xc[k][:, :]),
                                    per_token(N.rstd[k][:, :], QT), ALU.mult).then_inc(N.xn_ready, 1)

        def square(act, N, k, u):
            act.wait_ge(N.xc_ready, ready(u))
            act.wait_ge(N.var_ready, free(u))
            nc.scalar.activation(N.sq[k][:, :], N.xc[k][:, :], ACT.Square).then_inc(N.sq_ready, 1)

        def root(pool, N, k, u):
            pool.wait_ge(N.var_ready, ready(u))
            pool.wait_ge(N.xn_ready, free(u))
            nc.gpsimd.tensor_tensor(N.rstd[k][:, :], N.var[k][:, :], w("minus_half", HP), ALU.pow)\
                .then_inc(N.rstd_ready, 1)

        def turn(dst, src):
            for half in two:
                for pair in two:
                    o, c = (half * 2 + pair) * 128, pair * LP + half * HP
                    x = nc.tensor.transpose(dst[:, c:c + HP], src[:, o:o + 128], w("ident", HP, 0, HP))
            return x

        def empty(eng, i, job, is_act):
            kind, k, pair, e, parity = job
            j = a_jobs.index(job)
            if on_act[j] != is_act:
                return
            u = 2 * i + k
            if kind == "t":
                dst, bias = t1, w("b_s1")
                for p in two:
                    if k:
                        wait_emptied(eng, i, a_index("s2", 0, parity=p))
                    else:
                        wait_before(eng, i, a_index("s2", 1, parity=p))
            elif kind == "s2":
                dst, bias = s2[parity], w("b_s2")
                eng.wait_ge(y_psum, ready(u - 1))
            else:
                dst, bias = h1[4 * pair + 2 * e + parity], w("b_e1", a=2 * pair + e, b=2 * pair + e + 1)
                eng.wait_ge(z_psum, 4 * u + 2 * pair + parity + 1)
            eng.wait_ge(a_filled[j % 3], a_users[j % 3] * i + j // 3 + 1)
            src = A[j % 3][:, 0:QF]
            if is_act:
                x = nc.scalar.activation(dst[:, :], src, ACT.Relu, bias=bias)
            else:
                x = nc.vector.tensor_scalar(dst[:, :], src, bias, 0.0, ALU.add, ALU.max)
            x.then_inc(a_emptied[j % 3], 1)

        parts = gsplit[:, :].rearrange("p (t h c) -> p t h c", h=2, c=2 * E)

        with nc.Block() as block:
            @block.gpsimd
            def _(pool):
                for x in (N1.rstd_ready, N2.rstd_ready, gates_done):
                    pool.sem_inc(x, 2)
                whole = features(gw[:, :], 2 * E)
                g = nc.gpsimd

                def each(name, u, i, entry):
                    k = entry[1]
                    if name == "var1":
                        root(pool, N1, k, u)
                    elif name == "var2":
                        root(pool, N2, k, u)
                    elif name == "split_gates":
                        pool.wait_ge(g_step, G_STEPS * (u + 1))
                        pool.wait_ge(gt_psum, free(u, 1))
                        g.tensor_tensor(parts[:, :, 1, :], whole, parts[:, :, 0, :], ALU.subtract)\
                            .then_inc(gates_done, 1)

                steps(pool)(each)

            @block.tensor
            def _(pe):
                for x in (ct_psum, out_psum, xs_psum, lg_psum, y_psum):
                    pe.sem_inc(x, 2)
                pe.sem_inc(gt_psum, 1)
                mm = nc.tensor.matmul

                def fill(i, job):
                    kind, k, pair, e, parity = job
                    j = a_jobs.index(job)
                    r = 64 * parity
                    wait_bank(pe, i, j)
                    o = A[j % 3][:, 0:QF]
                    if kind == "t":
                        pe.wait_ge(xs_done, ready(2 * i + k))
                        x = mm(o, w("sW1"), xs[k][:, :], start=True, stop=True)
                    elif kind == "s2":
                        wait_emptied(pe, i, a_index("t", k))
                        x = mm(o, w("sW2", 64, first=r), t1[r:r + 64, :], start=True, stop=True)
                    else:
                        c = (2 * pair + e) * 128
                        x = mm(o, w("eW1", 64, c, c + 128, first=r), xs[k][r:r + 64, :], start=True, stop=True)
                    x.then_inc(a_filled[j % 3], 1)

                def each(name, u, i, entry):
                    k = entry[1]
                    tiles = [(half, pair, half * 2 + pair, pair * LP + half * HP) for half in two for pair in two]
                    if name == "turn1":
                        pe.wait_ge(N1.xn_ready, ready(u))
                        pe.wait_ge(gt_done, free(u))
                        turn(B[k], N1.xn[k]).then_inc(ct_psum, 1)
                    elif name == "out":
                        pe.wait_ge(ct_done, ready(u))
                        for half, pair, t, c in tiles:
                            x = mm(B[k][0:HP, t * 128:t * 128 + 128], ct[k][:, c:c + HP], s["outw"][:, :],
                                   start=True, stop=True)
                        x.then_inc(out_psum, 1)
                    elif name == "turn2":
                        pe.wait_ge(N2.xn_ready, ready(u))
                        turn(B[k], N2.xn[k]).then_inc(xs_psum, 1)
                    elif name == "logits":
                        pe.wait_ge(xs_done, ready(u))
                        for half, pair, t, c in tiles:
                            x = mm(B[k][0:HP, t * 8:t * 8 + 8], xs[k][:, c:c + HP], w("gW"), start=True, stop=True)
                        x.then_inc(lg_psum, 1)
                    elif name == "turn_gates":
                        pe.wait_ge(gates_done, ready(u))
                        for half, pair, t, c in tiles:
                            x = nc.tensor.transpose(B[k][0:4 * E, c:c + HP], gsplit[:, t * 4 * E:(t + 1) * 4 * E],
                                                    w("ident", HP, 0, HP))
                        x.then_inc(gt_psum, 1)
                    elif name in ("t", "s2", "w1"):
                        fill(i, entry)
                    elif name == "z":
                        _, _, pair, p = entry
                        n = 4 * u + 2 * pair + p
                        pe.wait_ge(zr_done, ready(n - 1))
                        for e in two:
                            wait_emptied(pe, i, a_index("w1", k, pair, e, p))
                            c = (2 * pair + e) * 64
                            x = mm(Z[64 * e:64 * e + 64, 0:QF], w("eW2", a=c, b=c + 64),
                                   h1[4 * pair + 2 * e + p][:, :], start=True, stop=True)
                        x.then_inc(z_psum, 1)
                        pe.wait_ge(gt_done, ready(u))
                        pe.wait_ge(zg_done, ready(n - 1))
                        c = (2 * pair + p) * 128
                        mm(G[:, 0:QF], spread[:, c:c + 128].bitcast(F32R), gT[k][:, :].bitcast(F32R),
                           start=True, stop=True).then_inc(g_psum, 1)
                    elif name == "y":
                        pe.wait_ge(zg_done, ready(4 * u + 3))
                        for p in two:
                            wait_emptied(pe, i, a_index("s2", k, parity=p))
                        pe.wait_ge(y_done, ready(u - 1))
                        for half, q, t, c in tiles:
                            o = Y[0:HP, t * 128:t * 128 + 128]
                            mm(o, gT[k][:, c:c + HP], w("third_b", GONE + 1),
                               start=True, stop=False)
                            for p in two:
                                for j, (name, x) in enumerate((("sW3", s2[p]), ("eW3a", zg[p]), ("eW3b", zg[2 + p]))):
                                    first = D * (1 - p)
                                    x = mm(o, x[:, c:c + HP], w(name, a=first, b=first + 128), start=False,
                                           stop=p == 1 and j == 2)
                        x.then_inc(y_psum, 1)

                steps(pe)(each)

            @block.scalar
            def _(act):
                for x in a_emptied:
                    act.sem_inc(x, 1)
                for x in (N1.sq_ready, N2.sq_ready, ct_done, xs_done, zr_done, gt_done):
                    act.sem_inc(x, 2)
                act.sem_inc(z_psum, 4)

                def each(name, u, i, entry):
                    k = entry[1]
                    if name == "centre1":
                        square(act, N1, k, u)
                    elif name == "ct":
                        act.wait_ge(ct_psum, ready(u))
                        act.wait_ge(out_psum, free(u))
                        nc.scalar.activation(ct[k][:, :], B[k][:, 0:QF], ACT.Copy).then_inc(ct_done, 1)
                    elif name == "square2":
                        square(act, N2, k, u)
                    elif name == "xs":
                        act.wait_ge(xs_psum, ready(u))
                        act.wait_ge(y_psum, free(u))
                        nc.scalar.activation(xs[k][:, :], B[k][:, 0:QF], ACT.Copy).then_inc(xs_done, 1)
                    elif name in ("exp1", "exp2"):
                        act.wait_ge(g_step, G_STEPS * u + (2 if name == "exp1" else 13))
                        nc.scalar.activation(ex[:, :], ex[:, :], ACT.Exp).then_inc(g_exp, 1)
                    elif name == "gT":
                        act.wait_ge(gt_psum, ready(u, 1))
                        act.wait_ge(y_psum, free(u))
                        nc.scalar.activation(gT[k][0:4 * E, :].bitcast(F32R), B[k][0:4 * E, 0:QF], ACT.Copy)\
                            .then_inc(gt_done, 1)
                    elif name in ("t", "s2", "w1"):
                        empty(act, i, entry, True)
                    elif name == "z":
                        _, _, pair, p = entry
                        n = 4 * u + 2 * pair + p
                        act.wait_ge(z_psum, n + 1 + 4)
                        act.wait_ge(zg_done, free(n))
                        nc.scalar.activation(zr[p][:, :], Z[:, 0:QF], ACT.Relu,
                                             bias=w("b_e2", a=pair, b=pair + 1)).then_inc(zr_done, 1)

                act.wait_ge(set_up, 3)
                steps(act)(each)

            @block.vector
            def _(dve):
                for N in (N1, N2):
                    for x in (N.xc_ready, N.var_ready, N.xn_ready):
                        dve.sem_inc(x, 2)
                for x in (new_done, lg_done, zg_done, y_done):
                    dve.sem_inc(x, 2)
                v = nc.vector
                ones = w("mask", GONE + 1, HP, 2 * HP).rearrange("p (a c) -> p a c", a=1)\
                    .broadcast_to([GONE + 1, 4, HP])
                for x in gT:
                    v.tensor_copy(features(x[:, :], HP).bitcast(F32R), ones).then_inc(set_up, 1)
                v.tensor_copy(spread[:, :].bitcast(F32R), w("spread", GONE + 1)).then_inc(set_up, 1)

                def softmax_of(ch, src):
                    ch.tick(v.tensor_reduce(top[:, :], features(src[:, :], E), AX.X, ALU.max))
                    ch.settle()
                    ch.tick(v.tensor_tensor(features(ex[:, :], E), features(src[:, :], E),
                                            per_token(top[:, :], QT, E), ALU.subtract))

                def normalise(ch, dst):
                    ch.tick(v.tensor_reduce(tot[:, :], features(ex[:, :], E), AX.X, ALU.add))
                    ch.settle()
                    ch.tick(v.reciprocal(tot[:, :], tot[:, :]))
                    ch.settle()
                    ch.tick(v.tensor_tensor(features(dst[:, :], E), features(ex[:, :], E),
                                            per_token(tot[:, :], QT, E), ALU.mult))
                    ch.settle()

                def each(name, u, i, entry):
                    k = entry[1]
                    if name == "gates1":
                        dve.wait_ge(lg_done, ready(u))
                        softmax_of(Chain(dve, g_step, G_STEPS * u), lg[k])
                    elif name == "gates2":
                        dve.wait_ge(g_exp, 2 * u + 1)
                        ch = Chain(dve, g_step, G_STEPS * u, 2)
                        normalise(ch, gates)
                        other = gates[:, :].rearrange("p (t o e) -> p t o e", o=1, e=E).broadcast_to([HP, QT, E, E])
                        own = gates[:, :].rearrange("p (t e o) -> p t e o", e=E, o=1).broadcast_to([HP, QT, E, E])
                        for c, op in ((ge, ALU.is_ge), (gt, ALU.is_gt)):
                            pairs = c[:, :].rearrange("p (t e f) -> p t e f", e=E, f=E)
                            ch.tick(v.tensor_tensor(pairs, other, own, op))
                        ch.settle()
                        for c, name in ((ge, "r_lower"), (gt, "r_higher")):
                            c = features(c[:, :], E * E)
                            ch.tick(v.tensor_tensor(c, c, row_of(w(name, HP), QT), ALU.mult))
                        ch.settle()
                        ch.tick(v.tensor_tensor(ge[:, :], ge[:, :], gt[:, :], ALU.add))
                        ch.settle()
                        ch.tick(v.tensor_reduce(rank[:, :], features(ge[:, :], E), AX.X, ALU.add))
                        softmax_of(ch, gates)
                    elif name == "gates3":
                        dve.wait_ge(g_exp, 2 * u + 2)
                        dve.wait_ge(gates_done, ready(u - 1))
                        ch = Chain(dve, g_step, G_STEPS * u, 13)
                        ch.tick(v.scalar_tensor_tensor(out=ex[:, :], in0=rank[:, :], scalar=1.5, in1=ex[:, :],
                                                       op0=ALU.is_lt, op1=ALU.mult))
                        ch.settle()
                        normalise(ch, gw)
                        dve.wait_ge(gt_psum, free(u, 1))
                        gate = ex[:, :].rearrange("p (t a e) -> p t a e", a=2, e=E)
                        total = tot[:, :].rearrange("p (t a e) -> p t a e", a=2, e=1).broadcast_to([HP, QT // 2, 2, E])
                        ch.tick(v.tensor_tensor(parts[:, :, 0, :].rearrange("p t (a e) -> p t a e", e=E)
                                                .bitcast(F32R), gate, total, ALU.mult))
                        assert ch.n == G_STEPS
                    elif name == "centre1":
                        centre(dve, N1, k, u, features(comb[:, bass.ds(u * 512, 512)]))
                    elif name == "var1":
                        variance(dve, N1, k, u)
                    elif name == "scale1":
                        scale(dve, N1, k, u, ct_psum)
                    elif name == "new":
                        dve.wait_ge(out_psum, ready(u))
                        dve.wait_ge(y_done, free(u))
                        v.tensor_tensor(new[k][:, :], hid[:, bass.ds(u * 512, 512)], B[k][0:HP, :], ALU.add)\
                            .then_inc(new_done, 1)
                        dve.wait_ge(new_done, ready(u))
                        centre(dve, N2, k, u, features(new[k][:, :]))
                    elif name == "var2":
                        variance(dve, N2, k, u)
                    elif name == "scale2":
                        scale(dve, N2, k, u, xs_psum)
                    elif name == "lg":
                        dve.wait_ge(lg_psum, ready(u))
                        v.tensor_tensor(features(lg[k][:, :], E), features(B[k][0:HP, 0:QT * E], E),
                                        row_of(w("r_gb", HP), QT), ALU.add).then_inc(lg_done, 1)
                    elif name in ("t", "s2", "w1"):
                        empty(dve, i, entry, False)
                    elif name == "z":
                        _, _, pair, p = entry
                        n = 4 * u + 2 * pair + p
                        dve.wait_ge(zr_done, ready(n))
                        dve.wait_ge(g_psum, n + 1)
                        dve.wait_ge(y_psum, ready(u - 1))
                        v.tensor_tensor(zg[2 * pair + p][:, :], zr[p][:, :], G[:, 0:QF], ALU.mult)\
                            .then_inc(zg_done, 1)
                    elif name == "y":
                        dve.wait_ge(y_psum, ready(u))
                        dve.wait_ge(out_stored[k], 32 * i + 16)
                        v.tensor_tensor(y[k][:, :], new[k][:, :], Y[0:HP, :], ALU.add).then_inc(y_done, 1)

                steps(dve)(each)

            @block.sync
            def _(sp):
                for x in out_stored:
                    sp.sem_inc(x, 16)
                with sp.Fori(0, NQ // 2) as i:
                    for k in two:
                        u = 2 * i + k
                        sp.wait_ge(y_done, ready(u))
                        for half in two:
                            rows = HP if half == 0 else L - HP
                            sp.dma_start(out[bass.ds(4 * u, 4), half * HP:half * HP + rows, :]
                                         .rearrange("b p f -> p b f"),
                                         y[k][0:rows, half * 256:half * 256 + 256].rearrange("p (b f) -> p b f", f=D))\
                                .then_inc(out_stored[k], 16)
                for k in two:
                    sp.wait_ge(out_stored[k], 16 + 32 * (NQ // 2))



def cubic(t):
    a, at = -0.75, abs(t)
    if at <= 1.0:
        return ((a + 2.0) * at - (a + 3.0)) * at * at + 1.0
    return ((a * at - 5.0 * a) * at + 8.0 * a) * at - 4.0 * a if at < 2.0 else 0.0


def diag(m, copies=2):
    r, c = m.shape
    out = np.zeros((r * copies, c * copies), m.dtype)
    for k in range(copies):
        out[k * r:(k + 1) * r, k * c:(k + 1) * c] = m
    return out


def token_pack():
    pack = np.zeros((128, TOK_W), np.float32)

    def put(name, a):
        at, width = TOK_COLS[name]
        assert a.shape[1] == width
        pack[0:a.shape[0], at:at + width] = a

    interp = np.zeros((TAPS, WIN))
    for j in range(WIN):
        for tap in range(4):
            interp[j // UP + tap, j] = cubic((j % UP) / UP - (tap - 1))
    put("interp", diag(interp.astype(np.float32)))
    j, k = np.arange(WIN)[:, None], np.arange(WIN)[None, :]
    angle = 2 * np.pi * ((j * np.where(k < NBIN, k, k - NBIN + 1)) % WIN) / WIN
    put("dft", diag((0.5 * np.where(k < NBIN, np.cos(angle), -np.sin(angle))).astype(np.float32)))
    put("b_gauss", np.full((128, 1), -0.7, np.float32))
    put("b_poly", np.full((128, 1), 1.3, np.float32))
    return pack


def phase_columns(kinds, unit=1.0):
    rows = [(-1.0, -unit, PI / 2) if kind == "c" else (1.0, unit, 0.0) for kind in kinds for _ in range(P)]
    return np.array(rows, np.float32)


def main_constants(put):
    put("ident", np.eye(128, dtype=np.float32))
    m, l = np.arange(HP)[:, None], np.arange(HP)[None, :]
    tri = (m <= l).astype(np.float32)
    put("mask", np.concatenate([tri, np.ones((HP, HP), np.float32)], 1))
    inv = (1.0 / (np.arange(LP) + 1.0))[None, :]
    put("mean0", (np.concatenate([tri, np.ones((HP, HP))], 1) * inv).astype(np.float32))
    put("mean1", (tri * inv[:, HP:]).astype(np.float32))
    s = np.tile(np.eye(P, dtype=np.float32), (H, 1))
    z = np.zeros_like(s)
    put("select", np.concatenate([s, z, z, s, z, s, -s, z], 1))
    put("posA", phase_columns("cscs"))
    put("posB", phase_columns("ccss"))
    put("posP", phase_columns("cscs", PI_BELOW))
    part_of = np.eye(2 * E, dtype=np.float32).reshape(2 * E, 2, 2, 2).transpose(0, 2, 1, 3).reshape(2 * E, 4, 2, 1)
    put("spread", np.tile(np.broadcast_to(part_of, (2 * E, 4, 2, 64)).reshape(2 * E, -1), (2, 1)))
    e, other = np.arange(E)[:, None], np.arange(E)[None, :]
    put("r_lower", np.tile((other < e).astype(np.float32).reshape(1, -1), (HP, 1)))
    put("r_higher", np.tile((other > e).astype(np.float32).reshape(1, -1), (HP, 1)))
    put("half_pi", np.full((128, 1), PI / 2, np.float32))
    put("minus_half", np.full((128, 8), -0.5, np.float32))


def kernel(**inputs):
    import concourse.bacc as _bacc
    from concourse import mybir as _mybir
    from concourse.bass_utils import run_bass_kernel_spmd as _run

    a = {k.replace("L0_attn_", "").replace("L0_ffn_", ""): np.asarray(v) for k, v in inputs.items()}
    pack = np.zeros((128, MAIN_W), np.float32)

    def put(name, m, first=0):
        at, width = MAIN_COLS[name]
        assert m.shape[1] == width, (name, m.shape)
        pack[first:first + m.shape[0], at:at + width] = m

    def col(name, v, copies=1):
        put(name, np.tile(v.reshape(-1, 1), (copies, 1)))

    def row(name, v):
        put(name, np.tile(v.reshape(1, -1), (HP, 1)))

    def dup(m):
        return np.concatenate([m, m], 1)

    def between(m):
        z = np.zeros_like(m)
        return np.concatenate([z, m, z], 1)

    main_constants(put)
    pos = np.zeros((P, LP), np.float32)
    pos[:, :L] = a["pos_phases"][:L].T
    put("pos", np.tile(pos, (4, 1)))
    put("hop1p", dup(a["hop_w1"][D:]))
    put("kce_t", dup(a["kce_w"].T))
    col("kce_b", a["kce_b"])
    put("kskc", dup(a["ksk_w1"][D:]))
    put("hop1", diag(a["hop_w1"][:D]))
    put("ksk1", diag(a["ksk_w1"][:D]))
    put("sg1", diag(a["sg_w1"]))
    put("key1", diag(dup(a["cpe_w"])))
    put("mc", diag(a["mc_w"]))
    put("ve", diag(a["ve_w"]))
    hop2 = a["hop_w2"].reshape(D, H, P + 1)
    put("hopc", np.tile(hop2[:, :, :P].reshape(D, H * P), (2, 1)))
    put("hopw", diag(hop2[:, :, P]))
    put("ksk2", diag(dup(a["ksk_w2"])))
    put("sg2", diag(a["sg_w2"]))
    put("outw", diag(a["out_w"]))
    put("outw64", a["out_w"])
    put("lnb", np.tile(a["ln_b"].reshape(D, 1), (1, HP)))
    col("lng", a["ln_g"], 2)
    col("b_hop1", a["hop_b1"], 2)
    col("b_ksk1", a["ksk_b1"], 2)
    col("b_sg1", a["sg_b1"], 2)
    col("b_cpe", a["cpe_b"], 4)
    hopb = a["hop_b2"].reshape(H, P + 1)
    col("b_hopc", hopb[:, :P].reshape(-1))
    row("r_hopw", hopb[:, P])
    col("b_ksk2", a["ksk_b2"], 4)
    col("b_sg2", a["sg_b2"], HP)
    put("sW1", diag(a["sW1"]))
    put("sW2", np.tile(a["sW2"], (2, 1)))
    put("sW3", between(a["sW3"]))
    put("eW1", np.tile(a["eW1"].transpose(1, 0, 2).reshape(D, -1), (2, 1)))
    put("eW2", a["eW2"].transpose(1, 0, 2).reshape(128, -1))
    for name, pair in (("eW3a", 0), ("eW3b", 1)):
        put(name, between(a["eW3"].reshape(2, 128, D)[pair]))
    put("gW", diag(a["gW"]))
    col("b_s1", a["sb1"], 2)
    col("b_s2", a["sb2"])
    put("b_e1", a["eb1"].T)
    put("b_e2", a["eb2"].reshape(2, 128).T)
    row("r_mc", a["mc_b"])
    row("r_ve", a["ve_b"])
    row("r_out", a["out_b"])
    row("r_gb", a["gb"])
    third = np.zeros((GONE + 1, 2 * D), np.float32)
    for p in range(2):
        for part in range(2):
            r = (part * 2 + p) * E
            third[r:r + E, p * D:p * D + D] = a["eb3"]
        third[GONE, p * D:p * D + D] = a["sb3"]
    put("third_b", third)
    row("r_delta", a["window_deltas"])

    at = np.clip(np.arange(TAPS)[:, None] - 1 + (WIN // UP) * np.arange(LP)[None, :], 0, NS - 1)
    windows = a["x"][:, at].reshape(NB // 2, 2, TAPS, LP).transpose(1, 2, 0, 3).reshape(2 * TAPS, -1)

    nc = _bacc.Bacc("TRN2", target_bir_lowering=False, num_devices=1)
    arrays, args = {}, []
    for name, arr in (("tok_pack", token_pack()), ("main_pack", pack), ("windows", windows)):
        arrays[name] = np.ascontiguousarray(arr)
        args.append(nc.dram_tensor(name, arr.shape, _mybir.dt.from_np(arr.dtype), kind="ExternalInput").ap())
    args.append(nc.dram_tensor("tower_out", (NB, L, D), _mybir.dt.float32, kind="ExternalOutput").ap())
    audio_tower(nc, *args)
    r = _run(nc, [arrays], core_ids=[0])
    return r.results[0]["tower_out"]
```

```python
from contextlib import ExitStack

import numpy as np

import concourse.bass as bass
from concourse import mybir

F32, F32R = mybir.dt.float32, mybir.dt.float32r
ALU = mybir.AluOpType
ACT = mybir.ActivationFunctionType
AX = mybir.AxisListType

NB, NS = 32, 4000
L, D, P, H, WN = 249, 64, 32, 4, 5
HP = 125
LP = 2 * HP
WIN, UP = 64, 4
NQ = NB // 4
QT = 4 * 2
QF = 2 * LP
NT = NB * 2
TAPS = WIN // UP + 3
NBIN = WIN // 2 + 1
E = 4
GONE = 32
G_STEPS = 18
ALPHA, BETA = 0.12, 0.9
PI = float(np.pi)
PI_BELOW = float(np.nextafter(np.float32(np.pi), np.float32(0)))
ROUND = 1.5 * 2.0 ** 23
TWO_PI = (6.28125, 2 * PI - 6.28125 - (2 * PI - 6.28125) % 2.0 ** -19, (2 * PI - 6.28125) % 2.0 ** -19)



def columns(widths):
    at, out = 0, {}
    for name, w in widths:
        out[name] = (at, w)
        at += w
    return out, at


TOK_COLS, TOK_W = columns([("interp", 128), ("dft", 128), ("b_gauss", 1), ("b_poly", 1)])
MAIN_COLS, MAIN_W = columns([
    ("ident", 128), ("mask", 2 * HP), ("mean0", LP), ("mean1", HP), ("select", 2 * 128),
    ("posA", 3), ("posB", 3), ("posP", 3), ("half_pi", 1), ("minus_half", 8),
    ("pos", LP), ("hop1p", 128), ("kce_t", 128), ("kce_b", 1), ("kskc", 128),
    ("hop1", 128), ("ksk1", 128), ("sg1", 64), ("key1", 128), ("mc", 128), ("ve", 128),
    ("hopc", 128), ("hopw", 8), ("ksk2", 128), ("sg2", 2), ("outw", 128), ("outw64", 64),
    ("lnb", HP), ("lng", 1),
    ("b_hop1", 1), ("b_ksk1", 1), ("b_sg1", 1), ("b_cpe", 1), ("b_hopc", 1), ("b_ksk2", 1), ("b_sg2", 1),
    ("sW1", 128), ("sW2", 128), ("sW3", 3 * D), ("eW1", E * 128), ("eW2", E * 64), ("eW3a", 3 * D), ("eW3b", 3 * D), ("gW", 8),
    ("b_s1", 1), ("b_s2", 1), ("b_e1", E), ("b_e2", 2),
    ("r_mc", D), ("r_ve", D), ("r_hopw", H), ("r_out", D), ("r_gb", E), 
    ("r_delta", WN), ("r_lower", E * E), ("r_higher", E * E), ("spread", 4 * 128), ("third_b", 128),
])


def ready(u, slots=2):
    return u + (1 + slots)


def free(u, slots=2):
    return u + 1


def bodies(eng, body):
    with eng.Fori(0, NQ // 2 - 1) as i:
        body(i, True)
    body(NQ // 2 - 1, False)


class Chain:

    def __init__(self, eng, sem, base=0, n=0):
        self.eng, self.sem, self.base, self.n = eng, sem, base, n

    def tick(self, ins):
        ins.then_inc(self.sem, 1)
        self.n += 1
        return ins

    def settle(self):
        self.eng.wait_ge(self.sem, self.base + self.n)


def audio_tower(nc, tok_pack, main_pack, windows, out):
    ctx = ExitStack()
    with ctx:
        def sb(name, shape, stack=ctx):
            return stack.enter_context(nc.sbuf_tensor(name, shape, F32))

        def bank(name, stack):
            return stack.enter_context(nc.psum_tensor(name, [128, 512], F32))

        def sem(name):
            return ctx.enter_context(nc.semaphore(name))

        main = sb("main", [128, MAIN_W])
        table = sb("table", [128, 1])
        hid = sb("hid", [HP, NT * D])

        def w(name, rows=128, a=0, b=None, first=0):
            at, width = MAIN_COLS[name]
            return main[first:first + rows, at + a:at + (width if b is None else b)]

        main_loaded = sem("main_loaded")

        with ExitStack() as st:
            s, setup_work = setup(nc, sb, bank, sem, w, main_loaded, st)
            tokens(nc, sb, bank, sem, tok_pack, main_pack, windows, main, main_loaded, hid, table, setup_work)
        cont = sb("cont", [HP, NT * D])
        with ExitStack() as st:
            cen = sb("cen", [128, NQ * 2 * QF], st)
            key, sto = sb("key", [128, NQ * QF], st), sb("sto", [128, NQ * QF], st)
            val = sb("val", [HP, NT * D], st)
            wid, gat = sb("wid", [HP, NT * H], st), sb("gat", [HP, NT], st)
            split = sb("mix_split", [HP, NQ * 128], st)
            attention_inputs(nc, sb, bank, sem, w, s, table, split, hid, cen, key, sto, cont, val, wid, gat)

            def retrieval(start_of_rest):
                attend(nc, sb, bank, sem, w, s, cen, key, sto, cont, val, wid, gat, split, start_of_rest)

            project_and_experts(nc, sb, bank, sem, w, s, hid, cont, out, (cen, key, sto), retrieval)


def tokens(nc, sb, bank, sem, tok_pack, main_pack, windows, main, main_loaded, hid, table, setup_work):
    with ExitStack() as st:
        tok = sb("tok", [128, TOK_W], st)
        win = sb("win", [2 * TAPS, NQ * QF], st)
        power = sb("power", [HP, NT * NBIN], st)
        sq = [sb(f"sq{s}", [128, QF], st) for s in range(2)]
        poly = [sb(f"poly{s}", [128, QF], st) for s in range(2)]
        gauss = [sb(f"gauss{s}", [128, QF], st) for s in range(2)]
        kw = [sb(f"kw{s}", [128, QF], st) for s in range(2)]
        parts2 = [sb(f"parts2_{s}", [HP, 512], st) for s in range(2)]
        CW = NT * NBIN // 2
        CT = NT // 2
        mag = sb("mag", [HP, 2 * CW], st)
        d = sb("d", [HP, 2 * CW], st)
        e = sb("e", [HP, 2 * CW], st)
        mx = sb("mx", [HP, NT], st)
        psI = [bank(f"psI{s}", st) for s in range(2)]
        psD = [bank(f"psD{s}", st) for s in range(2)]

        tok_loaded, win_loaded = sem("tok_loaded"), sem("win_loaded")
        interp_ready, poly_ready, square_ready, gauss_ready = (
            sem("interp_ready"), sem("poly_ready"), sem("square_ready"), sem("gauss_ready"))
        kw_ready, dft_ready, parts_ready, power_ready = (
            sem("kw_ready"), sem("dft_ready"), sem("parts_ready"), sem("power_ready"))
        mag_ready, over_ready, mask_ready, gap_ready, gap_abs, exp_ready, log_ready = (
            sem("mag_ready"), sem("over_ready"), sem("mask_ready"), sem("gap_ready"), sem("gap_abs"), sem("exp_ready"),
            sem("log_ready"))
        vec_step = sem("tok_vec_step")

        def t(name, rows=128):
            at, width = TOK_COLS[name]
            return tok[0:rows, at:at + width]

        with nc.Block() as block:
            @block.sync
            def _(sp):
                sp.dma_start(tok[:, :], tok_pack[:, :]).then_inc(tok_loaded, 16)
                for c in range(4):
                    a, b = c * 2 * QF, (c + 1) * 2 * QF
                    sp.dma_start(win[:, a:b], windows[:, a:b]).then_inc(win_loaded, 16)
                    sp.wait_ge(win_loaded, 16 * (c + 1))
                sp.dma_start(main[:, :], main_pack[:, :]).then_inc(main_loaded, 16)

            @block.tensor
            def _(pe):
                pe.sem_inc(interp_ready, 2)
                pe.sem_inc(dft_ready, 2)
                pe.wait_ge(tok_loaded, 16)

                def interpolate(i):
                    pe.wait_ge(win_loaded, 16 * i + 16)
                    for s in range(2):
                        pe.wait_ge(poly_ready, free(2 * i + s))
                        nc.tensor.matmul(psI[s][:, 0:QF], t("interp", 2 * TAPS),
                                         win[:, bass.ds((2 * i + s) * QF, QF)], start=True, stop=True)\
                            .then_inc(interp_ready, 1)

                def body(i, more):
                    if more:
                        interpolate(i + 1)
                    for s in range(2):
                        pe.wait_ge(kw_ready, ready(2 * i + s))
                        pe.wait_ge(parts_ready, free(2 * i + s))
                        for half in range(2):
                            for pair in range(2):
                                c = pair * LP + half * HP
                                o = (half * 2 + pair) * 128
                                mm = nc.tensor.matmul(psD[s][0:HP, o:o + 128], kw[s][:, c:c + HP], t("dft"),
                                                      start=True, stop=True)
                        mm.then_inc(dft_ready, 1)

                interpolate(0)
                bodies(pe, body)
                setup_work["tensor"](pe)

            @block.scalar
            def _(act):
                for x in (poly_ready, square_ready, gauss_ready, parts_ready):
                    act.sem_inc(x, 2)
                act.wait_ge(tok_loaded, 16)
                nc.scalar.activation(table[0:1, :], t("b_poly", 1), ACT.Exp)

                def kernels(i):
                    for s in range(2):
                        act.wait_ge(interp_ready, ready(2 * i + s))
                        nc.scalar.activation(sq[s][:, :], psI[s][:, 0:QF], ACT.Square, bias=t("b_gauss"))\
                            .then_inc(square_ready, 1)
                        act.wait_ge(kw_ready, free(2 * i + s))
                        nc.scalar.activation(poly[s][:, :], psI[s][:, 0:QF], ACT.Square, bias=t("b_poly"))\
                            .then_inc(poly_ready, 1)
                        act.wait_ge(square_ready, ready(2 * i + s))
                        nc.scalar.activation(gauss[s][:, :], sq[s][:, :], ACT.Exp, scale=-0.5)\
                            .then_inc(gauss_ready, 1)

                def body(i, more):
                    if more:
                        kernels(i + 1)
                    else:
                        magnitudes(0)
                    for s in range(2):
                        act.wait_ge(dft_ready, ready(2 * i + s))
                        act.wait_ge(power_ready, free(2 * i + s))
                        nc.scalar.activation(parts2[s][:, :], psD[s][0:HP, :], ACT.Square)\
                            .then_inc(parts_ready, 1)

                def magnitudes(c):
                    a, b = c * CW, (c + 1) * CW
                    act.wait_ge(power_ready, ready((c + 1) * NQ // 2 - 1))
                    nc.scalar.activation(mag[:, a:b], power[:, a:b], ACT.Sqrt).then_inc(mag_ready, 1)

                kernels(0)
                bodies(act, body)
                magnitudes(1)
                for c in range(2):
                    a, b = c * CW, (c + 1) * CW
                    act.wait_ge(over_ready, c + 1)
                    nc.scalar.activation(e[:, a:b], d[:, a:b], ACT.Tanh, scale=0.5).then_inc(mask_ready, 1)
                for c in range(2):
                    a, b = c * CW, (c + 1) * CW
                    act.wait_ge(gap_ready, c + 1)
                    nc.scalar.activation(power[:, a:b], d[:, a:b], ACT.Abs).then_inc(gap_abs, 1)
                    act.wait_ge(gap_abs, c + 1)
                    nc.scalar.activation(e[:, a:b], power[:, a:b], ACT.Exp, scale=-0.5).then_inc(exp_ready, 1)
                for c in range(2):
                    a, b = c * CW, (c + 1) * CW
                    act.wait_ge(exp_ready, c + 1)
                    nc.scalar.activation(power[:, a:b], e[:, a:b], ACT.Ln, bias=1.0).then_inc(log_ready, 1)
                setup_work["scalar"](act)

            @block.vector
            def _(dve):
                dve.sem_inc(kw_ready, 2)
                dve.sem_inc(power_ready, 2)

                def mix_kernels(i):
                    for s in range(2):
                        dve.wait_ge(gauss_ready, ready(2 * i + s))
                        dve.wait_ge(poly_ready, ready(2 * i + s))
                        dve.wait_ge(dft_ready, free(2 * i + s))
                        nc.vector.tensor_tensor(kw[s][:, :], poly[s][:, :], gauss[s][:, :], ALU.add)\
                            .then_inc(kw_ready, 1)

                def body(i, more):
                    if more:
                        mix_kernels(i + 1)
                    else:
                        setup_work["vector"][0](dve)
                        maxima(0)
                    for s in range(2):
                        dve.wait_ge(parts_ready, ready(2 * i + s))
                        v = parts2[s][:, :].rearrange("p (t f) -> p t f", f=WIN)
                        o = power[:, bass.ds((2 * i + s) * (QT * NBIN), QT * NBIN)]\
                            .rearrange("p (t f) -> p t f", f=NBIN)
                        nc.vector.tensor_copy(o[:, :, 0:NBIN:NBIN - 1], v[:, :, 0:NBIN:NBIN - 1])
                        nc.vector.tensor_tensor(o[:, :, 1:NBIN - 1], v[:, :, 1:NBIN - 1], v[:, :, NBIN:WIN],
                                                ALU.add).then_inc(power_ready, 1)
                    if not more:
                        threshold(0)

                ch = Chain(dve, vec_step)

                def view(x, c):
                    return x[:, c * CW:(c + 1) * CW].rearrange("p (t f) -> p t f", f=NBIN)

                def top(c):
                    return mx[:, c * CT:(c + 1) * CT].rearrange("p (t a) -> p t a", a=1)\
                        .broadcast_to([HP, CT, NBIN])

                def maxima(c):
                    dve.wait_ge(mag_ready, c + 1)
                    ch.tick(nc.vector.tensor_reduce(mx[:, c * CT:(c + 1) * CT], view(mag, c), AX.X, ALU.max))

                def threshold(c):
                    ch.settle()
                    nc.vector.scalar_tensor_tensor(out=view(d, c), in0=top(c), scalar=-ALPHA, in1=view(mag, c),
                                                   op0=ALU.mult, op1=ALU.add).then_inc(over_ready, 1)

                mix_kernels(0)
                bodies(dve, body)
                maxima(1)
                threshold(1)
                for c in range(2):
                    a, b = c * CW, (c + 1) * CW
                    dve.wait_ge(mask_ready, c + 1)
                    ch.tick(nc.vector.scalar_tensor_tensor(out=mag[:, a:b], in0=e[:, a:b], scalar=1.0,
                                                           in1=mag[:, a:b], op0=ALU.add, op1=ALU.mult))
                    ch.settle()
                    nc.vector.scalar_tensor_tensor(out=view(d, c), in0=top(c), scalar=-2 * BETA,
                                                   in1=view(mag, c), op0=ALU.mult, op1=ALU.add)\
                        .then_inc(gap_ready, 1)
                    dve.wait_ge(gap_ready, c + 1)
                    ch.tick(nc.vector.scalar_tensor_tensor(out=view(mag, c), in0=top(c), scalar=2 * BETA,
                                                           in1=view(mag, c), op0=ALU.mult, op1=ALU.min))
                setup_work["vector"][1](dve)
                for c in range(2):
                    a, b = c * CW, (c + 1) * CW
                    dve.wait_ge(log_ready, c + 1)
                    h = hid[:, c * CT * D:(c + 1) * CT * D].rearrange("p (t f) -> p t f", f=D)
                    m, lg = view(mag, c), view(power, c)
                    ch.settle()
                    ch.tick(nc.vector.scalar_tensor_tensor(out=h[:, :, 0:NBIN], in0=m, scalar=0.5, in1=lg,
                                                           op0=ALU.mult, op1=ALU.subtract))
                    ch.settle()
                    ch.tick(nc.vector.tensor_copy(h[:, :, NBIN:D], h[:, :, NBIN - 2:0:-1]))
                ch.settle()


def setup(nc, sb, bank, sem, w, main_loaded, loc):
    s = {}
    s["kskc"] = sb("kskc_bd", [128, 128])
    s["b_ksk"] = sb("b_ksk", [128, 1])
    s["outw"] = sb("outw_scaled", [128, 128])
    s["r_out"] = sb("r_outb", [HP, D])
    s["hop_pos"] = sb("hop_pos", [128, LP])
    s["tabA"] = sb("tabA", [128, LP])
    s["tabB"] = sb("tabB", [128, LP])
    s["cosd"] = sb("cosd", [HP, WN])
    s["sind"] = sb("sind", [HP, WN])
    s["decay"] = sb("decay", [HP, WN])
    s["b_sg2"] = sb("b_sg2_half", [HP, 1])
    ps0, ps1 = bank("ps_setup0", loc), bank("ps_setup1", loc)
    turns, rest, shape = (sb(n, [128, LP + WN], loc) for n in ("turns", "rest", "shape"))
    shapeB = sb("shapeB", [128, LP], loc)
    setup_products, trig_args, trig_done = sem("setup_products"), sem("trig_args"), sem("trig_done")
    step, act_step = sem("setup_step"), sem("setup_act_step")
    def tensor(pe):
        pe.wait_ge(main_loaded, 16)
        nc.tensor.matmul(ps0[:, 0:64], w("kce_t", 64), w("kskc", 64, 0, 64), start=True, stop=True)
        nc.tensor.matmul(ps0[:, 64:65], w("kskc", 64), w("kce_b", 64), start=True, stop=True)
        nc.tensor.matmul(ps0[0:HP, 128:192], w("lnb", 64), w("outw64", 64), start=True, stop=True)
        nc.tensor.matmul(ps1[:, 0:LP], w("hop1p", 32), w("pos", 32), start=True, stop=True)\
            .then_inc(setup_products, 1)

    ch = Chain(None, step)

    def scale_and_count_turns(dve):
        ch.eng = dve
        dve.wait_ge(main_loaded, 16)
        ch.tick(nc.vector.memset(s["kskc"][:, :], 0.0))
        ch.tick(nc.vector.tensor_scalar(s["outw"][:, :], w("outw"), w("lng"), None, ALU.mult))
        ch.tick(nc.vector.tensor_scalar(s["b_sg2"][:, :], w("b_sg2", HP), 0.5, None, ALU.mult))
        ch.tick(nc.vector.tensor_tensor(s["decay"][:, :], w("r_delta", HP), w("r_delta", HP), ALU.mult))
        ch.tick(nc.vector.tensor_copy(rest[:, 0:LP], w("pos")))
        ch.tick(nc.vector.memset(rest[:, LP:LP + WN], 0.0))
        ch.settle()
        ch.tick(nc.vector.tensor_scalar(rest[0:HP, LP:LP + WN], w("r_delta", HP), 0.1, None, ALU.mult))
        ch.tick(nc.vector.tensor_scalar(s["decay"][:, :], s["decay"][:, :], -0.5, None, ALU.mult))
        ch.settle()
        ch.tick(nc.vector.tensor_scalar(turns[:, :], rest[:, :], 1 / (2 * PI), ROUND, ALU.mult, ALU.add))
        ch.settle()
        ch.tick(nc.vector.tensor_scalar(turns[:, :], turns[:, :], -ROUND, None, ALU.add))

    def reduce_phases(dve):
        for part in TWO_PI:
            ch.settle()
            ch.tick(nc.vector.scalar_tensor_tensor(out=rest[:, :], in0=turns[:, :], scalar=-part,
                                                   in1=rest[:, :], op0=ALU.mult, op1=ALU.add))
        ch.settle()
        ch.tick(nc.vector.tensor_scalar(rest[:, :], rest[:, :], PI_BELOW, -PI_BELOW, ALU.min, ALU.max))
        ch.settle()
        nc.vector.scalar_tensor_tensor(out=shape[:, 0:LP], in0=rest[:, 0:LP], scalar=w("posA", b=1),
                                       in1=rest[:, 0:LP], op0=ALU.mult, op1=ALU.max).then_inc(trig_args, 1)
        nc.vector.scalar_tensor_tensor(out=shapeB[:, :], in0=rest[:, 0:LP], scalar=w("posB", b=1),
                                       in1=rest[:, 0:LP], op0=ALU.mult, op1=ALU.max).then_inc(trig_args, 1)
        nc.vector.scalar_tensor_tensor(out=shape[0:HP, LP:], in0=rest[0:HP, LP:], scalar=-1.0,
                                       in1=rest[0:HP, LP:], op0=ALU.mult, op1=ALU.max)\
            .then_inc(trig_args, 1)
        dve.wait_ge(setup_products, 1)
        for r in (0, 64):
            ch.tick(nc.vector.tensor_copy(s["kskc"][r:r + 64, r:r + 64], ps0[r:r + 64, 0:64]))
        ch.tick(nc.vector.tensor_tensor(s["b_ksk"][:, :], ps0[:, 64:65], w("b_ksk1"), ALU.add))
        ch.tick(nc.vector.tensor_tensor(s["r_out"][:, :], ps0[0:HP, 128:192], w("r_out", HP), ALU.add))

    def scalar(act):
        act.wait_ge(trig_args, 3)
        nc.scalar.activation(s["tabA"][:, :], shape[:, 0:LP], ACT.Sin, bias=w("posA", a=2, b=3),
                             scale=w("posA", a=1, b=2))
        nc.scalar.activation(s["tabB"][:, :], shapeB[:, :], ACT.Sin, bias=w("posB", a=2, b=3),
                             scale=w("posB", a=1, b=2))
        nc.scalar.activation(s["cosd"][:, :], shape[0:HP, LP:], ACT.Sin, bias=w("half_pi", HP),
                             scale=-1.0)
        nc.scalar.activation(s["sind"][:, :], rest[0:HP, LP:], ACT.Sin)
        act.wait_ge(setup_products, 1)
        nc.scalar.activation(s["hop_pos"][:, :], ps1[:, 0:LP], ACT.Identity, bias=w("b_hop1"))
    return s, {"tensor": tensor, "vector": (scale_and_count_turns, reduce_phases), "scalar": scalar}


def per_token(stat, n, f=D):
    return stat.rearrange("p (t a) -> p t a", a=1).broadcast_to([stat.shape[0], n, f])


def features(x, f=D):
    return x.rearrange("p (t f) -> p t f", f=f)


def row_of(x, n):
    return x.rearrange("p (a f) -> p a f", a=1).broadcast_to([x.shape[0], n, x.shape[1]])


def attention_inputs(nc, sb, bank, sem, w, s, table, split, hid, cen, key, sto, cont, val, wid, gat):
    with ExitStack() as st:
        two = range(2)
        mu, var, rstd, tg = ([sb(f"{n}{k}", [HP, QT], st) for k in two] for n in ("mu", "var", "rstd", "tg"))
        xc, xn, vraw = ([sb(f"{n}{k}", [HP, 512], st) for k in two] for n in ("xc", "xn", "vraw"))
        sqx = [sb(f"sqx{k}", [HP, 512], st) for k in two]
        xb = sb("xb", [HP, 512], st)
        xt, cm, hopin, hh, kh = ([sb(f"{n}{k}", [128, QF], st) for k in two] for n in ("xt", "cm", "hopin", "hh", "kh"))
        sh = [sb(f"sh{k}", [64, QF], st) for k in two]
        hs = [[sb(f"hh_split{k}_{p}", [128, QF], st) for p in two] for k in two]
        hopc_high, hopc_low = sb("hopc_high", [128, 128], st), sb("hopc_low", [128, 128], st)
        hs_high, hs_done, hopc_split = sem("in_hs_high"), sem("in_hs_done"), sem("in_hopc_split")
        B = [[bank(f"in{k}_{j}", st) for j in range(4)] for k in two]
        ww = window_weights(nc, sem, w, s, "wa", (0, NQ - 2), wid, split,
                            sb("ww_room", [HP, (NQ - 2) * QT * H * (WN + 5)], st))
        (xc_ready, sqx_ready, var_ready, rstd_ready, xn_ready, hx_done, xt_psum, xt_done, cm_psum, cm_done,
         hop_psum, hopin_done, hh_done, sg_psum, sg_done, ksk_psum, ksk_done, key_psum, key_done, cont_psum,
         cont_done, val_psum, val_done, gv_done, cen0_psum, cen0_done, cen1_psum, cen1_done, st_psum, st_done,
         small_psum, width_done, tg_done, gat_ready) = (sem("in_" + n) for n in (
             "xc_ready sqx_ready var_ready rstd_ready xn_ready hx_done xt_psum xt_done cm_psum cm_done "
             "hop_psum hopin_done hh_done sg_psum sg_done ksk_psum ksk_done key_psum key_done cont_psum "
             "cont_done val_psum val_done gv_done cen0_psum cen0_done cen1_psum cen1_done st_psum st_done "
             "small_psum width_done tg_done gat_ready").split())
        vec_step, xb_ready = sem("in_vec_step"), sem("in_xb_ready")
        STEPS = 6

        def tile(x, half, pair, n=HP):
            c = pair * LP + half * HP
            return x[:, c:c + n]

        with nc.Block() as block:
            @block.tensor
            def _(pe):
                for x in (xt_psum, cm_psum, hop_psum, sg_psum, ksk_psum, key_psum, cont_psum, val_psum,
                          cen0_psum, cen1_psum, st_psum, small_psum):
                    pe.sem_inc(x, 2)
                mm = nc.tensor.matmul
                def turn_and_mean(i):
                    for k in two:
                        u = 2 * i + k
                        b0, b1 = B[k][0], B[k][1]
                        pe.wait_ge(xn_ready, ready(u))
                        pe.wait_ge(cen1_done, free(u))
                        for half in two:
                            for pair in two:
                                o = (half * 2 + pair) * 128
                                x = nc.tensor.transpose(tile(b0, half, pair), xn[k][:, o:o + 128],
                                                        w("ident", HP, 0, HP))
                        x.then_inc(xt_psum, 1)
                        pe.wait_ge(cen0_done, free(u))
                        for pair in two:
                            mm(tile(b1, 0, pair, LP), xn[k][:, pair * 128:pair * 128 + 128], w("mean0", HP),
                               start=True, stop=False)
                            x = mm(tile(b1, 1, pair), xn[k][:, 256 + pair * 128:256 + pair * 128 + 128],
                                   w("mean1", HP), start=False, stop=True)
                        x.then_inc(cm_psum, 1)
                def body(i, more):
                    for k in two:
                        u = 2 * i + k
                        b2, b3 = B[k][2], B[k][3]
                        pe.wait_ge(xt_done, ready(u))
                        pe.wait_ge(st_done, free(u))
                        mm(b2[:, 0:QF], w("hop1"), xt[k][:, :], start=True, stop=True).then_inc(hop_psum, 1)
                        pe.wait_ge(tg_done, free(u))
                        mm(b3[0:64, 0:QF], w("sg1"), xt[k][:, :], start=True, stop=True).then_inc(sg_psum, 1)
                    for k in two:
                        u = 2 * i + k
                        b0, b1 = B[k][0], B[k][1]
                        pe.wait_ge(cm_done, ready(u))
                        mm(b1[:, 0:QF], w("ksk1"), xt[k][:, :], start=True, stop=False)
                        mm(b1[:, 0:QF], s["kskc"][:, :], cm[k][:, :], start=False, stop=True)\
                            .then_inc(ksk_psum, 1)
                        mm(b0[:, 0:QF], w("key1"), xt[k][:, :], start=True, stop=True).then_inc(key_psum, 1)
                    for k in two:
                        u = 2 * i + k
                        for b, name, read, signal in ((B[k][2], "mc", hopin_done, cont_psum),
                                                      (B[k][3], "ve", sg_done, val_psum)):
                            pe.wait_ge(read, ready(u))
                            for half in two:
                                for pair in two:
                                    o = (half * 2 + pair) * 128
                                    x = mm(b[0:HP, o:o + 128], tile(xt[k], half, pair), w(name),
                                           start=True, stop=True)
                            x.then_inc(signal, 1)
                    for k in two:
                        u = 2 * i + k
                        b0, b1, b3 = B[k][0], B[k][1], B[k][3]
                        pe.wait_ge(ksk_done, ready(u))
                        pe.wait_ge(hs_done, ready(u))
                        for c in (hopc_high, hopc_low):
                            x = mm(b1[:, 0:QF], c[:, :].bitcast(F32R), hs[k][0][:, :].bitcast(F32R),
                                   start=c is hopc_high, stop=c is hopc_low)
                        x.then_inc(cen0_psum, 1)
                        pe.wait_ge(key_done, ready(u))
                        for c in (hopc_high, hopc_low):
                            x = mm(b0[:, 0:QF], c[:, :].bitcast(F32R), hs[k][1][:, :].bitcast(F32R),
                                   start=c is hopc_high, stop=c is hopc_low)
                        x.then_inc(cen1_psum, 1)
                        pe.wait_ge(cont_done, ready(u))
                        mm(B[k][2][:, 0:QF], w("ksk2"), kh[k][:, :], start=True, stop=True).then_inc(st_psum, 1)
                        pe.wait_ge(val_done, ready(u))
                        for pair in two:
                            o = 0 * 2 + pair
                            mm(b3[0:HP, o * 8:o * 8 + 8], tile(hh[k], 0, pair), w("hopw"),
                               start=True, stop=True)
                            x = mm(b3[0:HP, 32 + o * 2:34 + o * 2], tile(sh[k], 0, pair), w("sg2", 64),
                                   start=True, stop=True)
                        for pair in two:
                            o = 1 * 2 + pair
                            mm(b3[0:HP, o * 8:o * 8 + 8], tile(hh[k], 1, pair), w("hopw"),
                               start=True, stop=True)
                            x = mm(b3[0:HP, 32 + o * 2:34 + o * 2], tile(sh[k], 1, pair), w("sg2", 64),
                                   start=True, stop=True)
                        x.then_inc(small_psum, 1)
                    if more:
                        turn_and_mean(i + 1)

                turn_and_mean(0)
                pe.wait_ge(hopc_split, 2)
                bodies(pe, body)

            @block.scalar
            def _(act):
                for x in (sqx_ready, xt_done, sg_done, hh_done, ksk_done, key_done, cen0_done, cen1_done,
                          st_done, tg_done, hs_high):
                    act.sem_inc(x, 2)
                f = nc.scalar.activation
                def squares(i):
                    for k in two:
                        u = 2 * i + k
                        act.wait_ge(xc_ready, ready(u))
                        act.wait_ge(var_ready, free(u))
                        f(sqx[k][:, :], xc[k][:, :], ACT.Square).then_inc(sqx_ready, 1)

                def body(i, more):
                    for k in two:
                        u = 2 * i + k
                        act.wait_ge(xt_psum, ready(u))
                        act.wait_ge(val_psum, free(u))
                        f(xt[k][:, :], B[k][0][:, 0:QF], ACT.Copy).then_inc(xt_done, 1)
                    if not more:
                        ww["widths"](act)
                    for k in two:
                        u = 2 * i + k
                        act.wait_ge(small_psum, free(u))
                        act.wait_ge(sg_psum, ready(u))
                        f(sh[k][:, :], B[k][3][0:64, 0:QF], ACT.Gelu, bias=w("b_sg1", 64)).then_inc(sg_done, 1)
                        act.wait_ge(hopin_done, ready(u))
                        f(hh[k][:, :], hopin[k][:, :], ACT.Gelu).then_inc(hh_done, 1)
                        act.wait_ge(cen1_psum, free(u))
                        act.wait_ge(hh_done, ready(u))
                        for p in two:
                            rows = slice(64 * p, 64 * p + 64)
                            x = f(hs[k][p][rows, :].bitcast(F32R), hh[k][rows, :], ACT.Copy)
                        x.then_inc(hs_high, 1)
                    if more:
                        squares(i + 1)
                    for k in two:
                        u = 2 * i + k
                        act.wait_ge(ksk_psum, ready(u))
                        act.wait_ge(st_psum, free(u))
                        f(kh[k][:, :], B[k][1][:, 0:QF], ACT.Gelu, bias=s["b_ksk"][:, :]).then_inc(ksk_done, 1)
                        act.wait_ge(key_psum, ready(u))
                        f(key[:, bass.ds(u * QF, QF)], B[k][0][:, 0:QF], ACT.Tanh, bias=w("b_cpe"))\
                            .then_inc(key_done, 1)
                    if not more:
                        ww["weights"](act)
                    for k in two:
                        u = 2 * i + k
                        for parity, b, need, signal in ((0, 1, cen0_psum, cen0_done), (1, 0, cen1_psum, cen1_done)):
                            act.wait_ge(need, ready(u))
                            f(cen[:, bass.ds(u * (2 * QF) + parity * QF, QF)], B[k][b][:, 0:QF], ACT.Tanh,
                              bias=w("b_hopc")).then_inc(signal, 1)
                    for k in two:
                        u = 2 * i + k
                        act.wait_ge(st_psum, ready(u))
                        f(sto[:, bass.ds(u * QF, QF)], B[k][2][:, 0:QF], ACT.Tanh, bias=w("b_ksk2"))\
                            .then_inc(st_done, 1)
                        act.wait_ge(small_psum, ready(u))
                        act.wait_ge(width_done, ready(u))
                        act.wait_ge(gat_ready, free(u))
                        f(tg[k][:, :], B[k][3][0:HP, 32:40], ACT.Tanh, bias=s["b_sg2"][:, :], scale=0.5)\
                            .then_inc(tg_done, 1)

                f(table[0:HP, :], s["b_sg2"][:, :], ACT.Gelu)
                squares(0)
                bodies(act, body)

            @block.vector
            def _(dve):
                for x in (xc_ready, var_ready, xn_ready, cm_done, hopin_done, cont_done, val_done, width_done,
                          gat_ready, hs_done):
                    dve.sem_inc(x, 2)
                v = nc.vector
                def centre(i):
                    ch = Chain(dve, vec_step, STEPS * i)
                    for k in two:
                        u = 2 * i + k
                        x = features(hid[:, bass.ds(u * 512, 512)])
                        ch.tick(v.tensor_reduce(mu[k][:, :], x, AX.X, ALU.add))
                        ch.settle()
                        ch.tick(v.tensor_scalar(mu[k][:, :], mu[k][:, :], -1.0 / D, None, ALU.mult))
                        ch.settle()
                        v.tensor_tensor(features(xc[k][:, :]), x, per_token(mu[k][:, :], QT), ALU.add)\
                            .then_inc(xc_ready, 1)

                def variance(i):
                    ch = Chain(dve, vec_step, STEPS * i, 4)
                    for k in two:
                        u = 2 * i + k
                        dve.wait_ge(sqx_ready, ready(u))
                        dve.wait_ge(rstd_ready, free(u))
                        ch.tick(v.tensor_reduce(var[k][:, :], features(sqx[k][:, :]), AX.X, ALU.add))
                        ch.settle()
                        v.tensor_scalar(var[k][:, :], var[k][:, :], 1.0 / D, 1e-5, ALU.mult, ALU.add)\
                            .then_inc(var_ready, 1)

                def scale(i):
                    for k in two:
                        u = 2 * i + k
                        dve.wait_ge(rstd_ready, ready(u))
                        dve.wait_ge(cm_psum, free(u))
                        dve.wait_ge(hx_done, free(u))
                        v.tensor_tensor(features(xn[k][:, :]), features(xc[k][:, :]), per_token(rstd[k][:, :], QT),
                                        ALU.mult).then_inc(xn_ready, 1)

                def body(i, more):
                    for k in two:
                        u = 2 * i + k
                        dve.wait_ge(cm_psum, ready(u))
                        dve.wait_ge(ksk_psum, free(u))
                        v.tensor_copy(cm[k][:, :], B[k][1][:, 0:QF]).then_inc(cm_done, 1)
                    for k in two:
                        u = 2 * i + k
                        dve.wait_ge(hop_psum, ready(u))
                        dve.wait_ge(hh_done, free(u))
                        v.tensor_tensor(features(hopin[k][:, :], LP), features(B[k][2][:, 0:QF], LP),
                                        row_of(s["hop_pos"][:, :], 2), ALU.add).then_inc(hopin_done, 1)
                    if more:
                        centre(i + 1)
                    else:
                        ww["reciprocals"](dve)
                    for k in two:
                        u = 2 * i + k
                        dve.wait_ge(hs_high, ready(u))
                        for p in two:
                            rows, other = slice(64 * p, 64 * p + 64), slice(64 - 64 * p, 128 - 64 * p)
                            x = v.tensor_tensor(hs[k][p][other, :].bitcast(F32R), hh[k][rows, :],
                                                hs[k][p][rows, :], ALU.subtract)
                        x.then_inc(hs_done, 1)
                    for k in two:
                        u = 2 * i + k
                        dve.wait_ge(cont_psum, ready(u))
                        v.tensor_tensor(features(cont[:, bass.ds(u * 512, 512)]), features(B[k][2][0:HP, :]),
                                        row_of(w("r_mc", HP), QT), ALU.add).then_inc(cont_done, 1)
                        dve.wait_ge(val_psum, ready(u))
                        dve.wait_ge(gv_done, free(u))
                        v.tensor_tensor(features(vraw[k][:, :]), features(B[k][3][0:HP, :]),
                                        row_of(w("r_ve", HP), QT), ALU.add).then_inc(val_done, 1)
                        if more and k == 0:
                            variance(i + 1)
                    if more:
                        scale(i + 1)
                    else:
                        ww["sums"](dve)
                        ww["normalise"](dve)
                    for k in two:
                        u = 2 * i + k
                        dve.wait_ge(small_psum, ready(u))
                        v.tensor_tensor(features(wid[:, bass.ds(u * 32, 32)], H), features(B[k][3][0:HP, 0:32], H),
                                        row_of(w("r_hopw", HP), QT), ALU.add).then_inc(width_done, 1)
                        dve.wait_ge(tg_done, ready(u))
                        v.tensor_scalar(gat[:, bass.ds(u * QT, QT)], tg[k][:, :], 0.5, 0.5, ALU.mult, ALU.add)\
                            .then_inc(gat_ready, 1)

                centre(0)
                v.tensor_copy(hopc_high[:, :].bitcast(F32R), w("hopc")).then_inc(hopc_split, 1)
                variance(0)
                dve.wait_ge(hopc_split, 1)
                v.tensor_tensor(hopc_low[:, :].bitcast(F32R), w("hopc"), hopc_high[:, :], ALU.subtract)\
                    .then_inc(hopc_split, 1)
                scale(0)
                bodies(dve, body)

            @block.gpsimd
            def _(pool):
                for x in (rstd_ready, hx_done, gv_done):
                    pool.sem_inc(x, 2)
                g = nc.gpsimd
                def roots(i):
                    for k in two:
                        u = 2 * i + k
                        pool.wait_ge(var_ready, ready(u))
                        pool.wait_ge(xn_ready, free(u))
                        g.tensor_tensor(rstd[k][:, :], var[k][:, :], w("minus_half", HP), ALU.pow)\
                            .then_inc(rstd_ready, 1)

                def body(i, more):
                    for k in two:
                        u = 2 * i + k
                        pool.wait_ge(xn_ready, ready(u))
                        pool.wait_ge(hx_done, free(u + 1))
                        g.tensor_tensor(features(xb[:, :]), features(xn[k][:, :]), row_of(s["r_out"][:, :], QT),
                                        ALU.add).then_inc(xb_ready, 1)
                        pool.wait_ge(xb_ready, u + 1)
                        h = hid[:, bass.ds(u * 512, 512)]
                        g.tensor_tensor(h, h, xb[:, :], ALU.add).then_inc(hx_done, 1)
                    if more:
                        roots(i + 1)
                    else:
                        ww["totals"](pool)
                    for k in two:
                        u = 2 * i + k
                        pool.wait_ge(val_done, ready(u))
                        pool.wait_ge(gat_ready, ready(u))
                        g.tensor_tensor(features(val[:, bass.ds(u * 512, 512)]), features(vraw[k][:, :]),
                                        per_token(gat[:, bass.ds(u * QT, QT)], QT), ALU.mult)\
                            .then_inc(gv_done, 1)

                roots(0)
                bodies(pool, body)


def window_weights(nc, sem, w, s, name, quads, wid, split, room):
    q0, q1 = quads
    n = (q1 - q0) * QT * H
    wid = wid[:, q0 * QT * H:q1 * QT * H]
    at = [0]

    def take(width):
        at[0] += width
        return room[0:HP, at[0] - width:at[0]]

    ew, recip, both, total = take(WN * n), take(n), take(n), take(n)
    mix = take(2 * n).rearrange("p (a c) -> p a c", a=2)
    width_ready, recip_ready, ew_ready, total_ready, step, split_ready = (sem(f"{name}_{x}") for x in (
        "width_ready", "recip_ready", "ew_ready", "total_ready", "step", "split_ready"))
    ch = Chain(None, step)

    def widths(act):
        nc.scalar.activation(both, wid, ACT.Tanh, scale=0.5).then_inc(width_ready, 1)

    def reciprocals(dve):
        v, ch.eng = nc.vector, dve
        dve.wait_ge(width_ready, 1)
        ch.tick(v.tensor_scalar(both, both, 1.1, None, ALU.add))
        ch.settle()
        ch.tick(v.tensor_tensor(both, both, both, ALU.mult))
        ch.settle()
        ch.tick(v.tensor_scalar(both, both, 1e-6, None, ALU.add))
        ch.settle()
        v.reciprocal(recip, both).then_inc(recip_ready, 1)

    def weights(act):
        act.wait_ge(recip_ready, 1)
        for d in range(WN):
            nc.scalar.activation(ew[:, d * n:(d + 1) * n], recip, ACT.Exp, scale=s["decay"][:, d:d + 1])\
                .then_inc(ew_ready, 1)

    def totals(pool):
        add = nc.gpsimd.tensor_tensor
        for d in range(1, WN):
            pool.wait_ge(ew_ready, d + 1)
            if d > 1:
                pool.wait_ge(total_ready, d - 1)
            before = ew[:, 0:n] if d == 1 else total
            add(total, before, ew[:, d * n:(d + 1) * n], ALU.add).then_inc(total_ready, 1)
        pool.wait_ge(total_ready, WN - 1)
        nc.gpsimd.tensor_scalar(total, total, 1e-6, None, ALU.add).then_inc(total_ready, 1)

    def sums(dve):
        v = nc.vector
        for d in range(WN):
            e = ew[:, d * n:(d + 1) * n]
            dve.wait_ge(ew_ready, d + 1)
            ch.settle()
            for a, tab in ((0, "cosd"), (1, "sind")):
                if d == 0:
                    ch.tick(v.tensor_scalar(mix[:, a, :], e, s[tab][:, d:d + 1], None, ALU.mult))
                else:
                    ch.tick(v.scalar_tensor_tensor(out=mix[:, a, :], in0=e, scalar=s[tab][:, d:d + 1],
                                                   in1=mix[:, a, :], op0=ALU.mult, op1=ALU.add))

    def normalise(dve):
        v = nc.vector
        dve.wait_ge(total_ready, WN)
        ch.tick(v.reciprocal(total, total))
        ch.settle()
        parts = split[:, q0 * 128:q1 * 128].rearrange("p (t h a c) -> p t h a c", h=2, a=2, c=16)
        for a in range(2):
            for out in (parts[:, :, 0, a, :].bitcast(F32R), mix[:, a, :].rearrange("p (t c) -> p t c", c=16)):
                ch.tick(v.scalar_tensor_tensor(out=out, in0=mix[:, a, :].rearrange("p (t c) -> p t c", c=16),
                                               scalar=1.0 / (H * P ** 0.5),
                                               in1=total.rearrange("p (t c) -> p t c", c=16),
                                               op0=ALU.mult, op1=ALU.mult))
        ch.settle()
        for a in range(2):
            v.tensor_tensor(parts[:, :, 1, a, :], mix[:, a, :].rearrange("p (t c) -> p t c", c=16),
                            parts[:, :, 0, a, :], ALU.subtract).then_inc(split_ready, 1)

    return {"widths": widths, "reciprocals": reciprocals, "weights": weights, "totals": totals, "sums": sums,
            "normalise": normalise, "split_ready": split_ready}


def done(n, back=0):
    return n + (9 - back)


def attend(nc, sb, bank, sem, w, s, cen, key, sto, cont, val, wid, gat, split, start_of_rest):
    with ExitStack() as st:
        two = range(2)
        kk, qq = ([sb(f"{n}{k}", [128, QF], st) for k in two] for n in ("kk", "qq"))
        mag = sb("cen_abs", [128, 2 * QF], st)
        cs = [sb(f"cs{k}", [128, 4, 2, LP], st) for k in two]
        root = sb("root", [HP, NT], st)
        mT, heads = sb("mT", [128, NQ * LP], st), sb("heads", [128, 8, 128], st)
        ua, vb = ([sb(f"{n}{k}", [128, 2, LP], st) for k in two] for n in ("ua", "vb"))
        turned = [sb(f"turned{k}", [128, 2, LP], st) for k in two]
        qd = [sb(f"qd{k}", [128, LP], st) for k in two]
        sm = [sb(f"sm{k}", [HP, 6 * HP], st) for k in two]
        part = sb("part", [HP, 512], st)
        psAB, psO, psD, psF, psP1, psP2 = (bank(f"at_{n}", st) for n in ("ab", "o", "d", "f", "p1", "p2"))
        ku_ready, ks_ready, abs_done, cs_ready, heads_ready, comb_ready, part_ready = (sem("at_" + n) for n in (
            "ku_ready", "ks_ready", "abs_done", "cs_ready", "heads_ready", "comb_ready", "part_ready"))
        ab_psum, uv_ready, y_ready, o_psum, qd_ready, s_psum, smd_ready, smf_ready, pv_psum = (
            sem("at_" + n) for n in ("ab_psum", "uv_ready", "y_ready", "o_psum", "qd_ready", "s_psum",
                                     "smd_ready", "smf_ready", "pv_psum"))
        ww = window_weights(nc, sem, w, s, "wb", (NQ - 2, NQ), wid, split,
                            cs[1][:, :, :, :].rearrange("p a b c -> p (a b c)"))
        turned_in = (psD, psF, psP1, psP2)
        cum = sb("cum", [HP, NT], st)
        spare = sb("spare", [1, 1], st)
        cum_psum, cum_ready, cum_root, root_ready, mt_psum, mt_done = (sem("at_" + n) for n in (
            "cum_psum", "cum_ready", "cum_root", "root_ready", "mt_psum", "mt_done"))
        BODY = 8
        DIAG, OFF = ((0, HP), (2 * HP, 3 * HP)), (4 * HP, 5 * HP)

        def where(n):
            return n // 4 % 2, n % 4 // 2, n % 2

        with nc.Block() as block:
            @block.gpsimd
            def _(pool):
                pool.sem_inc(y_ready, BODY)
                g = nc.gpsimd.tensor_tensor

                def turn(i, n):
                    u = BODY * i + n
                    pool.wait_ge(uv_ready, done(u))
                    pool.wait_ge(o_psum, done(u, 2))
                    x, y, z = turned[n % 2], ua[n % 2], vb[n % 2]
                    g(x[:, 0, :], y[:, 0, :], z[:, 0, :], ALU.subtract)
                    g(x[:, 1, :], y[:, 1, :], z[:, 1, :], ALU.add).then_inc(y_ready, 1)

                def body(i, last):
                    for n in range(BODY):
                        if last:
                            start_of_rest["gpsimd"](pool, n)
                        if not (last and n + 3 >= BODY):
                            turn(i, n + 3)

                nc.gpsimd.memset(heads[64:128, :, :], 0.0).then_inc(heads_ready, 1)
                nc.gpsimd.memset(mT[64:128, :], 0.0).then_inc(heads_ready, 1)
                pool.wait_ge(heads_ready, 3)
                ww["totals"](pool)
                for n in range(3):
                    turn(0, n)
                with pool.Fori(0, NQ // 2 - 1) as i:
                    body(i, False)
                body(NQ // 2 - 1, True)

            @block.scalar
            def _(act):
                for x in (ks_ready, cs_ready):
                    act.sem_inc(x, 2)
                act.sem_inc(smf_ready, BODY)
                f = nc.scalar.activation

                def absolutes(u):
                    act.wait_ge(cs_ready, ready(u - 1))
                    act.wait_ge(uv_ready, done(4 * u + 3, BODY))
                    f(mag[:, :], cen[:, bass.ds(u * (2 * QF), 2 * QF)], ACT.Abs).then_inc(abs_done, 1)

                def centres(u, k):
                    c = cen[:, bass.ds(u * (2 * QF), 2 * QF)]
                    f(cs[k][:, :, 1, :], features(c, LP), ACT.Sin, scale=PI_BELOW)
                    act.wait_ge(abs_done, u + 1)
                    f(cs[k][:, :, 0, :], features(mag[:, :], LP), ACT.Sin, bias=w("half_pi"),
                      scale=-PI_BELOW).then_inc(cs_ready, 1)

                def keys(u, k):
                    act.wait_ge(ku_ready, ready(u))
                    for x in (kk[k], qq[k]):
                        y = f(x[:, :], x[:, :], ACT.Sin, bias=w("posP", a=2, b=3), scale=w("posP", a=1, b=2))
                    y.then_inc(ks_ready, 1)

                def copy_off(g, n):
                    act.wait_ge(s_psum, done(g))
                    act.wait_ge(pv_psum, done(g, 2))
                    f(sm[n % 2][:, 4 * HP:6 * HP], psF[0:HP, 0:2 * HP], ACT.Copy).then_inc(smf_ready, 1)

                def body(i, last):
                    for n in range(BODY):
                        if last:
                            start_of_rest["scalar"](act, n)
                        g = BODY * i + n
                        if n % 4 == 0 and not (last and n // 4 + 1 > 1):
                            absolutes(2 * i + n // 4 + 1)
                            centres(2 * i + n // 4 + 1, (n // 4 + 1) % 2)
                        if n % 4 == 1 and not (last and n // 4 + 1 > 1):
                            keys(2 * i + n // 4 + 1, (n // 4 + 1) % 2)
                        if not (last and n + 1 >= BODY):
                            copy_off(g + 1, n + 1)

                def turn_weights(j):
                    act.wait_ge(mt_psum, j + 1)
                    f(mT[0:64, j * QF:(j + 1) * QF].bitcast(F32R), turned_in[j][0:64, 0:QF], ACT.Copy)\
                        .then_inc(mt_done, 1)

                ww["widths"](act)
                absolutes(0)
                ww["weights"](act)
                turn_weights(0)
                centres(0, 0)
                keys(0, 0)
                for j in range(1, 3):
                    turn_weights(j)
                act.wait_ge(cum_ready, 1)
                f(cum[:, :], cum[:, :], ACT.Sqrt, scale=float(P)).then_inc(cum_root, 1)
                f(spare[:, :], w("half_pi", 1), ACT.Sin)
                turn_weights(3)
                copy_off(0, 0)
                with act.Fori(0, NQ // 2 - 1) as i:
                    body(i, False)
                body(NQ // 2 - 1, True)

            @block.tensor
            def _(pe):
                for x in (ab_psum, o_psum, s_psum, pv_psum):
                    pe.sem_inc(x, BODY)
                mm = nc.tensor.matmul

                def spread(i, n):
                    k, parity, pair = where(n)
                    pe.wait_ge(uv_ready, done(BODY * i + n, 1))
                    for a in two:
                        x = mm(psAB[:, a * LP:a * LP + LP], heads[:, 4 * a + 2 * pair + parity, :].bitcast(F32R),
                               mT[:, bass.ds((2 * i + n // 4) * LP, LP)].bitcast(F32R), start=True, stop=True)
                    x.then_inc(ab_psum, 1)

                def query(i, n):
                    g = BODY * i + n
                    pe.wait_ge(y_ready, done(g))
                    pe.wait_ge(qd_ready, done(g, 1))
                    mm(psO[:, 0:LP], w("select", b=128), turned[n % 2][:, 0, :], start=True, stop=False)
                    mm(psO[:, 0:LP], w("select", a=128), turned[n % 2][:, 1, :], start=False, stop=True)\
                        .then_inc(o_psum, 1)

                def scores(i, n):
                    k, parity, pair = where(n)
                    g = BODY * i + n
                    r, c = 64 * parity, pair * LP
                    pe.wait_ge(ks_ready, ready(2 * i + n // 4))
                    pe.wait_ge(qd_ready, done(g))
                    pe.wait_ge(smd_ready, done(g, 1))
                    pe.wait_ge(smf_ready, done(g, 1))
                    for j, (keys, q) in enumerate(((s["tabA"], qd[n % 2]),
                                                   (kk[k][r:r + 64, c:c + LP], qq[k][r:r + 64, c:c + LP]))):
                        for m, l in ((0, 0), (0, 1), (1, 1)):
                            b, o = (psD, DIAG[j][m]) if m == l else (psF, j * HP)
                            x = mm(b[0:HP, o:o + HP], keys[:, m * HP:m * HP + HP], q[:, l * HP:l * HP + HP],
                                   start=True, stop=True)
                    x.then_inc(s_psum, 1)

                def weigh(i, n):
                    k, parity, pair = where(n)
                    b = pair * 2 + parity
                    g = BODY * i + n
                    pe.wait_ge(smd_ready, done(g))
                    pe.wait_ge(smf_ready, done(g))
                    if n % 4 == 0:
                        pe.wait_ge(comb_ready, ready(2 * i + n // 4 - 1))
                    sc = sm[n % 2]
                    for j, (ps, rows) in enumerate(((psP1, cont), (psP2, val))):
                        first = rows[:, bass.ds((2 * i + k) * 512 + b * D, D)]
                        second = rows[:, bass.ds((2 * i + k) * 512 + (4 + b) * D, D)]
                        mm(ps[0:HP, b * D:b * D + D], sc[:, DIAG[j][0]:DIAG[j][0] + HP], first,
                           start=True, stop=True)
                        o = ps[0:HP, (4 + b) * D:(5 + b) * D]
                        mm(o, sc[:, OFF[j]:OFF[j] + HP], first, start=True, stop=False)
                        x = mm(o, sc[:, DIAG[j][1]:DIAG[j][1] + HP], second, start=False, stop=True)
                    x.then_inc(pv_psum, 1)

                def body(i, last):
                    for n in range(BODY):
                        if last:
                            start_of_rest["tensor"](pe, n)
                        for stage, ahead in ((spread, 3), (query, 2), (scores, 1), (weigh, 0)):
                            if not (last and n + ahead >= BODY):
                                stage(i, n + ahead)

                def turn_weights(j):
                    for t in range(4):
                        c = (4 * j + t) * 64
                        x = nc.tensor.transpose(turned_in[j][0:64, t * HP:t * HP + HP], split[:, c:c + 64],
                                                w("ident", HP, 0, HP))
                    x.then_inc(mt_psum, 1)

                m, ps = w("mask", HP), psO
                g = gat[:, :].rearrange("p (q h b) -> p q h b", h=2, b=4)
                mm(ps[0:HP, 0:32], m[:, 0:HP], g[:, :, 0, :], start=True, stop=True)
                mm(ps[0:HP, 32:64], m[:, HP:2 * HP], g[:, :, 0, :], start=True, stop=False)
                mm(ps[0:HP, 32:64], m[:, 0:HP], g[:, :, 1, :], start=False, stop=True).then_inc(cum_psum, 1)
                for j in range(3):
                    turn_weights(j)
                pe.wait_ge(heads_ready, 3)
                pe.wait_ge(mt_done, 1)
                for stage, n in ((spread, 0), (spread, 1)):
                    stage(0, n)
                pe.wait_ge(cum_ready, 1)
                for stage, n in ((query, 0), (spread, 2), (query, 1)):
                    stage(0, n)
                pe.wait_ge(ww["split_ready"], 2)
                turn_weights(3)
                pe.wait_ge(mt_done, 4)
                scores(0, 0)
                with pe.Fori(0, NQ // 2 - 1) as i:
                    body(i, False)
                body(NQ // 2 - 1, True)

            @block.vector
            def _(dve):
                for x in (uv_ready, qd_ready, smd_ready):
                    dve.sem_inc(x, BODY)
                for x in (ku_ready, comb_ready):
                    dve.sem_inc(x, 2)
                v = nc.vector

                def keys(u, k):
                    dve.wait_ge(s_psum, done(4 * u + 3, BODY))
                    for x, src in ((kk[k], sto), (qq[k], key)):
                        p = src[:, bass.ds(u * QF, QF)]
                        y = v.scalar_tensor_tensor(out=x[:, :], in0=p, scalar=w("posP", b=1), in1=p,
                                                   op0=ALU.mult, op1=ALU.max)
                    y.then_inc(ku_ready, 1)

                def turn(i, n):
                    k, parity, pair = where(n)
                    g = BODY * i + n
                    dve.wait_ge(ab_psum, done(g))
                    dve.wait_ge(cs_ready, ready(2 * i + n // 4))
                    dve.wait_ge(y_ready, done(g, 2))
                    c = cs[k][:, parity * 2 + pair, :, :]
                    v.tensor_tensor(ua[n % 2][:, :, :], c, row_of(psAB[:, 0:LP], 2), ALU.mult)
                    v.tensor_tensor(vb[n % 2][:, :, :], c[:, 1::-1, :], row_of(psAB[:, LP:2 * LP], 2), ALU.mult)\
                        .then_inc(uv_ready, 1)

                def place(i, n):
                    g = BODY * i + n
                    dve.wait_ge(o_psum, done(g))
                    dve.wait_ge(s_psum, done(g, 2))
                    v.tensor_tensor(qd[n % 2][:, :], psO[:, 0:LP], s["tabB"][:, :], ALU.mult)\
                        .then_inc(qd_ready, 1)

                def mask(i, n):
                    g = BODY * i + n
                    dve.wait_ge(s_psum, done(g))
                    dve.wait_ge(pv_psum, done(g, 2))
                    v.tensor_tensor(features(sm[n % 2][:, 0:4 * HP], HP), features(psD[0:HP, 0:4 * HP], HP),
                                    row_of(w("mask", HP, 0, HP), 4), ALU.mult).then_inc(smd_ready, 1)

                def combine(u):
                    dve.wait_ge(pv_psum, done(4 * u + 3))
                    dve.wait_ge(comb_ready, ready(u - 1))
                    v.tensor_tensor(features(part[:, :]), features(psP2[0:HP, :]),
                                    per_token(root[:, bass.ds(u * QT, QT)], QT), ALU.mult).then_inc(part_ready, 1)
                    dve.wait_ge(part_ready, u + 1)
                    c = cont[:, bass.ds(u * 512, 512)]
                    v.tensor_tensor(c, part[:, :], psP1[0:HP, :], ALU.add).then_inc(comb_ready, 1)

                def body(i, last):
                    for n in range(BODY):
                        if last:
                            start_of_rest["vector"](dve, n)
                        if n % 4 == 1 and not (last and n // 4 + 1 > 1):
                            keys(2 * i + n // 4 + 1, (n // 4 + 1) % 2)
                        for stage, ahead in ((turn, 3), (place, 2), (mask, 1)):
                            if not (last and n + ahead >= BODY):
                                stage(i, n + ahead)
                        if n % 4 == 3:
                            combine(2 * i + n // 4)

                ww["reciprocals"](dve)
                dve.wait_ge(cum_psum, 1)
                v.tensor_scalar(cum[:, :].rearrange("p (q h b) -> p h q b", h=2, b=4),
                                psO[0:HP, 0:64].rearrange("p (h q b) -> p h q b", h=2, b=4), 1.0, None, ALU.max)\
                    .then_inc(cum_ready, 1)
                one = w("ident", 64, 0, 64)
                x, y = (one[:, c:c + 32].rearrange("p (a o) -> p a o", o=1).broadcast_to([64, 32, P])
                        for c in (0, 32))
                v.tensor_tensor(heads[0:64, :, :].rearrange("p j (h f) -> p (j h) f", f=P).bitcast(F32R), x, y,
                                ALU.add).then_inc(heads_ready, 1)
                keys(0, 0)
                ww["sums"](dve)
                ww["normalise"](dve)
                for stage, n in ((turn, 0), (turn, 1), (place, 0), (turn, 2), (place, 1)):
                    stage(0, n)
                dve.wait_ge(cum_root, 1)
                v.reciprocal(root[:, :], cum[:, :]).then_inc(root_ready, 1)
                mask(0, 0)
                dve.wait_ge(root_ready, 1)
                with dve.Fori(0, NQ // 2 - 1) as i:
                    body(i, False)
                body(NQ // 2 - 1, True)


class Norm:

    def __init__(self, name, sb, sem, st):
        self.mu, self.var, self.rstd = ([sb(f"{name}_{n}{k}", [HP, QT], st) for k in range(2)]
                                        for n in ("mu", "var", "rstd"))
        self.xc, self.sq, self.xn = ([sb(f"{name}_{n}{k}", [HP, 512], st) for k in range(2)]
                                     for n in ("xc", "sq", "xn"))
        self.mu_ready, self.xc_ready, self.sq_ready, self.sum_ready, self.var_ready, self.rstd_ready, \
            self.xn_ready = (sem(f"{name}_{n}") for n in (
                "mu_ready", "xc_ready", "sq_ready", "sum_ready", "var_ready", "rstd_ready", "xn_ready"))


def project_and_experts(nc, sb, bank, sem, w, s, hid, comb, out, used, retrieval):
    with ExitStack() as st:
        two = range(2)
        room = [[x, 0, 6 * width] for x, width in zip(used, (2 * QF, QF, QF))]

        def take(name, shape, stack):
            for r in room:
                if r[1] + shape[1] <= r[2]:
                    r[1] += shape[1]
                    return r[0][0:shape[0], r[1] - shape[1]:r[1]]
            raise ValueError(name)

        N1, N2 = Norm("n1", take, sem, st), Norm("n2", take, sem, st)
        ct, xs = ([take(f"{n}{k}", [128, QF], st) for k in two] for n in ("ct", "xs"))
        new = [take(f"new{k}", [HP, 512], st) for k in two]
        xsplit = [[sb(f"xsplit0_{p}", [128, QF], st) for p in two]]
        lg = [take(f"lg{k}", [HP, QT * E], st) for k in two]
        ex, top = take("ex", [HP, QT * E], st), take("top", [HP, QT], st)
        B = [bank(f"B{k}", st) for k in two]


        def section(k):
            m = 1 - k
            return [("centre1", k), ("out", m), ("new", m), ("w1", k, 1, 0, 0), ("s2", k, 0, 0, 0),
                    ("turn_gates", k), ("gT", k), ("square2", m), ("var2", m), ("w1", k, 1, 0, 1),
                    ("s2", k, 0, 0, 1), ("z", k, 0, 0), ("w1", k, 1, 1, 0), ("scale2", m), ("z", k, 0, 1),
                    ("w1", k, 1, 1, 1), ("turn2", m), ("xs", m), ("var1", k), ("z", k, 1, 0), ("logits", m),
                    ("scale1", k), ("z", k, 1, 1), ("split", m), ("lg", m), ("t", m, 0, 0, 0), ("turn1", k),
                    ("y", k, 0), ("exp1", m), ("ct", k), ("w1", m, 0, 0, 0), ("gates1", m), ("gates2", m),
                    ("w1", m, 0, 0, 1), ("y", k, 1), ("gates3", m), ("y", k, 2), ("split_gates", m),
                    ("w1", m, 0, 1, 0), ("y", k, 3), ("exp2", m), ("w1", m, 0, 1, 1)]

        plan = section(0) + section(1)
        after_next = ("centre1", "var1", "scale1", "turn1", "ct")
        early_start = [[("centre1", 0)],
                       [("centre1", 1), ("var1", 0)],
                       [("scale1", 0), ("var1", 1)],
                       [("turn1", 0), ("ct", 0), ("scale1", 1)],
                       [("out", 0), ("turn1", 1)],
                       [("new", 0), ("square2", 0), ("ct", 1)],
                       [("var2", 0)],
                       [("scale2", 0), ("turn2", 0)]]
        late_start = [("xs", 0), ("logits", 0), ("split", 0), ("t", 0, 0, 0, 0), ("lg", 0), ("gates1", 0), ("exp1", 0), ("w1", 0, 0, 0, 0), ("w1", 0, 0, 0, 1), ("gates2", 0),
                      ("exp2", 0), ("w1", 0, 0, 1, 0), ("w1", 0, 0, 1, 1), ("gates3", 0), ("split_gates", 0)]

        def quad_of(i, at):
            name, k = plan[at][:2]
            now = at // (len(plan) // 2)
            return 2 * i + now + (2 if name in after_next else 1 if k != now else 0)

        def steps(eng, step):
            for entry in late_start:
                step(eng, entry[0], entry[1], -1, entry)
            with eng.Fori(0, NQ // 2 - 1) as i:
                for at, entry in enumerate(plan):
                    step(eng, entry[0], quad_of(i, at), i, entry)
            i = NQ // 2 - 1
            for at, entry in enumerate(plan):
                if quad_of(i, at) < NQ:
                    step(eng, entry[0], quad_of(i, at), i, entry)

        a_jobs = [entry for entry in plan if entry[0] in ("t", "s2", "w1")]
        NA = len(a_jobs)
        a_users = [len(range(b, NA, 3)) for b in range(3)]
        early = sum(entry in a_jobs for entry in late_start)
        early = [len(range(b, NA, 3)) - len(range(b, NA - early, 3)) for b in range(3)]
        on_act = [j % 11 not in (3, 6, 9) for j in range(NA)]
        a_filled = [sem(f"a_filled{b}") for b in range(3)]
        a_emptied = [sem(f"a_emptied{b}") for b in range(3)]
        (ct_psum, ct_done, out_psum, new_done, xs_psum, xs_done, lg_psum, lg_done, g_step, g_exp, gates_done,
         gt_psum, gt_done, split_done, z_psum, zr_done, g_psum, zg_done, y_psum, y_done, set_up) = (
            sem("tl_" + n) for n in (
                "ct_psum", "ct_done", "out_psum", "new_done", "xs_psum", "xs_done", "lg_psum", "lg_done", "g_step",
                "g_exp", "gates_done", "gt_psum", "gt_done", "split_done", "z_psum", "zr_done", "g_psum", "zg_done",
                "y_psum", "y_done", "set_up"))
        out_stored = [sem(f"out_stored{k}") for k in two]


        def a_value(i, j):
            return a_users[j % 3] * (i + 1) + j // 3 + 1

        def wait_emptied(eng, i, kind, slot, pair=0, e=0, parity=0):
            job = (kind, slot, pair, e, parity)
            j = a_jobs.index(job)
            eng.wait_ge(a_emptied[j % 3], a_value(i - 1 if slot == 0 and job in late_start else i, j))


        def centre(dve, N, k, u, x):
            v = nc.vector
            v.tensor_reduce(N.mu[k][:, :], x, AX.X, ALU.add).then_inc(N.mu_ready, 1)
            dve.wait_ge(N.mu_ready, 2 * u + 1)
            v.tensor_scalar(N.mu[k][:, :], N.mu[k][:, :], -1.0 / D, None, ALU.mult).then_inc(N.mu_ready, 1)
            dve.wait_ge(N.mu_ready, 2 * u + 2)
            v.tensor_tensor(features(N.xc[k][:, :]), x, per_token(N.mu[k][:, :], QT), ALU.add)\
                .then_inc(N.xc_ready, 1)

        def variance(dve, N, k, u):
            v = nc.vector
            dve.wait_ge(N.sq_ready, ready(u))
            dve.wait_ge(N.rstd_ready, free(u))
            v.tensor_reduce(N.var[k][:, :], features(N.sq[k][:, :]), AX.X, ALU.add).then_inc(N.sum_ready, 1)
            dve.wait_ge(N.sum_ready, u + 1)
            v.tensor_scalar(N.var[k][:, :], N.var[k][:, :], 1.0 / D, 1e-5, ALU.mult, ALU.add)\
                .then_inc(N.var_ready, 1)

        def scale(dve, N, k, u, read):
            dve.wait_ge(N.rstd_ready, ready(u))
            dve.wait_ge(read, free(u))
            nc.vector.tensor_tensor(features(N.xn[k][:, :]), features(N.xc[k][:, :]),
                                    per_token(N.rstd[k][:, :], QT), ALU.mult).then_inc(N.xn_ready, 1)

        def square(act, N, k, u):
            act.wait_ge(N.xc_ready, ready(u))
            act.wait_ge(N.var_ready, free(u))
            nc.scalar.activation(N.sq[k][:, :], N.xc[k][:, :], ACT.Square).then_inc(N.sq_ready, 1)

        def root(pool, N, k, u):
            pool.wait_ge(N.var_ready, ready(u))
            pool.wait_ge(N.xn_ready, free(u))
            nc.gpsimd.tensor_tensor(N.rstd[k][:, :], N.var[k][:, :], w("minus_half", HP), ALU.pow)\
                .then_inc(N.rstd_ready, 1)

        def turn(dst, src):
            for half in two:
                for pair in two:
                    o, c = (half * 2 + pair) * 128, pair * LP + half * HP
                    x = nc.tensor.transpose(dst[:, c:c + HP], src[:, o:o + 128], w("ident", HP, 0, HP))
            return x

        def empty(eng, i, u, job, is_act):
            kind, k, pair, e, parity = job
            j = a_jobs.index(job)
            if on_act[j] != is_act:
                return
            if kind == "t":
                dst, bias = t1, w("b_s1")
                for p in two:
                    b = a_jobs.index(("s2", 1 - k, 0, 0, p))
                    eng.wait_ge(a_emptied[b % 3], a_value(i, b))
            elif kind == "s2":
                dst, bias = s2[parity], w("b_s2")
                eng.wait_ge(y_psum, ready(u - 1))
            else:
                dst, bias = h1[4 * pair + 2 * e + parity], w("b_e1", a=2 * pair + e, b=2 * pair + e + 1)
                eng.wait_ge(z_psum, 4 * u + 2 * pair + parity + 1)
            eng.wait_ge(a_filled[j % 3], a_value(i, j))
            src = A[j % 3][:, 0:QF]
            if is_act:
                x = nc.scalar.activation(dst[:, :], src, ACT.Relu, bias=bias)
            else:
                x = nc.vector.tensor_scalar(dst[:, :], src, bias, 0.0, ALU.add, ALU.max)
            x.then_inc(a_emptied[j % 3], 1)

        tiles = [(half, pair, half * 2 + pair, pair * LP + half * HP) for half in two for pair in two]

        def gpsimd(pool, name, u, i, entry):
            k = entry[1]
            if name == "var1":
                root(pool, N1, k, u)
            elif name == "var2":
                root(pool, N2, k, u)
            elif name == "split_gates":
                pool.wait_ge(g_step, G_STEPS * (u + 1))
                pool.wait_ge(gt_psum, free(u, 1))
                nc.gpsimd.tensor_tensor(parts[:, :, 1, :], features(gw[:, :], 2 * E), parts[:, :, 0, :], ALU.subtract)\
                    .then_inc(gates_done, 1)

        mm = nc.tensor.matmul

        def fill(pe, i, u, job):
            kind, k, pair, e, parity = job
            j = a_jobs.index(job)
            r = 64 * parity
            pe.wait_ge(a_emptied[j % 3], a_value(i, j) - 1)
            o = A[j % 3][:, 0:QF]
            if kind == "t":
                pe.wait_ge(xs_done, ready(u))
                x = mm(o, w("sW1"), xs[k][:, :], start=True, stop=True)
            elif kind == "s2":
                wait_emptied(pe, i, "t", k)
                x = mm(o, w("sW2", 64, first=r), t1[r:r + 64, :], start=True, stop=True)
            else:
                c = (2 * pair + e) * 128
                pe.wait_ge(split_done, ready(u))
                x = xsplit[k][parity][:, :].bitcast(F32R)
                mm(o, w1_high[:, c:c + 128].bitcast(F32R), x, start=True, stop=False)
                x = mm(o, w1_low[:, c:c + 128].bitcast(F32R), x, start=False, stop=True)
            x.then_inc(a_filled[j % 3], 1)

        def tensor(pe, name, u, i, entry):
            k = entry[1]
            if name == "turn1":
                pe.wait_ge(N1.xn_ready, ready(u))
                pe.wait_ge(gt_done, free(u))
                turn(B[k], N1.xn[k]).then_inc(ct_psum, 1)
            elif name == "out":
                pe.wait_ge(ct_done, ready(u))
                for half, pair, t, c in tiles:
                    x = mm(B[k][0:HP, t * 128:t * 128 + 128], ct[k][:, c:c + HP], s["outw"][:, :],
                           start=True, stop=True)
                x.then_inc(out_psum, 1)
            elif name == "turn2":
                pe.wait_ge(N2.xn_ready, ready(u))
                turn(B[k], N2.xn[k]).then_inc(xs_psum, 1)
            elif name == "logits":
                pe.wait_ge(xs_done, ready(u))
                for half, pair, t, c in tiles:
                    x = mm(B[k][0:HP, t * 8:t * 8 + 8], xs[k][:, c:c + HP], w("gW"), start=True, stop=True)
                x.then_inc(lg_psum, 1)
            elif name == "turn_gates":
                pe.wait_ge(gates_done, ready(u))
                for half, pair, t, c in tiles:
                    x = nc.tensor.transpose(B[k][0:4 * E, c:c + HP], gsplit[:, t * 4 * E:(t + 1) * 4 * E],
                                            w("ident", HP, 0, HP))
                x.then_inc(gt_psum, 1)
            elif name in ("t", "s2", "w1"):
                fill(pe, i, u, entry)
            elif name == "z":
                _, _, pair, p = entry
                n = 4 * u + 2 * pair + p
                pe.wait_ge(zr_done, ready(n - 1))
                for e in two:
                    wait_emptied(pe, i, "w1", k, pair, e, p)
                    c = (2 * pair + e) * 64
                    x = mm(Z[64 * e:64 * e + 64, 0:QF], w("eW2", a=c, b=c + 64),
                           h1[4 * pair + 2 * e + p][:, :], start=True, stop=True)
                x.then_inc(z_psum, 1)
                pe.wait_ge(gt_done, ready(u))
                pe.wait_ge(zg_done, ready(n - 1))
                c = (2 * pair + p) * 128
                mm(G[:, 0:QF], spread[:, c:c + 128].bitcast(F32R), gT[k][:, :].bitcast(F32R),
                   start=True, stop=True).then_inc(g_psum, 1)
            elif name == "y":
                half, q, t, c = tiles[entry[2]]
                if t == 0:
                    pe.wait_ge(zg_done, ready(4 * u + 3))
                    for p in two:
                        wait_emptied(pe, i, "s2", k, parity=p)
                    pe.wait_ge(y_done, ready(u - 1))
                o = Y[0:HP, t * 128:t * 128 + 128]
                mm(o, gT[k][:, c:c + HP], w("third_b", GONE + 1), start=True, stop=False)
                for p in two:
                    for j, (third, x) in enumerate((("sW3", s2[p]), ("eW3a", zg[p]), ("eW3b", zg[2 + p]))):
                        first = D * (1 - p)
                        x = mm(o, x[:, c:c + HP], w(third, a=first, b=first + 128), start=False,
                               stop=p == 1 and j == 2)
                if t == 3:
                    x.then_inc(y_psum, 1)

        def scalar(act, name, u, i, entry):
            k = entry[1]
            if name == "centre1":
                square(act, N1, k, u)
            elif name == "ct":
                act.wait_ge(ct_psum, ready(u))
                act.wait_ge(out_psum, free(u))
                nc.scalar.activation(ct[k][:, :], B[k][:, 0:QF], ACT.Copy).then_inc(ct_done, 1)
            elif name == "square2":
                square(act, N2, k, u)
            elif name == "xs":
                act.wait_ge(xs_psum, ready(u))
                act.wait_ge(y_psum, free(u))
                for p in two:
                    r = slice(64 * p, 64 * p + 64)
                    nc.scalar.activation(xsplit[k][p][r, :].bitcast(F32R), B[k][r, 0:QF], ACT.Copy)
                nc.scalar.activation(xs[k][:, :], B[k][:, 0:QF], ACT.Copy).then_inc(xs_done, 1)
            elif name in ("exp1", "exp2"):
                act.wait_ge(g_step, G_STEPS * u + (2 if name == "exp1" else 13))
                nc.scalar.activation(ex[:, :], ex[:, :], ACT.Exp).then_inc(g_exp, 1)
            elif name == "gT":
                act.wait_ge(gt_psum, ready(u, 1))
                act.wait_ge(y_psum, free(u))
                nc.scalar.activation(gT[k][0:4 * E, :].bitcast(F32R), B[k][0:4 * E, 0:QF], ACT.Copy)\
                    .then_inc(gt_done, 1)
            elif name in ("t", "s2", "w1"):
                empty(act, i, u, entry, True)
            elif name == "z":
                _, _, pair, p = entry
                n = 4 * u + 2 * pair + p
                act.wait_ge(z_psum, n + 1 + 4)
                act.wait_ge(zg_done, free(n))
                nc.scalar.activation(zr[p][:, :], Z[:, 0:QF], ACT.Relu,
                                     bias=w("b_e2", a=pair, b=pair + 1)).then_inc(zr_done, 1)

        v = nc.vector

        def softmax_of(ch, src):
            ch.tick(v.tensor_reduce(top[:, :], features(src[:, :], E), AX.X, ALU.max))
            ch.settle()
            ch.tick(v.tensor_tensor(features(ex[:, :], E), features(src[:, :], E),
                                    per_token(top[:, :], QT, E), ALU.subtract))

        def normalise(ch, dst):
            ch.tick(v.tensor_reduce(tot[:, :], features(ex[:, :], E), AX.X, ALU.add))
            ch.settle()
            ch.tick(v.reciprocal(tot[:, :], tot[:, :]))
            ch.settle()
            ch.tick(v.tensor_tensor(features(dst[:, :], E), features(ex[:, :], E),
                                    per_token(tot[:, :], QT, E), ALU.mult))
            ch.settle()

        def vector(dve, name, u, i, entry):
            k = entry[1]
            if name == "gates1":
                dve.wait_ge(lg_done, ready(u))
                softmax_of(Chain(dve, g_step, G_STEPS * u), lg[k])
            elif name == "gates2":
                dve.wait_ge(g_exp, 2 * u + 1)
                ch = Chain(dve, g_step, G_STEPS * u, 2)
                normalise(ch, gates)
                other = gates[:, :].rearrange("p (t o e) -> p t o e", o=1, e=E).broadcast_to([HP, QT, E, E])
                own = gates[:, :].rearrange("p (t e o) -> p t e o", e=E, o=1).broadcast_to([HP, QT, E, E])
                for c, op in ((ge, ALU.is_ge), (gt, ALU.is_gt)):
                    pairs = c[:, :].rearrange("p (t e f) -> p t e f", e=E, f=E)
                    ch.tick(v.tensor_tensor(pairs, other, own, op))
                ch.settle()
                for c, name in ((ge, "r_lower"), (gt, "r_higher")):
                    c = features(c[:, :], E * E)
                    ch.tick(v.tensor_tensor(c, c, row_of(w(name, HP), QT), ALU.mult))
                ch.settle()
                ch.tick(v.tensor_tensor(ge[:, :], ge[:, :], gt[:, :], ALU.add))
                ch.settle()
                ch.tick(v.tensor_reduce(rank[:, :], features(ge[:, :], E), AX.X, ALU.add))
                softmax_of(ch, gates)
            elif name == "gates3":
                dve.wait_ge(g_exp, 2 * u + 2)
                dve.wait_ge(gates_done, ready(u - 1))
                ch = Chain(dve, g_step, G_STEPS * u, 13)
                ch.tick(v.scalar_tensor_tensor(out=ex[:, :], in0=rank[:, :], scalar=1.5, in1=ex[:, :],
                                               op0=ALU.is_lt, op1=ALU.mult))
                ch.settle()
                normalise(ch, gw)
                dve.wait_ge(gt_psum, free(u, 1))
                gate = ex[:, :].rearrange("p (t a e) -> p t a e", a=2, e=E)
                total = tot[:, :].rearrange("p (t a e) -> p t a e", a=2, e=1).broadcast_to([HP, QT // 2, 2, E])
                ch.tick(v.tensor_tensor(parts[:, :, 0, :].rearrange("p t (a e) -> p t a e", e=E)
                                        .bitcast(F32R), gate, total, ALU.mult))
                assert ch.n == G_STEPS
            elif name == "centre1":
                centre(dve, N1, k, u, features(comb[:, bass.ds(u * 512, 512)]))
            elif name == "var1":
                variance(dve, N1, k, u)
            elif name == "scale1":
                scale(dve, N1, k, u, ct_psum)
            elif name == "new":
                dve.wait_ge(out_psum, ready(u))
                dve.wait_ge(y_done, free(u))
                v.tensor_tensor(new[k][:, :], hid[:, bass.ds(u * 512, 512)], B[k][0:HP, :], ALU.add)\
                    .then_inc(new_done, 1)
                dve.wait_ge(new_done, ready(u))
                centre(dve, N2, k, u, features(new[k][:, :]))
            elif name == "var2":
                variance(dve, N2, k, u)
            elif name == "scale2":
                scale(dve, N2, k, u, xs_psum)
            elif name == "split":
                dve.wait_ge(xs_done, ready(u))
                dve.wait_ge(y_psum, free(u))
                for p in two:
                    r, other = slice(64 * p, 64 * p + 64), slice(64 - 64 * p, 128 - 64 * p)
                    x = v.tensor_tensor(xsplit[k][p][other, :].bitcast(F32R), xs[k][r, :],
                                        xsplit[k][p][r, :], ALU.subtract)
                x.then_inc(split_done, 1)
            elif name == "lg":
                dve.wait_ge(lg_psum, ready(u))
                v.tensor_tensor(features(lg[k][:, :], E), features(B[k][0:HP, 0:QT * E], E),
                                row_of(w("r_gb", HP), QT), ALU.add).then_inc(lg_done, 1)
            elif name in ("t", "s2", "w1"):
                empty(dve, i, u, entry, False)
            elif name == "z":
                _, _, pair, p = entry
                n = 4 * u + 2 * pair + p
                dve.wait_ge(zr_done, ready(n))
                dve.wait_ge(g_psum, n + 1)
                dve.wait_ge(y_psum, ready(u - 1))
                v.tensor_tensor(zg[2 * pair + p][:, :], zr[p][:, :], G[:, 0:QF], ALU.mult)\
                    .then_inc(zg_done, 1)
            elif name == "y" and entry[2] == 3:
                dve.wait_ge(y_psum, ready(u))
                dve.wait_ge(out_stored[k], 32 * i + 16)
                v.tensor_tensor(y[k][:, :], new[k][:, :], Y[0:HP, :], ALU.add).then_inc(y_done, 1)

        step = {"gpsimd": gpsimd, "tensor": tensor, "scalar": scalar, "vector": vector}
        credit = {"gpsimd": (N1.rstd_ready, N2.rstd_ready, gates_done),
                  "tensor": (ct_psum, out_psum, xs_psum, lg_psum, y_psum),
                  "scalar": (N1.sq_ready, N2.sq_ready, ct_done, xs_done, zr_done, gt_done),
                  "vector": (N1.xc_ready, N1.var_ready, N1.xn_ready, N2.xc_ready, N2.var_ready, N2.xn_ready,
                             new_done, lg_done, zg_done, y_done, split_done)}

        def start_of_rest(name):
            def at_batch(eng, n):
                if n == 0:
                    for x in credit[name]:
                        eng.sem_inc(x, 2)
                for entry in early_start[n]:
                    step[name](eng, entry[0], entry[1], -1, entry)
            return at_batch

        retrieval({name: start_of_rest(name) for name in step})

        w1_high, w1_low = (sb(n, [128, E * 128], st) for n in ("w1_high", "w1_low"))
        s2, zr = ([sb(f"{n}{k}", [128, QF], st) for k in two] for n in ("s2_", "zr"))
        y = [sb(f"y{k}", [HP, 512], st) for k in two]
        xsplit.append([sb(f"xsplit1_{p}", [128, QF], st) for p in two])
        t1 = sb("t1", [128, QF], st)
        h1 = [sb(f"h1_{j}", [128, QF], st) for j in range(8)]
        zg = [sb(f"zg{j}", [128, QF], st) for j in range(4)]
        gates, gw, gsplit = (sb(n, [HP, QT * E * m], st) for n, m in (("gates", 1), ("gw", 1), ("gsplit", 2)))
        tot, rank = sb("tot", [HP, QT], st), sb("rank", [HP, QT * E], st)
        ge, gt = (sb(n, [HP, QT * E * E], st) for n in ("ge", "gt"))
        gT = [sb(f"gT{k}", [GONE + 1, QF], st) for k in two]
        spread = sb("spread", [GONE + 1, 4 * 128], st)
        A = [bank(f"A{j}", st) for j in range(3)]
        Z, G, Y = bank("Z", st), bank("G", st), bank("Y", st)
        parts = gsplit[:, :].rearrange("p (t h c) -> p t h c", h=2, c=2 * E)

        with nc.Block() as block:
            @block.gpsimd
            def _(pool):
                steps(pool, gpsimd)

            @block.tensor
            def _(pe):
                pe.sem_inc(gt_psum, 1)
                for b in range(3):
                    pe.sem_inc(a_filled[b], a_users[b] - early[b])
                pe.wait_ge(set_up, 5)
                steps(pe, tensor)

            @block.scalar
            def _(act):
                for b in range(3):
                    act.sem_inc(a_emptied[b], a_users[b] - early[b])
                act.sem_inc(z_psum, 4)
                act.wait_ge(set_up, 3)
                steps(act, scalar)

            @block.vector
            def _(dve):
                ones = w("mask", GONE + 1, HP, 2 * HP).rearrange("p (a c) -> p a c", a=1)\
                    .broadcast_to([GONE + 1, 4, HP])
                for x in gT:
                    v.tensor_copy(features(x[:, :], HP).bitcast(F32R), ones).then_inc(set_up, 1)
                v.tensor_copy(spread[:, :].bitcast(F32R), w("spread", GONE + 1)).then_inc(set_up, 1)
                v.tensor_copy(w1_high[:, :].bitcast(F32R), w("eW1")).then_inc(set_up, 1)
                dve.wait_ge(set_up, 4)
                v.tensor_tensor(w1_low[:, :].bitcast(F32R), w("eW1"), w1_high[:, :], ALU.subtract)\
                    .then_inc(set_up, 1)
                steps(dve, vector)

            @block.sync
            def _(sp):
                for x in out_stored:
                    sp.sem_inc(x, 16)
                with sp.Fori(0, NQ // 2) as i:
                    for k in two:
                        u = 2 * i + k
                        sp.wait_ge(y_done, ready(u))
                        for half in two:
                            rows = HP if half == 0 else L - HP
                            sp.dma_start(out[bass.ds(4 * u, 4), half * HP:half * HP + rows, :]
                                         .rearrange("b p f -> p b f"),
                                         y[k][0:rows, half * 256:half * 256 + 256].rearrange("p (b f) -> p b f", f=D))\
                                .then_inc(out_stored[k], 16)
                for k in two:
                    sp.wait_ge(out_stored[k], 16 + 32 * (NQ // 2))



def cubic(t):
    a, at = -0.75, abs(t)
    if at <= 1.0:
        return ((a + 2.0) * at - (a + 3.0)) * at * at + 1.0
    return ((a * at - 5.0 * a) * at + 8.0 * a) * at - 4.0 * a if at < 2.0 else 0.0


def diag(m, copies=2):
    r, c = m.shape
    out = np.zeros((r * copies, c * copies), m.dtype)
    for k in range(copies):
        out[k * r:(k + 1) * r, k * c:(k + 1) * c] = m
    return out


def token_pack():
    pack = np.zeros((128, TOK_W), np.float32)

    def put(name, a):
        at, width = TOK_COLS[name]
        assert a.shape[1] == width
        pack[0:a.shape[0], at:at + width] = a

    interp = np.zeros((TAPS, WIN))
    for j in range(WIN):
        for tap in range(4):
            interp[j // UP + tap, j] = cubic((j % UP) / UP - (tap - 1))
    put("interp", diag(interp.astype(np.float32)))
    j, k = np.arange(WIN)[:, None], np.arange(WIN)[None, :]
    angle = 2 * np.pi * ((j * np.where(k < NBIN, k, k - NBIN + 1)) % WIN) / WIN
    put("dft", diag((0.5 * np.where(k < NBIN, np.cos(angle), -np.sin(angle))).astype(np.float32)))
    put("b_gauss", np.full((128, 1), -0.7, np.float32))
    put("b_poly", np.full((128, 1), 1.3, np.float32))
    return pack


def phase_columns(kinds, unit=1.0):
    rows = [(-1.0, -unit, PI / 2) if kind == "c" else (1.0, unit, 0.0) for kind in kinds for _ in range(P)]
    return np.array(rows, np.float32)


def main_constants(put):
    put("ident", np.eye(128, dtype=np.float32))
    m, l = np.arange(HP)[:, None], np.arange(HP)[None, :]
    tri = (m <= l).astype(np.float32)
    put("mask", np.concatenate([tri, np.ones((HP, HP), np.float32)], 1))
    inv = (1.0 / (np.arange(LP) + 1.0))[None, :]
    put("mean0", (np.concatenate([tri, np.ones((HP, HP))], 1) * inv).astype(np.float32))
    put("mean1", (tri * inv[:, HP:]).astype(np.float32))
    s = np.tile(np.eye(P, dtype=np.float32), (H, 1))
    z = np.zeros_like(s)
    put("select", np.concatenate([s, z, z, s, z, s, -s, z], 1))
    put("posA", phase_columns("cscs"))
    put("posB", phase_columns("ccss"))
    put("posP", phase_columns("cscs", PI_BELOW))
    part_of = np.eye(2 * E, dtype=np.float32).reshape(2 * E, 2, 2, 2).transpose(0, 2, 1, 3).reshape(2 * E, 4, 2, 1)
    put("spread", np.tile(np.broadcast_to(part_of, (2 * E, 4, 2, 64)).reshape(2 * E, -1), (2, 1)))
    e, other = np.arange(E)[:, None], np.arange(E)[None, :]
    put("r_lower", np.tile((other < e).astype(np.float32).reshape(1, -1), (HP, 1)))
    put("r_higher", np.tile((other > e).astype(np.float32).reshape(1, -1), (HP, 1)))
    put("half_pi", np.full((128, 1), PI / 2, np.float32))
    put("minus_half", np.full((128, 8), -0.5, np.float32))


def kernel(**inputs):
    import concourse.bacc as _bacc
    from concourse import mybir as _mybir
    from concourse.bass_utils import run_bass_kernel_spmd as _run

    a = {k.replace("L0_attn_", "").replace("L0_ffn_", ""): np.asarray(v) for k, v in inputs.items()}
    pack = np.zeros((128, MAIN_W), np.float32)

    def put(name, m, first=0):
        at, width = MAIN_COLS[name]
        assert m.shape[1] == width, (name, m.shape)
        pack[first:first + m.shape[0], at:at + width] = m

    def col(name, v, copies=1):
        put(name, np.tile(v.reshape(-1, 1), (copies, 1)))

    def row(name, v):
        put(name, np.tile(v.reshape(1, -1), (HP, 1)))

    def dup(m):
        return np.concatenate([m, m], 1)

    def between(m):
        z = np.zeros_like(m)
        return np.concatenate([z, m, z], 1)

    main_constants(put)
    pos = np.zeros((P, LP), np.float32)
    pos[:, :L] = a["pos_phases"][:L].T
    put("pos", np.tile(pos, (4, 1)))
    put("hop1p", dup(a["hop_w1"][D:]))
    put("kce_t", dup(a["kce_w"].T))
    col("kce_b", a["kce_b"])
    put("kskc", dup(a["ksk_w1"][D:]))
    put("hop1", diag(a["hop_w1"][:D]))
    put("ksk1", diag(a["ksk_w1"][:D]))
    put("sg1", diag(a["sg_w1"]))
    put("key1", diag(dup(a["cpe_w"])))
    put("mc", diag(a["mc_w"]))
    put("ve", diag(a["ve_w"]))
    hop2 = a["hop_w2"].reshape(D, H, P + 1)
    put("hopc", np.tile(hop2[:, :, :P].reshape(D, H * P), (2, 1)))
    put("hopw", diag(hop2[:, :, P]))
    put("ksk2", diag(dup(a["ksk_w2"])))
    put("sg2", diag(a["sg_w2"]))
    put("outw", diag(a["out_w"]))
    put("outw64", a["out_w"])
    put("lnb", np.tile(a["ln_b"].reshape(D, 1), (1, HP)))
    col("lng", a["ln_g"], 2)
    col("b_hop1", a["hop_b1"], 2)
    col("b_ksk1", a["ksk_b1"], 2)
    col("b_sg1", a["sg_b1"], 2)
    col("b_cpe", a["cpe_b"], 4)
    hopb = a["hop_b2"].reshape(H, P + 1)
    col("b_hopc", hopb[:, :P].reshape(-1))
    row("r_hopw", hopb[:, P])
    col("b_ksk2", a["ksk_b2"], 4)
    col("b_sg2", a["sg_b2"], HP)
    put("sW1", diag(a["sW1"]))
    put("sW2", np.tile(a["sW2"], (2, 1)))
    put("sW3", between(a["sW3"]))
    put("eW1", np.tile(a["eW1"].transpose(1, 0, 2).reshape(D, -1), (2, 1)))
    put("eW2", a["eW2"].transpose(1, 0, 2).reshape(128, -1))
    for name, pair in (("eW3a", 0), ("eW3b", 1)):
        put(name, between(a["eW3"].reshape(2, 128, D)[pair]))
    put("gW", diag(a["gW"]))
    col("b_s1", a["sb1"], 2)
    col("b_s2", a["sb2"])
    put("b_e1", a["eb1"].T)
    put("b_e2", a["eb2"].reshape(2, 128).T)
    row("r_mc", a["mc_b"])
    row("r_ve", a["ve_b"])
    row("r_out", a["out_b"])
    row("r_gb", a["gb"])
    third = np.zeros((GONE + 1, 2 * D), np.float32)
    for p in range(2):
        for part in range(2):
            r = (part * 2 + p) * E
            third[r:r + E, p * D:p * D + D] = a["eb3"]
        third[GONE, p * D:p * D + D] = a["sb3"]
    put("third_b", third)
    row("r_delta", a["window_deltas"])

    at = np.clip(np.arange(TAPS)[:, None] - 1 + (WIN // UP) * np.arange(LP)[None, :], 0, NS - 1)
    windows = a["x"][:, at].reshape(NB // 2, 2, TAPS, LP).transpose(1, 2, 0, 3).reshape(2 * TAPS, -1)

    nc = _bacc.Bacc("TRN2", target_bir_lowering=False, num_devices=1)
    arrays, args = {}, []
    for name, arr in (("tok_pack", token_pack()), ("main_pack", pack), ("windows", windows)):
        arrays[name] = np.ascontiguousarray(arr)
        args.append(nc.dram_tensor(name, arr.shape, _mybir.dt.from_np(arr.dtype), kind="ExternalInput").ap())
    args.append(nc.dram_tensor("tower_out", (NB, L, D), _mybir.dt.float32, kind="ExternalOutput").ap())
    audio_tower(nc, *args)
    r = _run(nc, [arrays], core_ids=[0])
    return r.results[0]["tower_out"]
```
